# Optimizing a Trainium2 kernel written in Bass

```python
import numpy as np
import jax
import jax.numpy as jnp

def _softmax(x, axis=-1):
    return jax.nn.softmax(x, axis=axis)

def _gelu(x):
    return jax.nn.gelu(x, approximate=True)

def _silu(x):
    return jax.nn.silu(x)

def _sigmoid(x):
    return jax.nn.sigmoid(x)

def _layernorm(x, axis=-1, eps=1e-05):
    m = jnp.mean(x, axis=axis, keepdims=True)
    v = jnp.var(x, axis=axis, keepdims=True)
    return (x - m) / jnp.sqrt(v + eps)

def _scatter_add(tgt, idx, src, axis=0):
    return tgt.at[idx].add(src)

def _segment_sum(src, seg, n):
    return jax.ops.segment_sum(src, seg, n)
kernel_name = 'mk_xattn_ffn_d4_seqx_r8_e56258'

def setup_inputs(seed: int=0):
    np.random.seed(seed)
    _w = jnp.asarray

    def _rec_inputs():
        import jax
        import jax.numpy as jnp
        _rk = jax.random.key(seed)
        x = -0.0002928 + 1 * jax.random.normal(jax.random.fold_in(_rk, 1), (64, 128, 128), jnp.float32)
        _lenS = 128 - jax.random.randint(jax.random.fold_in(_rk, 7), (64,), 0, max(1, 128 // 4) + 1, jnp.int32)
        _lenS2 = 120 - jax.random.randint(jax.random.fold_in(_rk, 8), (64,), 0, max(1, 120 // 4) + 1, jnp.int32)
        _ctx_768P = jax.random.normal(jax.random.fold_in(_rk, 11), (64, 16, 96), jnp.float32)
        _ctx_768c = jax.random.dirichlet(jax.random.fold_in(_rk, 511), 0.3 * jnp.ones((16,), jnp.float32), (64, 120))
        _ctx_768t = jnp.einsum('bsk,bkd->bsd', _ctx_768c, _ctx_768P)
        _ctx_768t = _ctx_768t * jax.lax.rsqrt(jnp.mean(jnp.square(_ctx_768t)) + 1e-12) * 0.953939
        ctx_768 = 2.09791e-05 + 1.00001 * (_ctx_768t + 0.3 * jax.random.normal(jax.random.fold_in(_rk, 611), (64, 120, 96), jnp.float32))
        _validS = jnp.arange(128)[None, :] < _lenS[:, None]
        _validS2 = jnp.arange(120)[None, :] < _lenS2[:, None]
        _causal = jnp.tril(jnp.ones((128, 128), dtype=bool))
        mask_BxS_bk0 = jnp.logical_not(jnp.broadcast_to(_validS[:, :], (64, 128)))
        return (x, ctx_768, mask_BxS_bk0)
    x, ctx_768, mask_BxS_bk0 = _rec_inputs()

    def _L0_xattn_setup():
        import jax, jax.numpy as jnp
        import numpy as np
        H = 8
        D = 64
        SCALE = D ** (-0.5)
        key = jax.random.key(seed)
        ks = jax.random.split(key, 7)
        B, Nq, Nkv = (2, 256, 256)
        Cq, Ck, I = (128, 96, H * D)
        return {'x': jax.random.normal(ks[0], (B, Nq, Cq), jnp.float32), 'context': jax.random.normal(ks[1], (B, Nkv, Ck), jnp.float32), 'Wq': jax.random.normal(ks[2], (Cq, I), jnp.float32) * Cq ** (-0.5), 'Wk': jax.random.normal(ks[3], (Ck, I), jnp.float32) * Ck ** (-0.5), 'Wv': jax.random.normal(ks[4], (Ck, I), jnp.float32) * Ck ** (-0.5), 'Wo': jax.random.normal(ks[5], (I, Cq), jnp.float32) * I ** (-0.5), 'bo': jnp.zeros((Cq,), jnp.float32)}
    _L0_xattn_all = _L0_xattn_setup()
    _L0_xattn_in = {k: v for k, v in _L0_xattn_all.items() if k in ('Wq', 'Wk', 'Wv', 'Wo', 'bo')}
    del _L0_xattn_all

    def _L0_ffn_setup():
        import jax, jax.numpy as jnp
        import numpy as np
        B, S, F, E, K = (4, 128, 128, 8, 2)
        H = 4 * F
        key = jax.random.key(seed)
        ks = jax.random.split(key, 7)

        def xavier(k, shape):
            fan_in, fan_out = (shape[-2], shape[-1])
            scale = jnp.sqrt(6.0 / (fan_in + fan_out))
            return jax.random.uniform(k, shape, jnp.float32, -scale, scale)
        return {'x': jax.random.normal(ks[0], (B, S, F), jnp.float32), 'Wg': xavier(ks[1], (F, E)), 'bg': jnp.zeros((E,), jnp.float32), 'W1': xavier(ks[2], (E, F, H)), 'b1': jnp.zeros((E, H), jnp.float32), 'W2': xavier(ks[3], (E, H, F)), 'b2': jnp.zeros((E, F), jnp.float32)}
    _L0_ffn_all = _L0_ffn_setup()
    _L0_ffn_in = {k: v for k, v in _L0_ffn_all.items() if k in ('Wg', 'bg', 'W1', 'b1', 'W2', 'b2')}
    del _L0_ffn_all

    def _L1_xattn_setup():
        import jax, jax.numpy as jnp
        import numpy as np
        NUM_HEADS = 16
        key = jax.random.key(seed)
        k1, k2, k3, k4, k5 = jax.random.split(key, 5)
        B, N, C = (4, 256, 128)
        N2, Cy = (128, 96)
        x = jax.random.normal(k1, (B, N, C), dtype=jnp.float32)
        y = jax.random.normal(k2, (B, N2, Cy), dtype=jnp.float32)
        pad_mask = jax.random.randint(k3, (B, N), 0, 2).astype(jnp.bool_)
        Wq = jax.random.normal(k4, (C, C), dtype=jnp.float32) * C ** (-0.5)
        Wkv = jax.random.normal(k5, (2 * C, Cy), dtype=jnp.float32) * Cy ** (-0.5)
        return {'x': x, 'y': y, 'pad_mask': pad_mask, 'Wq': Wq, 'Wkv': Wkv}
    _L1_xattn_all = _L1_xattn_setup()
    _L1_xattn_in = {k: v for k, v in _L1_xattn_all.items() if k in ('Wq', 'Wkv')}
    del _L1_xattn_all

    def _L1_ffn_setup():
        import jax, jax.numpy as jnp
        import numpy as np
        DIM = 128

        def _reference_tuple_inner(x, W_r, W_k, W_v, mu_r, mu_k):
            B, T, C = x.shape
            x_prev = jnp.concatenate([jnp.zeros((B, 1, C), x.dtype), x[:, :-1, :]], axis=1)
            xr = mu_r * x + (1.0 - mu_r) * x_prev
            xk = mu_k * x + (1.0 - mu_k) * x_prev
            r = jax.nn.sigmoid(jnp.einsum('btc,dc->btd', xr, W_r))
            k = jnp.einsum('btc,dc->btd', xk, W_k)
            k_act = jnp.square(jax.nn.relu(k))
            out = r * jnp.einsum('btc,dc->btd', k_act, W_v)
            new_state = x[:, -1, :]
            return (out, new_state)
        key = jax.random.key(seed)
        ks = jax.random.split(key, 6)
        B, T, C = (8, 256, DIM)
        x = jax.random.normal(ks[0], (B, T, C), dtype=jnp.float32)
        s = 1.0 / np.sqrt(C)
        W_r = jax.random.uniform(ks[1], (C, C), jnp.float32, -s, s)
        W_k = jax.random.uniform(ks[2], (C, C), jnp.float32, -s, s)
        W_v = jax.random.uniform(ks[3], (C, C), jnp.float32, -s, s)
        mu_r = jax.random.uniform(ks[4], (C,), jnp.float32)
        mu_k = jax.random.uniform(ks[5], (C,), jnp.float32)
        return {'x': x, 'W_r': W_r, 'W_k': W_k, 'W_v': W_v, 'mu_r': mu_r, 'mu_k': mu_k}
    _L1_ffn_all = _L1_ffn_setup()
    _L1_ffn_in = {k: v for k, v in _L1_ffn_all.items() if k in ('W_r', 'W_k', 'W_v', 'mu_r', 'mu_k')}
    del _L1_ffn_all

    def _L2_xattn_setup():
        import jax, jax.numpy as jnp
        import numpy as np
        import math
        E = 128
        EV = 128
        FFN = 512
        DINO = 96
        B, S, P = (64, 64, 32)

        def bitnet_linear(x, W, b):
            w_scale = jnp.maximum(jnp.mean(jnp.abs(W)), 1e-05)
            qW = jnp.sign(W) * (jnp.abs(W) > 0.5 * w_scale).astype(W.dtype)
            i_scale = jnp.maximum(jnp.max(jnp.abs(x)), 1e-08) / 127.0
            qx = jnp.clip(jnp.round(x / i_scale), -128.0, 127.0)
            out = jnp.einsum('...i,oi->...o', qx, qW) * (w_scale * i_scale)
            return out + b
        key = jax.random.key(seed)
        ks = iter(jax.random.split(key, 32))

        def lin_w(fin, fout):
            return jax.random.normal(next(ks), (fout, fin), jnp.float32) * math.sqrt(2.0 / fin)
        return {'text_embeddings': jax.random.normal(next(ks), (B, S, E), jnp.float32), 'dinov2_features': jax.random.normal(next(ks), (B, P, DINO), jnp.float32), 'W_d2v': lin_w(DINO, EV), 'b_d2v': jnp.zeros((EV,), jnp.float32), 'W_img': lin_w(EV, E), 'b_img': jnp.zeros((E,), jnp.float32), 'W_txt': lin_w(E, E), 'b_txt': jnp.zeros((E,), jnp.float32), 'W_att0': lin_w(E, E // 2), 'b_att0': jnp.zeros((E // 2,), jnp.float32), 'W_att1': lin_w(E, E // 2), 'b_att1': jnp.zeros((E // 2,), jnp.float32), 'W_f1': lin_w(2 * E, FFN), 'b_f1': jnp.zeros((FFN,), jnp.float32), 'W_f2': lin_w(FFN, E), 'b_f2': jnp.zeros((E,), jnp.float32)}
    _L2_xattn_all = _L2_xattn_setup()
    _L2_xattn_in = {k: v for k, v in _L2_xattn_all.items() if k in ('W_d2v', 'b_d2v', 'W_img', 'b_img', 'W_txt', 'b_txt', 'W_att0', 'b_att0', 'W_att1', 'b_att1', 'W_f1', 'b_f1', 'W_f2', 'b_f2')}
    del _L2_xattn_all

    def _L2_ffn_setup():
        import jax, jax.numpy as jnp
        import numpy as np
        E = 8
        TOP_K = 2
        H = 128
        I = 64
        B, S = (2, 256)

        def _moe_forward(hidden_states, w_gate, w_fc, w_proj):
            b, s, h = hidden_states.shape
            x = hidden_states.reshape(-1, h)
            T = x.shape[0]
            router_logits = x @ w_gate.T
            topk_vals, topk_idx = jax.lax.top_k(router_logits, TOP_K)
            router_weights = jax.nn.softmax(topk_vals.astype(jnp.float32), axis=-1).astype(x.dtype)
            gates = jnp.zeros((T, E), x.dtype).at[jnp.arange(T)[:, None], topk_idx].add(router_weights)
            hmid = jax.nn.gelu(jnp.einsum('th,eih->tei', x, w_fc), approximate=False)
            y = jnp.einsum('tei,ehi->teh', hmid, w_proj)
            out = jnp.einsum('teh,te->th', y, gates)
            return out.reshape(b, s, h)
        key = jax.random.key(seed)
        k0, k1, k2, k3 = jax.random.split(key, 4)
        std = 0.02
        return {'hidden_states': jax.random.normal(k0, (B, S, H), dtype=jnp.float32), 'w_gate': jax.random.normal(k1, (E, H), dtype=jnp.float32) * std, 'w_fc': jax.random.normal(k2, (E, I, H), dtype=jnp.float32) * std, 'w_proj': jax.random.normal(k3, (E, H, I), dtype=jnp.float32) * (std / np.sqrt(48.0))}
    _L2_ffn_all = _L2_ffn_setup()
    _L2_ffn_in = {k: v for k, v in _L2_ffn_all.items() if k in ('w_gate', 'w_fc', 'w_proj')}
    del _L2_ffn_all

    def _L3_xattn_setup():
        import jax, jax.numpy as jnp
        import numpy as np
        N_HEADS = 16
        key = jax.random.key(seed)
        ks = jax.random.split(key, 8)
        b, l, m = (8, 128, 128)
        d_embed, d_cross = (128, 96)
        s_q = 1.0 / np.sqrt(d_embed)
        s_kv = 1.0 / np.sqrt(d_cross)
        return {'x': jax.random.normal(ks[0], (b, l, d_embed), jnp.float32), 'y': jax.random.normal(ks[1], (b, m, d_cross), jnp.float32), 'Wq': jax.random.normal(ks[2], (d_embed, d_embed), jnp.float32) * s_q, 'bq': jax.random.normal(ks[3], (d_embed,), jnp.float32) * 0.01, 'Wkv': jax.random.normal(ks[4], (2 * d_embed, d_cross), jnp.float32) * s_kv, 'bkv': jax.random.normal(ks[5], (2 * d_embed,), jnp.float32) * 0.01, 'Wo': jax.random.normal(ks[6], (d_embed, d_embed), jnp.float32) * s_q, 'bo': jax.random.normal(ks[7], (d_embed,), jnp.float32) * 0.01}
    _L3_xattn_all = _L3_xattn_setup()
    _L3_xattn_in = {k: v for k, v in _L3_xattn_all.items() if k in ('Wq', 'bq', 'Wkv', 'bkv', 'Wo', 'bo')}
    del _L3_xattn_all

    def _L3_ffn_setup():
        import jax, jax.numpy as jnp
        import numpy as np
        BLOCK = 32
        W_BITS = 4
        ACT_BITS = 16

        def act_qdq(x):
            qmax = 2.0 ** (ACT_BITS - 1) - 1.0
            scale = jnp.maximum(jnp.max(jnp.abs(x)) / qmax, 1e-12)
            return jnp.clip(jnp.round(x / scale), -qmax - 1.0, qmax) * scale

        def fixed_qdq_u16(x):
            scale = 1.0 / 65536.0
            return jnp.clip(jnp.round(x / scale), 0.0, 65535.0) * scale

        def lpbq_dequant(w):
            O, I = w.shape
            qmax = 2.0 ** (W_BITS - 1) - 1.0
            wb = w.reshape(O, I // BLOCK, BLOCK)
            s = jnp.maximum(jnp.max(jnp.abs(wb), axis=-1, keepdims=True) / qmax, 1e-12)
            wq = jnp.clip(jnp.round(wb / s), -qmax - 1.0, qmax) * s
            return wq.reshape(O, I)
        key = jax.random.key(seed)
        k1, k2, k3, k4 = jax.random.split(key, 4)
        B, S, H, I = (2, 512, 128, 384)
        x = jax.random.normal(k1, (B, S, H), jnp.float32)
        w_gate = jax.random.normal(k2, (I, H), jnp.float32) * 0.02
        w_up = jax.random.normal(k3, (I, H), jnp.float32) * 0.02
        w_down = jax.random.normal(k4, (H, I), jnp.float32) * 0.02
        return {'x': x, 'w_gate': w_gate, 'w_up': w_up, 'w_down': w_down}
    _L3_ffn_all = _L3_ffn_setup()
    _L3_ffn_in = {k: v for k, v in _L3_ffn_all.items() if k in ('w_gate', 'w_up', 'w_down')}
    del _L3_ffn_all
    return {'x': x, 'ctx_768': ctx_768, 'mask_BxS_bk0': mask_BxS_bk0, 'L0_xattn_Wq': _L0_xattn_in['Wq'], 'L0_xattn_Wk': _L0_xattn_in['Wk'], 'L0_xattn_Wv': _L0_xattn_in['Wv'], 'L0_xattn_Wo': _L0_xattn_in['Wo'], 'L0_xattn_bo': _L0_xattn_in['bo'], 'L0_ffn_Wg': _L0_ffn_in['Wg'], 'L0_ffn_bg': _L0_ffn_in['bg'], 'L0_ffn_W1': _L0_ffn_in['W1'], 'L0_ffn_b1': _L0_ffn_in['b1'], 'L0_ffn_W2': _L0_ffn_in['W2'], 'L0_ffn_b2': _L0_ffn_in['b2'], 'L1_xattn_Wq': _L1_xattn_in['Wq'], 'L1_xattn_Wkv': _L1_xattn_in['Wkv'], 'L1_ffn_W_r': _L1_ffn_in['W_r'], 'L1_ffn_W_k': _L1_ffn_in['W_k'], 'L1_ffn_W_v': _L1_ffn_in['W_v'], 'L1_ffn_mu_r': _L1_ffn_in['mu_r'], 'L1_ffn_mu_k': _L1_ffn_in['mu_k'], 'L2_xattn_W_d2v': _L2_xattn_in['W_d2v'], 'L2_xattn_b_d2v': _L2_xattn_in['b_d2v'], 'L2_xattn_W_img': _L2_xattn_in['W_img'], 'L2_xattn_b_img': _L2_xattn_in['b_img'], 'L2_xattn_W_txt': _L2_xattn_in['W_txt'], 'L2_xattn_b_txt': _L2_xattn_in['b_txt'], 'L2_xattn_W_att0': _L2_xattn_in['W_att0'], 'L2_xattn_b_att0': _L2_xattn_in['b_att0'], 'L2_xattn_W_att1': _L2_xattn_in['W_att1'], 'L2_xattn_b_att1': _L2_xattn_in['b_att1'], 'L2_xattn_W_f1': _L2_xattn_in['W_f1'], 'L2_xattn_b_f1': _L2_xattn_in['b_f1'], 'L2_xattn_W_f2': _L2_xattn_in['W_f2'], 'L2_xattn_b_f2': _L2_xattn_in['b_f2'], 'L2_ffn_w_gate': _L2_ffn_in['w_gate'], 'L2_ffn_w_fc': _L2_ffn_in['w_fc'], 'L2_ffn_w_proj': _L2_ffn_in['w_proj'], 'L3_xattn_Wq': _L3_xattn_in['Wq'], 'L3_xattn_bq': _L3_xattn_in['bq'], 'L3_xattn_Wkv': _L3_xattn_in['Wkv'], 'L3_xattn_bkv': _L3_xattn_in['bkv'], 'L3_xattn_Wo': _L3_xattn_in['Wo'], 'L3_xattn_bo': _L3_xattn_in['bo'], 'L3_ffn_w_gate': _L3_ffn_in['w_gate'], 'L3_ffn_w_up': _L3_ffn_in['w_up'], 'L3_ffn_w_down': _L3_ffn_in['w_down']}

def reference(x, ctx_768, mask_BxS_bk0, L0_xattn_Wq, L0_xattn_Wk, L0_xattn_Wv, L0_xattn_Wo, L0_xattn_bo, L0_ffn_Wg, L0_ffn_bg, L0_ffn_W1, L0_ffn_b1, L0_ffn_W2, L0_ffn_b2, L1_xattn_Wq, L1_xattn_Wkv, L1_ffn_W_r, L1_ffn_W_k, L1_ffn_W_v, L1_ffn_mu_r, L1_ffn_mu_k, L2_xattn_W_d2v, L2_xattn_b_d2v, L2_xattn_W_img, L2_xattn_b_img, L2_xattn_W_txt, L2_xattn_b_txt, L2_xattn_W_att0, L2_xattn_b_att0, L2_xattn_W_att1, L2_xattn_b_att1, L2_xattn_W_f1, L2_xattn_b_f1, L2_xattn_W_f2, L2_xattn_b_f2, L2_ffn_w_gate, L2_ffn_w_fc, L2_ffn_w_proj, L3_xattn_Wq, L3_xattn_bq, L3_xattn_Wkv, L3_xattn_bkv, L3_xattn_Wo, L3_xattn_bo, L3_ffn_w_gate, L3_ffn_w_up, L3_ffn_w_down):
    import jax
    import jax.numpy as jnp

    def _L0_xattn_ref(x, context, Wq, Wk, Wv, Wo, bo):
        import jax, jax.numpy as jnp
        import numpy as np
        H = 8
        D = 64
        SCALE = D ** (-0.5)
        B, Nq, _ = x.shape
        Nkv = context.shape[1]
        q = (x @ Wq).reshape(B, Nq, H, D)
        k = (context @ Wk).reshape(B, Nkv, H, D)
        v = (context @ Wv).reshape(B, Nkv, H, D)
        sim = jnp.einsum('bihd,bjhd->bhij', q, k) * SCALE
        attn = jax.nn.softmax(sim, axis=-1)
        out = jnp.einsum('bhij,bjhd->bihd', attn, v).reshape(B, Nq, H * D)
        return out @ Wo + bo

    def _L0_ffn_ref(x, Wg, bg, W1, b1, W2, b2):
        import jax, jax.numpy as jnp
        import numpy as np
        B, S, F, E, K = (4, 128, 128, 8, 2)
        H = 4 * F
        gate_probs = jax.nn.softmax(x @ Wg + bg, axis=-1)
        k = K
        _, top_idx = jax.lax.top_k(gate_probs, k)
        expert_mask = jax.nn.one_hot(top_idx, gate_probs.shape[-1], dtype=gate_probs.dtype).sum(-2)
        selected = gate_probs * expert_mask
        selected = selected / (selected.sum(-1, keepdims=True) + 1e-08)
        h = jax.nn.gelu(jnp.einsum('bsf,efh->bseh', x, W1) + b1)
        expert_out = jnp.einsum('bseh,ehf->bsef', h, W2) + b2[None, None]
        return jnp.einsum('bsef,bse->bsf', expert_out, selected)

    def _L1_xattn_ref(x, y, pad_mask, Wq, Wkv):
        import jax, jax.numpy as jnp
        import numpy as np
        NUM_HEADS = 16
        B, N, C = x.shape
        N2 = y.shape[1]
        H = NUM_HEADS
        d = C // H
        scale = d ** (-0.5)
        q = (x @ Wq.T).reshape(B, N, H, d).transpose(0, 2, 1, 3)
        kv = (y @ Wkv.T).reshape(B, N2, 2, H, d).transpose(2, 0, 3, 1, 4)
        k, v = (kv[0], kv[1])
        attn = jnp.einsum('bhnd,bhmd->bhnm', q * scale, k)
        attn = jnp.where(pad_mask[:, None, :, None], attn, jnp.float32(-1000000000.0))
        attn = jax.nn.softmax(attn, axis=-1)
        out = jnp.einsum('bhnm,bhmd->bhnd', attn, v)
        return out.transpose(0, 2, 1, 3).reshape(B, N, C)

    def _L1_ffn_ref(x, W_r, W_k, W_v, mu_r, mu_k):
        import jax, jax.numpy as jnp
        import numpy as np
        DIM = 128

        def _reference_tuple_inner(x, W_r, W_k, W_v, mu_r, mu_k):
            B, T, C = x.shape
            x_prev = jnp.concatenate([jnp.zeros((B, 1, C), x.dtype), x[:, :-1, :]], axis=1)
            xr = mu_r * x + (1.0 - mu_r) * x_prev
            xk = mu_k * x + (1.0 - mu_k) * x_prev
            r = jax.nn.sigmoid(jnp.einsum('btc,dc->btd', xr, W_r))
            k = jnp.einsum('btc,dc->btd', xk, W_k)
            k_act = jnp.square(jax.nn.relu(k))
            out = r * jnp.einsum('btc,dc->btd', k_act, W_v)
            new_state = x[:, -1, :]
            return (out, new_state)
        return _reference_tuple_inner(x, W_r, W_k, W_v, mu_r, mu_k)[0]

    def _L2_xattn_ref(text_embeddings, dinov2_features, W_d2v, b_d2v, W_img, b_img, W_txt, b_txt, W_att0, b_att0, W_att1, b_att1, W_f1, b_f1, W_f2, b_f2):
        import jax, jax.numpy as jnp
        import numpy as np
        import math
        E = 128
        EV = 128
        FFN = 512
        DINO = 96
        B, S, P = (64, 64, 32)

        def bitnet_linear(x, W, b):
            w_scale = jnp.maximum(jnp.mean(jnp.abs(W)), 1e-05)
            qW = jnp.sign(W) * (jnp.abs(W) > 0.5 * w_scale).astype(W.dtype)
            i_scale = jnp.maximum(jnp.max(jnp.abs(x)), 1e-08) / 127.0
            qx = jnp.clip(jnp.round(x / i_scale), -128.0, 127.0)
            out = jnp.einsum('...i,oi->...o', qx, qW) * (w_scale * i_scale)
            return out + b
        b, s, e = text_embeddings.shape
        vis = bitnet_linear(dinov2_features, W_d2v, b_d2v)
        image_embeds = bitnet_linear(vis, W_img, b_img)
        fused = bitnet_linear(text_embeddings, W_txt, b_txt)
        inv_sqrt_e = 1.0 / math.sqrt(e)
        for Wa, ba in ((W_att0, b_att0), (W_att1, b_att1)):
            kv = bitnet_linear(image_embeds, Wa, ba)
            k = jnp.concatenate([kv, kv], axis=-1)
            scores = jnp.einsum('bse,bpe->bsp', fused, k) * inv_sqrt_e
            attn = jax.nn.softmax(scores, axis=-1)
            fused = fused + 0.1 * jnp.einsum('bsp,bpe->bse', attn, k)
        avg_img = jnp.mean(image_embeds, axis=1, keepdims=True)
        concatenated = jnp.concatenate([fused, jnp.broadcast_to(avg_img, (b, s, e))], axis=-1)
        h = jax.nn.relu(bitnet_linear(concatenated, W_f1, b_f1))
        return bitnet_linear(h, W_f2, b_f2)

    def _L2_ffn_ref(hidden_states, w_gate, w_fc, w_proj):
        import jax, jax.numpy as jnp
        import numpy as np
        E = 8
        TOP_K = 2
        H = 128
        I = 64
        B, S = (2, 256)

        def _moe_forward(hidden_states, w_gate, w_fc, w_proj):
            b, s, h = hidden_states.shape
            x = hidden_states.reshape(-1, h)
            T = x.shape[0]
            router_logits = x @ w_gate.T
            topk_vals, topk_idx = jax.lax.top_k(router_logits, TOP_K)
            router_weights = jax.nn.softmax(topk_vals.astype(jnp.float32), axis=-1).astype(x.dtype)
            gates = jnp.zeros((T, E), x.dtype).at[jnp.arange(T)[:, None], topk_idx].add(router_weights)
            hmid = jax.nn.gelu(jnp.einsum('th,eih->tei', x, w_fc), approximate=False)
            y = jnp.einsum('tei,ehi->teh', hmid, w_proj)
            out = jnp.einsum('teh,te->th', y, gates)
            return out.reshape(b, s, h)
        return _moe_forward(hidden_states, w_gate, w_proj=w_proj, w_fc=w_fc)

    def _L3_xattn_ref(x, y, Wq, bq, Wkv, bkv, Wo, bo):
        import jax, jax.numpy as jnp
        import numpy as np
        N_HEADS = 16
        b, l, d = x.shape
        m = y.shape[1]
        h = N_HEADS
        dh = d // h
        q = (jnp.einsum('bld,ed->ble', x, Wq) + bq).reshape(b, l, h, dh)
        kv = (jnp.einsum('bmc,ec->bme', y, Wkv) + bkv).reshape(b, m, h, 2 * dh)
        k, v = (kv[..., :dh], kv[..., dh:])
        scale = 1.0 / jnp.sqrt(jnp.asarray(dh, x.dtype))
        att = jax.nn.softmax(jnp.einsum('blhd,bmhd->blmh', q, k) * scale, axis=2)
        out = jnp.einsum('blmh,bmhd->blhd', att, v).reshape(b, l, d)
        return jnp.einsum('bld,ed->ble', out, Wo) + bo

    def _L3_ffn_ref(x, w_gate, w_up, w_down):
        import jax, jax.numpy as jnp
        import numpy as np
        BLOCK = 32
        W_BITS = 4
        ACT_BITS = 16

        def act_qdq(x):
            qmax = 2.0 ** (ACT_BITS - 1) - 1.0
            scale = jnp.maximum(jnp.max(jnp.abs(x)) / qmax, 1e-12)
            return jnp.clip(jnp.round(x / scale), -qmax - 1.0, qmax) * scale

        def fixed_qdq_u16(x):
            scale = 1.0 / 65536.0
            return jnp.clip(jnp.round(x / scale), 0.0, 65535.0) * scale

        def lpbq_dequant(w):
            O, I = w.shape
            qmax = 2.0 ** (W_BITS - 1) - 1.0
            wb = w.reshape(O, I // BLOCK, BLOCK)
            s = jnp.maximum(jnp.max(jnp.abs(wb), axis=-1, keepdims=True) / qmax, 1e-12)
            wq = jnp.clip(jnp.round(wb / s), -qmax - 1.0, qmax) * s
            return wq.reshape(O, I)
        x = act_qdq(x)
        up = act_qdq(x @ lpbq_dequant(w_up).T)
        gate = act_qdq(x @ lpbq_dequant(w_gate).T)
        sig = fixed_qdq_u16(jax.nn.sigmoid(gate))
        gate = act_qdq(gate * sig)
        o = act_qdq(gate * up)
        return o @ lpbq_dequant(w_down).T
    x = x + _L0_xattn_ref(_layernorm(x, axis=-1), ctx_768, L0_xattn_Wq, L0_xattn_Wk, L0_xattn_Wv, L0_xattn_Wo, L0_xattn_bo)
    x = x + _L0_ffn_ref(_layernorm(x, axis=-1), L0_ffn_Wg, L0_ffn_bg, L0_ffn_W1, L0_ffn_b1, L0_ffn_W2, L0_ffn_b2)
    x = x + _L1_xattn_ref(_layernorm(x, axis=-1), ctx_768, mask_BxS_bk0, L1_xattn_Wq, L1_xattn_Wkv)
    x = x + _L1_ffn_ref(_layernorm(x, axis=-1), L1_ffn_W_r, L1_ffn_W_k, L1_ffn_W_v, L1_ffn_mu_r, L1_ffn_mu_k)
    x = x + _L2_xattn_ref(_layernorm(x, axis=-1), ctx_768, L2_xattn_W_d2v, L2_xattn_b_d2v, L2_xattn_W_img, L2_xattn_b_img, L2_xattn_W_txt, L2_xattn_b_txt, L2_xattn_W_att0, L2_xattn_b_att0, L2_xattn_W_att1, L2_xattn_b_att1, L2_xattn_W_f1, L2_xattn_b_f1, L2_xattn_W_f2, L2_xattn_b_f2)
    x = x + _L2_ffn_ref(_layernorm(x, axis=-1), L2_ffn_w_gate, L2_ffn_w_fc, L2_ffn_w_proj)
    x = x + _L3_xattn_ref(_layernorm(x, axis=-1), ctx_768, L3_xattn_Wq, L3_xattn_bq, L3_xattn_Wkv, L3_xattn_bkv, L3_xattn_Wo, L3_xattn_bo)
    x = x + _L3_ffn_ref(_layernorm(x, axis=-1), L3_ffn_w_gate, L3_ffn_w_up, L3_ffn_w_down)
    return x

_drawn_inputs = setup_inputs


def setup_inputs(seed=0):
    import zlib

    import numpy as np

    out = dict(_drawn_inputs(seed))
    spreads = {'L0_xattn_bo': (0.0, 0.1),
     'L0_ffn_bg': (0.0, 0.1),
     'L0_ffn_b1': (0.0, 0.1),
     'L0_ffn_b2': (0.0, 0.1),
     'L2_xattn_b_d2v': (0.0, 0.287),
     'L2_xattn_b_img': (0.0, 0.27),
     'L2_xattn_b_txt': (0.0, 0.1),
     'L2_xattn_b_att0': (0.0, 0.8),
     'L2_xattn_b_att1': (0.0, 0.8),
     'L2_xattn_b_f1': (0.0, 0.1),
     'L2_xattn_b_f2': (0.0, 0.1)}
    factors = {'L1_ffn_W_r': 3.399,
     'L1_ffn_mu_r': 6.954,
     'L2_xattn_W_att0': 3.64,
     'L2_xattn_W_att1': 3.872,
     'L2_ffn_w_gate': 8.0,
     'L2_ffn_w_fc': 8.0,
     'L2_ffn_w_proj': 8.0,
     'L3_xattn_bq': 23.474,
     'L3_xattn_bkv': 7.608,
     'L3_xattn_bo': 8.0,
     'L3_ffn_w_gate': 8.0,
     'L3_ffn_w_up': 8.0,
     'L3_ffn_w_down': 8.0}
    for name, (base, spread) in spreads.items():
        noise = np.random.default_rng([zlib.crc32(name.encode()), seed]).standard_normal(out[name].shape)
        drawn = base * np.exp(spread * noise) if base else spread * noise
        out[name] = jnp.asarray(drawn.astype(out[name].dtype))
    for name, factor in factors.items():
        out[name] = (out[name] * factor).astype(out[name].dtype)
    return out
```

```python
from contextlib import ExitStack

import concourse.bass as bass
from concourse import mybir

F32 = mybir.dt.float32
BF16 = mybir.dt.bfloat16
I16 = mybir.dt.int16
U8 = mybir.dt.uint8
ALU = mybir.AluOpType
ACT = mybir.ActivationFunctionType
AX = mybir.AxisListType
RMAX = bass.bass_isa.ReduceOp.max
RADD = bass.bass_isa.ReduceOp.add

NB, T, F = 64, 128, 128
NK, CK = 120, 96
LN_EPS = 1e-5
MAGIC = 1.5 * 2.0 ** 23
GB = 4
NG = NB // GB


def after(eng, sem, n):
    if isinstance(n, int) and n <= 0:
        return
    eng.wait_ge(sem, n)


def apart(eng, g, *waits):
    counts = [n if isinstance(n, int) else eng.to_reg(n) for _, n in waits]
    eng.wait_ge(g.s_constants, 1)
    for (sem, _), n in zip(waits, counts):
        after(eng, sem, n)


def ticks(eng, n, lag, tick):
    head = lag + 2 + (lag % 2)
    head = min(head, n)
    for t in range(head):
        tick(t, t % 2)
    if head < n:
        with eng.Fori(head // 2, n // 2) as j:
            tick(j * 2, 0)
            tick(j * 2 + 1, 1)
    for t in range(n, n + lag):
        tick(t, t % 2)


def stage(t, par, lag, n, fn):
    b = t - lag
    if isinstance(b, int) and not 0 <= b < n:
        return
    fn(b, (par - lag) % 2)


class Resident:
    pass


class Link:

    def __init__(self, eng, sem, per):
        self.eng, self.sem, self.per, self.k, self.b = eng, sem, per, 0, 0

    def unit(self, b):
        assert self.k in (0, self.per), (self.k, self.per)
        self.b, self.k = b, 0

    def __call__(self, ins):
        self.k += 1
        ins.then_inc(self.sem, 1)
        self.eng.wait_ge(self.sem, self.b * self.per + self.k)


class Layer:

    def __init__(self, nc, ctx, name):
        self.nc, self.ctx, self.name, self.sems = nc, ctx, name, []
        ctx.callback(self.release)

    def release(self):
        self.nc.clear_and_free_semaphores(self.sems)
        self.nc.all_engine_barrier()

    def sem(self, name):
        self.sems.append(self.nc.alloc_semaphore(f"{self.name}_{name}"))
        return self.sems[-1]

    def sb(self, name, shape, dt=F32):
        return self.ctx.enter_context(self.nc.sbuf_tensor(f"{self.name}_{name}", shape, dt))

    def psum(self, name, shape, dt=F32):
        return self.ctx.enter_context(self.nc.psum_tensor(f"{self.name}_{name}", shape, dt))


class Norm:

    def __init__(self, L, g, G, x_done, psum, masked=False, top=None):
        self.nc, self.g, self.G, self.x_done, self.psum = L.nc, g, G, x_done, psum
        self.masked, self.top = masked, top
        self.stats = L.sb("stats", [T, 2, G, 6])
        self.mv = L.sb("meanvar", [T, 2, G, 2])
        self.rstd = L.sb("rstd", [T, 2, G])
        self.xn = L.sb("xn", [T, 2, G * F])
        self.s_stats = L.sem("ln_stats")
        self.s_mean = L.sem("ln_mean")
        self.s_var = L.sem("ln_var")
        self.s_pow = L.sem("ln_pow")
        self.s_rstd = L.sem("ln_rstd")
        self.s_xn = L.sem("ln_xn")
        self.s_turned = L.sem("ln_turned")
        self.s_stored = L.sem("ln_stored")

    def batches(self, t, u):
        if self.G == 1:
            return t[:, bass.ds(u, 1), :] if not isinstance(u, int) else t[:, u:u + 1, :]
        if isinstance(u, int):
            return t[:, u * self.G:(u + 1) * self.G, :]
        return t[:, bass.ds(u * self.G, self.G), :]

    def one(self, t, u, k):
        b = u * self.G + k
        return t[:, b, :] if isinstance(b, int) else t[:, bass.ds(b, 1), :].rearrange("p a f -> p (a f)")

    def dve_mean(self, dve, u, p):
        apart(dve, self.g, (self.x_done, u + 1))
        for k in range(self.G):
            i = self.nc.vector.bn_stats(self.stats[:, p, k, :], self.one(self.g.X, u, k))
        i.then_inc(self.s_stats, 1)
        apart(dve, self.g,
              (self.s_rstd, u - 1),
              (self.s_stats, u + 1))
        for k in range(self.G):
            i = self.nc.vector.bn_aggr(self.mv[:, p, k, :], self.stats[:, p, k, :])
        i.then_inc(self.s_mean, 1)

    def pool_rstd(self, pool, u, p):
        apart(pool, self.g,
              (self.s_mean, u + 1),
              (self.s_xn, u - 1))
        self.nc.gpsimd.tensor_scalar(self.rstd[:, p, :], self.mv[:, p, :, 1], LN_EPS, 1.0, ALU.add, ALU.mult).then_inc(self.s_var, 1)
        pool.wait_ge(self.s_var, u + 1)
        i = self.nc.gpsimd.tensor_tensor(self.rstd[:, p, :], self.rstd[:, p, :], self.g.minus_half[:, 0:self.G], ALU.pow)
        if self.masked:
            i.then_inc(self.s_pow, 1)
            apart(pool, self.g, (self.s_pow, u + 1))
            if isinstance(u, int):
                keep = self.g.keep[:, u * self.G:(u + 1) * self.G]
            else:
                keep = self.g.keep[:, bass.ds(u * self.G, self.G)]
            i = self.nc.gpsimd.tensor_tensor(self.rstd[:, p, :], self.rstd[:, p, :], keep, ALU.mult)
        i.then_inc(self.s_rstd, 1)

    def dve_xn(self, dve, u, p):
        dve.wait_ge(self.s_rstd, u + 1)
        after(dve, self.s_turned, u - 1)
        for k in range(self.G):
            i = self.nc.vector.tensor_scalar(self.xn[:, p, k * F:(k + 1) * F], self.one(self.g.X, u, k),
                                             self.mv[:, p, k, 0:1], self.rstd[:, p, k:k + 1], ALU.subtract, ALU.mult)
        i.then_inc(self.s_xn, 1)
        if self.top is not None:
            dve.wait_ge(self.s_xn, u + 1)
            top = self.top[:, u:u + 1] if isinstance(u, int) else self.top[:, bass.ds(u, 1)]
            self.nc.vector.tensor_reduce(top, self.xn[:, p, :], AX.X, ALU.max, apply_absolute_value=True).then_inc(self.s_top, 1)

    def pe_turn(self, pe, u, p):
        pe.wait_ge(self.s_xn, u + 1)
        after(pe, self.s_stored, u)
        for k in range(self.G):
            i = self.nc.tensor.transpose(self.psum[:, k * F:(k + 1) * F], self.xn[:, p, k * F:(k + 1) * F], self.g.ident[:, :])
        i.then_inc(self.s_turned, 1)

    def act_store(self, act, u, p):
        act.wait_ge(self.s_turned, u + 1)
        self.nc.scalar.copy(self.batches(self.g.XT, u),
                            self.psum[:, 0:self.G * F].rearrange("p (a f) -> p a f", a=self.G)).then_inc(self.s_stored, 1)


def layer_load(nc, g, d, masked, top):
    with ExitStack() as ctx:
        L = Layer(nc, ctx, "ld")
        s_const = L.sem("const")
        s_x = [L.sem(f"x{i}") for i in range(4)]
        s_keep = L.sem("keep")
        s_xd, s_kept = L.sem("x_done"), L.sem("mask")
        ps = [L.psum(f"turn{i}", [128, 512]) for i in range(2)]
        mask8 = L.sb("mask8", [T, NB], U8)
        N = Norm(L, g, GB, s_xd, ps[0], masked=masked, top=g.top if top else None)
        N.s_top = L.sem('top')
        block = ctx.enter_context(nc.Block())

        @block.sync
        def _(sp):
            sp.dma_start(g.ident[:, :], d["c_ident"]).then_inc(s_const, 16)
            sp.dma_start(g.headmask[:, :], d["c_headmask"]).then_inc(s_const, 16)
            sp.dma_start(mask8[:, :], d["mask_t"]).then_inc(s_const, 16)
            sp.dma_start(g.rank[:, :], d["c_rank"]).then_inc(s_const, 16)
            for i in range(4):
                b = NB // 4 * i
                sp.dma_start(g.X[:, b:b + NB // 4, :], d["x"][b:b + NB // 4].rearrange("b t f -> t b f")).then_inc(s_x[i], 16)

        @block.gpsimd
        def _(pool):
            nc.gpsimd.memset(g.minus_half[:, :], -0.5).then_inc(s_keep, 1)
            pool.wait_ge(s_keep, 1)
            pool.wait_ge(s_kept, 1)
            ticks(pool, NG, 2, lambda t, p: stage(t, p, 0, NG, lambda u, q: N.pool_rstd(pool, u, q)))

        @block.vector
        def _(dve):
            dve.wait_ge(s_const, 64)
            dve.nop().then_inc(g.s_constants, 1)
            nc.vector.tensor_copy(g.keep[:, :], mask8[:, :]).then_inc(s_kept, 1)
            for i in range(4):
                dve.wait_ge(s_x[i], 16)
            dve.nop().then_inc(s_xd, NG)

            def tick(t, p):
                stage(t, p, 0, NG, lambda u, q: N.dve_mean(dve, u, q))
                stage(t, p, 1, NG, lambda u, q: N.dve_xn(dve, u, q))
            ticks(dve, NG, 2, tick)

        @block.tensor
        def _(pe):
            pe.wait_ge(s_const, 64)
            ticks(pe, NG, 2, lambda t, p: stage(t, p, 1, NG, lambda u, q: N.pe_turn(pe, u, q)))

        @block.scalar
        def _(act):
            ticks(act, NG, 2, lambda t, p: stage(t, p, 1, NG, lambda u, q: N.act_store(act, u, q)))


def layer_heads(nc, g, d, name, H, wide, wq, wk, wv, wo, bq, bk, bv, bo, scale, masked_next, top=None):
    D = 64 if wide else 8
    I = H * D
    NT = I // 128
    HB = 4
    SB = H // HB
    DV = D + 1
    O_CUT = 3 if wide else H
    HALVES = H // 8

    def head_at(at):
        return 2 * (at % HB) + at // HB if wide else at

    with ExitStack() as ctx:
        L = Layer(nc, ctx, name)
        s_w = L.sem("weights")
        s_ctx = [L.sem("ctx_in_even"), L.sem("ctx_in_odd")]
        s_setup = L.sem("setup")
        s_q, s_v = L.sem("q_projected"), L.sem("kv_projected")
        s_qc, s_kc, s_vc = L.sem("q_copied"), L.sem("k_copied"), L.sem("v_copied")
        s_S, s_max, s_sub, s_P = L.sem("scores"), L.sem("max"), L.sem("shifted"), L.sem("probs")
        s_PT, s_PTc, s_O = L.sem("probs_turned"), L.sem("probs_copied"), L.sem("outputs")
        s_rec, s_on = L.sem("sum_inverse"), L.sem("normed")
        s_oT, s_oTc, s_wo, s_x = L.sem("out_turned"), L.sem("out_copied"), L.sem("projected"), L.sem("x_done")
        s_woc, s_xb = L.sem("projected_copied"), L.sem("x_part")
        Wq = L.sb("wq", [F, I])
        Wk = L.sb("wk", [CK, I])
        Wv = L.sb("wv", [CK, I])
        s_wn = 3
        if wo is not None:
            Wo = L.sb("wo", [128, NT, F])
            BO = L.sb("bo", [128, F])
            s_wn += 2
        if bq is not None:
            BQ, BK, BV = L.sb("bq", [128, 1]), L.sb("bk", [128, 1]), L.sb("bv", [NK, I])
            s_wn += 3
        cs = L.sb("ctx", [CK, 2, NK])
        qT = L.sb("qT", [128, NT, T])
        kT = L.sb("kT", [128, NT if wide else HB, NK])
        va = L.sb("values", [NK, 2, H, DV])
        Sx = L.sb("probs", [T, 2, H, NK])
        mx = L.sb("max", [T, H])
        PTs = L.sb("probsT", [NK, H, T])
        rec = L.sb("sum_inv", [T, H])
        on = L.sb("out", [T, 2, H, D])
        if wo is not None:
            oTs = L.sb("outT", [128, NT, T])
            ws = L.sb("projected", [T, F])
        if wide:
            psS = L.psum("S", [128, 2, 512])
            psPT = L.psum("PT", [128, 2, 512])
            psQ = L.psum("Q", [128, 512])
            psK = L.psum("K", [128, 512])
            psV = L.psum("V", [128, 512])
            psO = L.psum("O", [128, 512])
            pq, pk, pv = psQ[:, 0:512], psK[:, 0:NT * NK], psV[0:NK, 0:512]
            pO = [psO[:, 0:O_CUT * DV], psV[:, 0:(H - O_CUT) * DV]]
        else:
            psS = L.psum("S", [128, 4, 512])
            psPT = L.psum("PT", [128, 2, 512])
            psQ = L.psum("Q", [128, 512])
            psO = L.psum("KVO", [128, 512])
            pq, pk, pv = psQ[:, 0:128], psO[:, 0:NK], psO[0:NK, 128:256]
            pO = [psO[:, 256:256 + H * DV]]
        poT, pWo = psQ[:, 0:NT * T], psQ[:, 0:F]
        N = Norm(L, g, 1, s_x, psQ)
        N.masked, N.top = masked_next, top
        N.s_top = L.sem("top")
        LAG_X = 3
        LAG_T = 4
        LAGS = LAG_T
        block = ctx.enter_context(nc.Block())

        @block.sync
        def _(sp):
            sp.dma_start(Wq[:, :], wq).then_inc(s_w, 16)
            sp.dma_start(Wk[:, :], wk).then_inc(s_w, 16)
            sp.dma_start(Wv[:, :], wv).then_inc(s_w, 16)
            if wo is not None:
                sp.dma_start(Wo[:, :, :], wo).then_inc(s_w, 16)
                sp.dma_start(BO[:, :], bo.partition_broadcast(128)).then_inc(s_w, 16)
            if bq is not None:
                sp.dma_start(BQ[:, :], bq).then_inc(s_w, 16)
                sp.dma_start(BK[:, :], bk).then_inc(s_w, 16)
                sp.dma_start(BV[:, :], bv.partition_broadcast(NK)).then_inc(s_w, 16)

            def load(b, p):
                after(sp, s_v, b - 1)
                if isinstance(b, int):
                    src = d["ctx_t"][b]
                else:
                    src = d["ctx_t"][bass.ds(b, 1)].rearrange("a c k -> (a c) k")
                sp.dma_start(cs[:, p, :], src).then_inc(s_ctx[p], 16)
            ticks(sp, NB, LAGS, lambda t, p: stage(t, p, 0, NB, load))

        @block.tensor
        def _(pe):
            pe.wait_ge(s_w, 16 * s_wn)

            def project(b, p):
                pe.wait_ge(s_ctx[p], (b - p) * 8 + 16)
                if wo is not None:
                    after(pe, s_woc, b - 2)
                else:
                    after(pe, N.s_stored, b - LAG_T)
                after(pe, s_qc, b)
                x = g.XT[:, b, :] if isinstance(b, int) else g.XT[:, bass.ds(b, 1), :].rearrange("p a t -> p (a t)")
                for i in range(NT):
                    m = nc.tensor.matmul(pq[:, i * T:(i + 1) * T], Wq[:, i * 128:(i + 1) * 128], x, start=True, stop=True)
                m.then_inc(s_q, 1)
                after(pe, s_kc, b)
                after(pe, s_vc, b)
                after(pe, s_on, b - 1)
                for i in range(NT):
                    m = nc.tensor.matmul(pk[:, i * NK:(i + 1) * NK], Wk[:, i * 128:(i + 1) * 128], cs[:, p, :], start=True, stop=True)
                nc.tensor.matmul(pv, cs[:, p, :], Wv[:, :], start=True, stop=True).then_inc(s_v, 1)

            def scores(b, p):
                pe.wait_ge(s_qc, b + 1)
                pe.wait_ge(s_kc, b + 1)
                after(pe, s_sub, b)
                if wide:
                    for h in range(H):
                        r = 64 * (h % 2)
                        m = nc.tensor.matmul(psS[:, h % 2, (h // 2) * NK:(h // 2 + 1) * NK], qT[r:r + 64, h // 2, :],
                                             kT[r:r + 64, h // 2, :], start=True, stop=True)
                else:
                    for i in range(SB):
                        r = 32 * i
                        m = nc.tensor.matmul(psS[:, i, 0:HB * NK], qT[r:r + 32, 0, :],
                                             kT[r:r + 32, :, :].rearrange("p h k -> p (h k)"), start=True, stop=True)
                m.then_inc(s_S, 1)

            def turn(b, p, half):
                if half == 0:
                    pe.wait_ge(s_P, b + 1)
                after(pe, s_PTc, b * HALVES + half)
                for h in range(8):
                    m = nc.tensor.transpose(psPT[0:NK, h // 4, (h % 4) * T:(h % 4 + 1) * T], Sx[:, p, 8 * half + h, :], g.ident[:, :])
                m.then_inc(s_PT, 1)

            def values(b, p, half):
                pe.wait_ge(s_PTc, b * HALVES + half + 1)
                if half == 0:
                    after(pe, s_on, b)
                    last = isinstance(b, int) and b == NB - 1
                    pe.wait_ge(s_kc, NB if last else b + 2)
                    pe.wait_ge(s_vc, NB if last else b + 2)
                for at in range(8 * half, 8 * half + 8):
                    h = head_at(at)
                    k = 0 if h < O_CUT else 1
                    c = (h - k * O_CUT) * DV
                    m = nc.tensor.matmul(pO[k][:, c:c + DV], PTs[:, at, :], va[:, p, h, :], start=True, stop=True)
                m.then_inc(s_O, 1)

            def turn_out(b, p):
                pe.wait_ge(s_on, b + 1)
                after(pe, N.s_stored, b + 3 - LAG_T)
                pe.wait_ge(s_qc, b + 3 if not isinstance(b, int) else min(b + 3, NB))
                o = on[:, p, :, :].rearrange("p h e -> p (h e)")
                for i in range(NT):
                    m = nc.tensor.transpose(poT[:, i * T:(i + 1) * T], o[:, i * 128:(i + 1) * 128], g.ident[:, :])
                m.then_inc(s_oT, 1)

            def project_out(b, p):
                pe.wait_ge(s_oTc, b + 1)
                for i in range(NT):
                    m = nc.tensor.matmul(pWo, oTs[:, i, :], Wo[:, i, :], start=(i == 0), stop=(i == NT - 1))
                m.then_inc(s_wo, 1)

            def turn_xn(b, p):
                pe.wait_ge(s_qc, b + LAG_T + 1 if not isinstance(b, int) else min(b + LAG_T + 1, NB))
                if wo is not None:
                    pe.wait_ge(s_woc, b + LAG_T - 2 if not isinstance(b, int) else min(b + LAG_T - 2, NB))
                N.pe_turn(pe, b, p)

            def tick(t, p):
                stage(t, p, 0, NB, project)
                stage(t, p, 1, NB, lambda b, q: turn(b, q, 0))
                stage(t, p, 0, NB, scores)
                stage(t, p, LAG_T, NB, turn_xn)
                for half in range(1, HALVES):
                    stage(t, p, 1, NB, lambda b, q, half=half: turn(b, q, half))
                if wo is not None:
                    stage(t, p, 2, NB, turn_out)
                    stage(t, p, 2, NB, project_out)
                for half in range(HALVES):
                    stage(t, p, 1, NB, lambda b, q, half=half: values(b, q, half))
            ticks(pe, NB, LAGS, tick)

        @block.scalar
        def _(act):
            act.wait_ge(s_w, 16 * s_wn)

            def queries(b, p):
                act.wait_ge(s_q, b + 1)
                after(act, s_S, b)
                i = pq.rearrange("p (n t) -> p n t", n=NT)
                if bq is None:
                    m = nc.scalar.copy(qT[:, :, :], i)
                else:
                    m = nc.scalar.activation(qT[:, :, :], i, ACT.Identity, bias=BQ[:, 0:1])
                m.then_inc(s_qc, 1)

            def probs(b, p):
                act.wait_ge(s_sub, b + 1)
                nc.scalar.activation(Sx[:, p, :, :], Sx[:, p, :, :], ACT.Exp, scale=scale).then_inc(s_P, 1)

            def copy_turned(b, p, half):
                act.wait_ge(s_PT, b * HALVES + half + 1)
                after(act, s_O, (b - 1) * HALVES + half + 1)
                nc.scalar.copy(PTs[:, 8 * half:8 * half + 8, :],
                               psPT[0:NK, :, :].rearrange("p a (h t) -> p (a h) t", h=4)).then_inc(s_PTc, 1)

            def out_copy(b, p):
                act.wait_ge(s_oT, b + 1)
                after(act, s_wo, b)
                nc.scalar.copy(oTs[:, :, :], poT.rearrange("p (n t) -> p n t", n=NT)).then_inc(s_oTc, 1)

            def projected_copy(b, p):
                act.wait_ge(s_wo, b + 1)
                after(act, s_xb, b)
                nc.scalar.copy(ws[:, :], pWo).then_inc(s_woc, 1)

            def tick(t, p):
                stage(t, p, 0, NB, queries)
                stage(t, p, 1, NB, lambda b, q: copy_turned(b, q, 0))
                stage(t, p, LAG_T, NB, lambda b, q: N.act_store(act, b, q))
                for half in range(1, HALVES):
                    stage(t, p, 1, NB, lambda b, q, half=half: copy_turned(b, q, half))
                if wo is not None:
                    stage(t, p, 2, NB, out_copy)
                    stage(t, p, 2, NB, projected_copy)
                stage(t, p, 0, NB, probs)
            ticks(act, NB, LAGS, tick)

        @block.gpsimd
        def _(pool):
            def update(b, p):
                x = N.one(g.X, b, 0)
                if wo is None:
                    apart(pool, g, (s_on, b + 1))
                    nc.gpsimd.tensor_tensor(x, x, on[:, p, :, :].rearrange("p h e -> p (h e)"), ALU.add).then_inc(s_x, 1)
                else:
                    apart(pool, g, (s_woc, b + 1))
                    nc.gpsimd.tensor_tensor(x, x, ws[:, :], ALU.add).then_inc(s_xb, 1)
                    apart(pool, g, (s_xb, b + 1))
                    nc.gpsimd.tensor_tensor(x, x, BO[:, :], ALU.add).then_inc(s_x, 1)

            pool.wait_ge(s_w, 16 * s_wn)

            def tick(t, p):
                stage(t, p, LAG_X, NB, lambda b, q: N.pool_rstd(pool, b, q))
                stage(t, p, 2, NB, update)
            ticks(pool, NB, LAGS, tick)

        @block.vector
        def _(dve):
            nc.vector.memset(va[:, :, :, :], 1.0).then_inc(s_setup, 1)
            dve.wait_ge(s_setup, 1)
            dve.wait_ge(s_w, 16 * s_wn)

            def keys(b, p):
                dve.wait_ge(s_v, b + 1)
                after(dve, s_S, b)
                if wide:
                    m = nc.vector.tensor_copy(kT[:, :, :], pk.rearrange("p (n k) -> p n k", n=NT))
                else:
                    k4 = pk.unsqueeze(1).broadcast_to([128, HB, NK])
                    m4 = g.headmask[:, :].unsqueeze(2).broadcast_to([128, HB, NK])
                    if bk is None:
                        m = nc.vector.tensor_tensor(kT[:, :, :], k4, m4, ALU.mult)
                    else:
                        m = nc.vector.scalar_tensor_tensor(kT[:, :, :], k4, BK[:, 0:1], m4, ALU.add, ALU.mult)
                m.then_inc(s_kc, 1)

            def values(b, p):
                after(dve, s_O, (b - 1) * HALVES)
                v = pv.rearrange("p (h e) -> p h e", h=H)
                if bv is None:
                    m = nc.vector.tensor_copy(va[:, p, :, 0:D], v)
                else:
                    m = nc.vector.tensor_tensor(va[:, p, :, 0:D], v, BV[:, :].rearrange("p (h e) -> p h e", h=H), ALU.add)
                m.then_inc(s_vc, 1)

            def shift(b, p):
                dve.wait_ge(s_S, b + 1)
                after(dve, s_sub, b)
                s = psS[:, :, 0:HB * NK].rearrange("p a (h k) -> p a h k", h=HB)
                nc.vector.tensor_reduce(mx[:, :].rearrange("p (a h) -> p a h", a=SB), s, AX.X, ALU.max).then_inc(s_max, 1)
                dve.wait_ge(s_max, b + 1)
                after(dve, s_PT, (b - 1) * HALVES)
                nc.vector.tensor_tensor(Sx[:, p, :, :].rearrange("p (a h) k -> p a h k", a=SB), s,
                                        mx[:, :].rearrange("p (a h) -> p a h", a=SB).unsqueeze(3).broadcast_to([128, SB, HB, NK]),
                                        ALU.subtract).then_inc(s_sub, 1)

            parts = [(0, O_CUT)] + ([(O_CUT, H)] if wide else [])

            def normalise(b, p):
                dve.wait_ge(s_O, (b + 1) * HALVES)
                after(dve, s_on, b)
                for k, (a, z) in enumerate(parts):
                    o = pO[k].rearrange("p (h e) -> p h e", e=DV)
                    i = nc.vector.reciprocal(rec[:, a:z], o[:, :, D])
                i.then_inc(s_rec, 1)
                dve.wait_ge(s_rec, b + 1)
                if wo is not None:
                    after(dve, s_oT, b - 1)
                else:
                    after(dve, s_x, b - 1)
                for k, (a, z) in enumerate(parts):
                    o = pO[k].rearrange("p (h e) -> p h e", e=DV)
                    i = nc.vector.tensor_tensor(on[:, p, a:z, :], o[:, :, 0:D],
                                                rec[:, a:z].unsqueeze(2).broadcast_to([128, z - a, D]), ALU.mult)
                i.then_inc(s_on, 1)

            def tick(t, p):
                stage(t, p, 2, NB, normalise)
                stage(t, p, 0, NB, keys)
                stage(t, p, 0, NB, values)
                stage(t, p, LAG_X, NB, lambda b, q: N.dve_mean(dve, b, q))
                stage(t, p, 0, NB, shift)
                stage(t, p, LAG_X, NB, lambda b, q: N.dve_xn(dve, b, q))
            ticks(dve, NB, LAGS, tick)



def group(t, u, n=GB):
    return t[:, u * n:(u + 1) * n, :] if isinstance(u, int) else t[:, bass.ds(u * n, n), :]


def flat(t):
    return t.rearrange("p a f -> p (a f)")


def layer_router(nc, g, d, name, wg, bg, softmax_all):
    E = 8
    with ExitStack() as ctx:
        L = Layer(nc, ctx, name)
        s_w, s_logit, s_sb = L.sem("weights"), L.sem("logits"), L.sem("logits_copied")
        s_turned, s_kept, s_exp, s_arg, s_link = L.sem("turned"), L.sem("kept"), L.sem("exp"), L.sem("exp_in"), L.sem("link")
        Wg = L.sb("wg", [F, E])
        Bg = L.sb("bg", [E, 1])
        ls = L.sb("logits", [E, 2, GB * T])
        V = L.sb("values", [T, NB, E])
        first, second = L.sb("first", [T, NB, E]), L.sb("second", [T, NB, E])
        top, low, rank = L.sb("top", [T, NB]), L.sb("low", [T, NB]), L.sb("rank_top", [T, NB])
        psL = L.psum("L", [128, 2, 512])
        psT = L.psum("T", [128, 2, 512])
        block = ctx.enter_context(nc.Block())

        @block.sync
        def _(sp):
            sp.dma_start(Wg[:, :], wg).then_inc(s_w, 16)
            if bg is not None:
                sp.dma_start(Bg[:, :], bg).then_inc(s_w, 16)

        @block.tensor
        def _(pe):
            pe.wait_ge(s_w, 16 if bg is None else 32)

            def logits(u, p):
                after(pe, s_sb, u - 1)
                nc.tensor.matmul(psL[0:E, p, :], Wg[:, :], flat(group(g.XT, u)), start=True, stop=True).then_inc(s_logit, 1)

            def turn(u, p):
                apart(pe, g,
                      (s_sb, u + 1),
                      (s_kept, u - 1))
                for k in range(GB):
                    i = nc.tensor.transpose(psT[:, p, k * E:(k + 1) * E], ls[:, p, k * T:(k + 1) * T], g.ident[0:E, 0:E])
                i.then_inc(s_turned, 1)

            def tick(t, p):
                stage(t, p, 0, NG, logits)
                stage(t, p, 1, NG, turn)
            ticks(pe, NG, 2, tick)

        @block.scalar
        def _(act):
            act.wait_ge(s_w, 16 if bg is None else 32)

            def copy(u, p):
                act.wait_ge(s_logit, u + 1)
                after(act, s_turned, u - 1)
                if bg is None:
                    i = nc.scalar.copy(ls[:, p, :], psL[0:E, p, :])
                else:
                    i = nc.scalar.activation(ls[:, p, :], psL[0:E, p, :], ACT.Identity, bias=Bg[:, 0:1])
                i.then_inc(s_sb, 1)
            ticks(act, NG, 2, lambda t, p: stage(t, p, 0, NG, copy))
            act.wait_ge(s_arg, 1)
            if softmax_all:
                nc.scalar.activation(V[:, :, :], V[:, :, :], ACT.Exp).then_inc(s_exp, 1)
            else:
                nc.scalar.activation(low[:, :], low[:, :], ACT.Exp).then_inc(s_exp, 1)

        @block.vector
        def _(dve):
            def keep(u, p):
                dve.wait_ge(s_turned, u + 1)
                nc.vector.tensor_copy(group(V, u), psT[:, p, 0:GB * E].rearrange("p (a e) -> p a e", a=GB)).then_inc(s_kept, 1)
            ticks(dve, NG, 2, lambda t, p: stage(t, p, 1, NG, keep))
            dve.wait_ge(s_kept, NG)
            link = Link(dve, s_link, 0)
            link.per = 1000
            wide = lambda t: t[:, :].unsqueeze(2).broadcast_to([T, NB, E])
            ranks = g.rank[:, :].unsqueeze(1).broadcast_to([T, NB, E])
            if softmax_all:
                link(nc.vector.tensor_reduce(top[:, :], V[:, :, :], AX.X, ALU.max))
                nc.vector.tensor_tensor(V[:, :, :], V[:, :, :], wide(top), ALU.subtract).then_inc(s_arg, 1)
                dve.wait_ge(s_exp, 1)
                link(nc.vector.tensor_reduce(top[:, :], V[:, :, :], AX.X, ALU.add))
                link(nc.vector.reciprocal(low[:, :], top[:, :]))
                link(nc.vector.tensor_tensor(V[:, :, :], V[:, :, :], wide(low), ALU.mult))

            def choose(one, best):
                link(nc.vector.tensor_reduce(best[:, :], V[:, :, :], AX.X, ALU.max))
                link(nc.vector.tensor_tensor(one[:, :, :], V[:, :, :], wide(best), ALU.is_equal))
                link(nc.vector.tensor_tensor(one[:, :, :], one[:, :, :], ranks, ALU.mult))
                link(nc.vector.tensor_reduce(rank[:, :], one[:, :, :], AX.X, ALU.max))
                link(nc.vector.tensor_tensor(one[:, :, :], one[:, :, :], wide(rank), ALU.is_equal))

            choose(first, top)
            if softmax_all:
                link(nc.vector.tensor_tensor(g.gate[:, :, :], V[:, :, :], first[:, :, :], ALU.mult))
            link(nc.vector.scalar_tensor_tensor(flat(V[:, :, :]), flat(first[:, :, :]), -3e38, flat(V[:, :, :]), ALU.mult, ALU.add))
            choose(second, low)
            if softmax_all:
                link(nc.vector.tensor_tensor(second[:, :, :], second[:, :, :], wide(low), ALU.mult))
                link(nc.vector.tensor_tensor(g.gate[:, :, :], g.gate[:, :, :], second[:, :, :], ALU.add))
                link(nc.vector.tensor_tensor(top[:, :], top[:, :], low[:, :], ALU.add))
                link(nc.vector.tensor_scalar(top[:, :], top[:, :], 1e-8, None, ALU.add))
                link(nc.vector.reciprocal(low[:, :], top[:, :]))
                link(nc.vector.tensor_tensor(g.gate[:, :, :], g.gate[:, :, :], wide(low), ALU.mult))
            else:
                nc.vector.tensor_tensor(low[:, :], low[:, :], top[:, :], ALU.subtract).then_inc(s_arg, 1)
                dve.wait_ge(s_exp, 1)
                link(nc.vector.tensor_scalar(top[:, :], low[:, :], 1.0, None, ALU.add))
                link(nc.vector.reciprocal(rank[:, :], top[:, :]))
                link(nc.vector.tensor_tensor(low[:, :], low[:, :], rank[:, :], ALU.mult))
                link(nc.vector.tensor_tensor(g.gate[:, :, :], first[:, :, :], wide(rank), ALU.mult))
                link(nc.vector.tensor_tensor(second[:, :, :], second[:, :, :], wide(low), ALU.mult))
                link(nc.vector.tensor_tensor(g.gate[:, :, :], g.gate[:, :, :], second[:, :, :], ALU.add))


def layer_experts(nc, g, d):
    E, M = 8, 4
    with ExitStack() as ctx:
        L = Layer(nc, ctx, "moe")
        s_w, s_h, s_act, s_y, s_add = L.sem("weights"), L.sem("hidden"), L.sem("gelu"), L.sem("outputs"), L.sem("added")
        s_gs, s_gt, s_gc, s_by, s_x = L.sem("gates"), L.sem("gates_turned"), L.sem("gates_copied"), L.sem("bias_out"), L.sem("x_done")
        W1 = L.sb("w1", [F, E, M * 128])
        W2 = L.sb("w2", [128, E, M, F])
        B1 = L.sb("b1", [128, E, M])
        B2 = L.sb("b2", [E, F])
        hs = L.sb("hidden", [128, 2, M, GB * T])
        gs = L.sb("gates", [T, GB, E])
        gT = L.sb("gatesT", [E, GB * T])
        psH, psY = L.psum("H", [128, M, 512]), L.psum("Y", [128, 2, 512])
        psG, psN = L.psum("G", [128, 512]), L.psum("N", [128, 512])
        N = Norm(L, g, GB, s_x, psN, masked=True)
        LAGS = 4
        block = ctx.enter_context(nc.Block())

        @block.sync
        def _(sp):
            for t, k in ((W1, "m0_w1"), (W2, "m0_w2"), (B1, "m0_b1"), (B2, "m0_b2")):
                sp.dma_start(t[:], d[k]).then_inc(s_w, 16)

        @block.tensor
        def _(pe):
            pe.wait_ge(s_w, 64)

            def hidden(u, p, e):
                for m in range(M):
                    n = (u * E + e) * M + m
                    after(pe, s_act, n - M + 1)
                    nc.tensor.matmul(psH[:, m, :], W1[:, e, m * 128:(m + 1) * 128], flat(group(g.XT, u)),
                                     start=True, stop=True).then_inc(s_h, 1)

            def outputs(u, p, e):
                n = u * E + e
                pe.wait_ge(s_act, (n + 1) * M)
                after(pe, s_add, n - 1)
                for k in range(GB):
                    for m in range(M):
                        i = nc.tensor.matmul(psY[:, e % 2, k * F:(k + 1) * F], hs[:, e % 2, m, k * T:(k + 1) * T], W2[:, e, m, :],
                                             start=(m == 0), stop=(m == M - 1))
                i.then_inc(s_y, 1)

            def turn_gates(u, p):
                pe.wait_ge(s_gs, u + 1)
                after(pe, s_x, u)
                for k in range(GB):
                    i = nc.tensor.transpose(psG[0:E, k * T:(k + 1) * T], gs[:, k, :], g.ident[:, :])
                i.then_inc(s_gt, 1)

            def bias(u, p):
                pe.wait_ge(s_gc, u + 1)
                for k in range(GB):
                    i = nc.tensor.matmul(psG[:, k * F:(k + 1) * F], gT[:, k * T:(k + 1) * T], B2[:, :], start=True, stop=True)
                i.then_inc(s_by, 1)

            def tick(t, p):
                for e in range(E):
                    stage(t, p, 0, NG, lambda u, q: hidden(u, q, e))
                    if e == 0:
                        stage(t, p, 1, NG, lambda u, q: outputs(u, q, E - 1))
                    else:
                        stage(t, p, 0, NG, lambda u, q: outputs(u, q, e - 1))
                    if e == 2:
                        stage(t, p, 0, NG, turn_gates)
                        stage(t, p, 2, NG, lambda u, q: N.pe_turn(pe, u, q))
                    if e == 4:
                        stage(t, p, 0, NG, bias)
            ticks(pe, NG, LAGS, tick)

        @block.scalar
        def _(act):
            act.wait_ge(s_w, 64)

            def gelu(u, p, e):
                for m in range(M):
                    act.wait_ge(s_h, (u * E + e) * M + m + 1)
                    if m == 0:
                        after(act, s_y, u * E + e - 1)
                    nc.scalar.activation(hs[:, e % 2, m, :], psH[:, m, :], ACT.Gelu_apprx_tanh, bias=B1[:, e, m:m + 1]).then_inc(s_act, 1)

            def gates(u, p):
                act.wait_ge(s_gt, u + 1)
                after(act, s_by, u)
                nc.scalar.copy(gT[:, :], psG[0:E, :]).then_inc(s_gc, 1)

            def tick(t, p):
                for e in range(E):
                    stage(t, p, 0, NG, lambda u, q: gelu(u, q, e))
                    if e == 3:
                        stage(t, p, 0, NG, gates)
                        stage(t, p, 2, NG, lambda u, q: N.act_store(act, u, q))
            ticks(act, NG, LAGS, tick)

        @block.gpsimd
        def _(pool):
            def gates(u, p):
                after(pool, s_gt, u)
                nc.gpsimd.tensor_copy(gs[:, :, :], group(g.gate, u)).then_inc(s_gs, 1)

            def tick(t, p):
                stage(t, p, 0, NG, gates)
                stage(t, p, 1, NG, lambda u, q: N.pool_rstd(pool, u, q))
            ticks(pool, NG, LAGS, tick)

        @block.vector
        def _(dve):
            def add(u, p, e):
                n = u * E + e
                dve.wait_ge(s_y, n + 1)
                after(dve, s_add, n)
                for k in range(GB):
                    x = N.one(g.X, u, k)
                    b = u * GB + k
                    w = g.gate[:, b, e:e + 1] if isinstance(b, int) else g.gate[:, bass.ds(b, 1), e]
                    i = nc.vector.scalar_tensor_tensor(x, psY[:, e % 2, k * F:(k + 1) * F], w, x, ALU.mult, ALU.add)
                i.then_inc(s_add, 1)
                if e == E - 1:
                    dve.wait_ge(s_by, u + 1)
                    dve.wait_ge(s_add, n + 1)
                    x = flat(group(g.X, u))
                    nc.vector.tensor_tensor(x, psG[:, :], x, ALU.add).then_inc(s_x, 1)

            def tick(t, p):
                stage(t, p, 1, NG, lambda u, q: add(u, q, E - 1))
                stage(t, p, 1, NG, lambda u, q: N.dve_mean(dve, u, q))
                for e in range(E - 1):
                    stage(t, p, 0, NG, lambda u, q: add(u, q, e))
                    if e == 0:
                        stage(t, p, 1, NG, lambda u, q: N.dve_xn(dve, u, q))
            ticks(dve, NG, LAGS, tick)


def layer_channel_mix(nc, g, d):
    with ExitStack() as ctx:
        L = Layer(nc, ctx, "mix")
        s_w, s_omu = L.sem("weights"), L.sem("one_minus_mu")
        s_r0, s_k0, s_xr, s_xk = L.sem("r_part"), L.sem("k_part"), L.sem("xr"), L.sem("xk")
        s_zr, s_zk, s_tanh, s_relu, s_sq = L.sem("zr"), L.sem("zk"), L.sem("tanh"), L.sem("relu"), L.sem("squared")
        s_v, s_rv, s_x = L.sem("v"), L.sem("rv"), L.sem("x_done")
        Wr, Wk, Wv = (L.sb(n, [F, F]) for n in ("wr", "wk", "wv"))
        mu = L.sb("mu", [F, 2])
        omu = L.sb("one_minus_mu", [F, 2])
        xm = L.sb("mixed", [F, 2, GB, T])
        rs = L.sb("tanh", [T, 2, GB * F])
        ks = L.sb("kact", [F, 2, GB * T])
        rv = L.sb("rv", [T, GB * F])
        psR, psK, psV, psN = (L.psum(n, [128, 512]) for n in ("R", "K", "V", "N"))
        N = Norm(L, g, GB, s_x, psN, top=g.top)
        N.s_top = L.sem("top")
        LAGS = 4
        block = ctx.enter_context(nc.Block())

        @block.sync
        def _(sp):
            for t, k in ((Wr, "m1_wr"), (Wk, "m1_wk"), (Wv, "m1_wv"), (mu, "m1_mu")):
                sp.dma_start(t[:], d[k]).then_inc(s_w, 16)

        @block.tensor
        def _(pe):
            pe.wait_ge(s_w, 64)

            def inner(u, p):
                pe.wait_ge(s_xr, u + 1)
                after(pe, s_tanh, u)
                for k in range(GB):
                    i = nc.tensor.matmul(psR[:, k * F:(k + 1) * F], xm[:, 0, k, :], Wr[:, :], start=True, stop=True)
                i.then_inc(s_zr, 1)
                pe.wait_ge(s_xk, u + 1)
                after(pe, s_relu, u)
                nc.tensor.matmul(psK[:, :], Wk[:, :], flat(xm[:, 1, :, :]), start=True, stop=True).then_inc(s_zk, 1)

            def outer(u, p):
                pe.wait_ge(s_sq, u + 1)
                after(pe, s_rv, u)
                for k in range(GB):
                    i = nc.tensor.matmul(psV[:, k * F:(k + 1) * F], ks[:, p, k * T:(k + 1) * T], Wv[:, :], start=True, stop=True)
                i.then_inc(s_v, 1)

            def tick(t, p):
                stage(t, p, 0, NG, inner)
                stage(t, p, 1, NG, outer)
                stage(t, p, 3, NG, lambda u, q: N.pe_turn(pe, u, q))
            ticks(pe, NG, LAGS, tick)

        @block.scalar
        def _(act):
            def inner(u, p):
                act.wait_ge(s_zr, u + 1)
                after(act, s_rv, u - 1)
                nc.scalar.activation(rs[:, p, :], psR[:, :], ACT.Tanh, scale=0.5).then_inc(s_tanh, 1)
                act.wait_ge(s_zk, u + 1)
                after(act, s_v, u - 1)
                nc.scalar.activation(ks[:, p, :], psK[:, :], ACT.Relu).then_inc(s_relu, 1)
                act.wait_ge(s_relu, u + 1)
                nc.scalar.activation(ks[:, p, :], ks[:, p, :], ACT.Square).then_inc(s_sq, 1)

            def tick(t, p):
                stage(t, p, 0, NG, inner)
                stage(t, p, 3, NG, lambda u, q: N.act_store(act, u, q))
            ticks(act, NG, LAGS, tick)

        @block.gpsimd
        def _(pool):
            ticks(pool, NG, LAGS, lambda t, p: stage(t, p, 2, NG, lambda u, q: N.pool_rstd(pool, u, q)))

        @block.vector
        def _(dve):
            dve.wait_ge(s_w, 64)
            nc.vector.tensor_scalar(omu[:, :], mu[:, :], -1.0, 1.0, ALU.mult, ALU.add).then_inc(s_omu, 1)
            dve.wait_ge(s_omu, 1)

            def mix(u, p):
                x = group(g.XT, u)
                for j, (part, done, used) in enumerate(((s_r0, s_xr, s_zr), (s_k0, s_xk, s_zk))):
                    after(dve, used, u)
                    nc.vector.tensor_scalar(xm[:, j, :, :], x, mu[:, j:j + 1], None, ALU.mult).then_inc(part, 1)
                for j, (part, done, used) in enumerate(((s_r0, s_xr, s_zr), (s_k0, s_xk, s_zk))):
                    dve.wait_ge(part, u + 1)
                    m = xm[:, j, :, 1:T]
                    nc.vector.scalar_tensor_tensor(m, x[:, :, 0:T - 1], omu[:, j:j + 1], m, ALU.mult, ALU.add).then_inc(done, 1)

            def update(u, p):
                dve.wait_ge(s_v, u + 1)
                dve.wait_ge(s_tanh, u + 1)
                after(dve, s_x, u)
                nc.vector.scalar_tensor_tensor(rv[:, :], rs[:, p, :], 1.0, psV[:, :], ALU.add, ALU.mult).then_inc(s_rv, 1)
                dve.wait_ge(s_rv, u + 1)
                x = flat(group(g.X, u))
                nc.vector.scalar_tensor_tensor(x, rv[:, :], 0.5, x, ALU.mult, ALU.add).then_inc(s_x, 1)

            def tick(t, p):
                stage(t, p, 0, NG, mix)
                stage(t, p, 2, NG, update)
                stage(t, p, 2, NG, lambda u, q: N.dve_mean(dve, u, q))
                stage(t, p, 3, NG, lambda u, q: N.dve_xn(dve, u, q))
            ticks(dve, NG, LAGS, tick)




BIT_COLS = {"d2v": (0, 128), "img": (128, 256), "txt": (256, 384), "att0": (384, 512), "att1": (512, 640),
            "f1": (640, 1664), "f2": (1664, 2176)}
BIT_AT = {k: i for i, k in enumerate(BIT_COLS)}


def quant_scale(nc, dve, link, tops, one, out, floor, levels):
    link(nc.vector.tensor_scalar(out[:, 0:1], one, floor, 1.0 / levels, ALU.max, ALU.mult))
    link(nc.vector.reciprocal(out[:, 1:2], out[:, 0:1]))


def layer_bit_weights(nc, g, d):
    n = len(BIT_COLS)
    with ExitStack() as ctx:
        L = Layer(nc, ctx, "bw")
        s_w, s_part, s_all, s_link = L.sem("weights"), L.sem("sums"), L.sem("totals"), L.sem("link")
        raw = L.sb("raw", [128, 2176])
        neg = L.sb("negative", [128, 1024])
        count = L.sb("inverse_counts", [128, n])
        sums, total, cut = L.sb("sums", [128, n]), L.sb("totals", [128, n]), L.sb("cuts", [128, 2, n])
        block = ctx.enter_context(nc.Block())

        @block.sync
        def _(sp):
            sp.dma_start(raw[0:CK, 0:128], d["b_d2v_w"]).then_inc(s_w, 16)
            sp.dma_start(raw[:, 128:2176], d["b_rest_w"]).then_inc(s_w, 16)
            sp.dma_start(count[:, :], d["c_bit_inverse_counts"]).then_inc(s_w, 16)

        @block.gpsimd
        def _(pool):
            pool.wait_ge(s_part, 1)
            nc.gpsimd.partition_all_reduce(total[:, :], sums[:, :], 128, RADD).then_inc(s_all, 1)

        @block.vector
        def _(dve):
            link = Link(dve, s_link, 1000)
            link(nc.vector.memset(raw[96:128, 0:128], 0.0))
            dve.wait_ge(s_w, 48)
            for i, (a, z) in enumerate(BIT_COLS.values()):
                k = nc.vector.tensor_reduce(sums[:, i:i + 1], raw[:, a:z], AX.X, ALU.add, apply_absolute_value=True)
            k.then_inc(s_part, 1)
            dve.wait_ge(s_all, 1)
            link(nc.vector.tensor_tensor(total[:, :], total[:, :], count[:, :], ALU.mult))
            link(nc.vector.tensor_scalar(g.ws[:, :], total[:, :], 1e-5, None, ALU.max))
            link(nc.vector.tensor_scalar(cut[:, 0, :], g.ws[:, :], 0.5, None, ALU.mult))
            link(nc.vector.tensor_scalar(cut[:, 1, :], g.ws[:, :], -0.5, None, ALU.mult))
            for i, (a, z) in enumerate(BIT_COLS.values()):
                link(nc.vector.tensor_scalar(neg[:, 0:z - a], raw[:, a:z], cut[:, 1, i:i + 1], None, ALU.is_lt))
                link(nc.vector.scalar_tensor_tensor(g.qw[:, a:z], raw[:, a:z], cut[:, 0, i:i + 1], neg[:, 0:z - a],
                                                    ALU.is_gt, ALU.subtract))


def layer_image(nc, g, d):
    CH = GB * NK
    with ExitStack() as ctx:
        L = Layer(nc, ctx, "im")
        s_in, s_b, s_link = L.sem("ctx_in"), L.sem("biases"), L.sem("link")
        s_top, s_all = L.sem("top"), L.sem("largest")
        s_avg = L.sem("average")
        A = L.sb("features", [128, NB, NK])
        qf = L.sb("shifted", [128, 2, CH])
        qb = L.sb("quantised", [128, 2, CH], BF16)
        ko = L.sb("keys", [128, 2, 2, CH])
        tops, one, most = L.sb("tops", [128, NG]), L.sb("one", [128, 1]), L.sb("most", [128, 1])
        scale, cs = L.sb("scale", [128, 2]), L.sb("product_scale", [128, 2])
        Bv, Bi, Ba = L.sb("b_d2v", [128, 1]), L.sb("b_img", [128, 1]), L.sb("b_att", [128, 2])
        ps = L.psum("out", [128, 4, 512])
        rounds = [("vis", ["d2v"]), ("img", ["img"]), ("key", ["att0", "att1"])]
        s_q, s_qf, s_mm, s_out, s_max = ([L.sem(f"{r}_{n}") for r, _ in rounds]
                                         for n in ("quantised", "shifted", "product", "features", "max"))
        s_ready = L.sem("scales_ready")
        s_kout = [L.sem("keys_out_even"), L.sem("keys_out_odd")]
        keys = d["keys"].rearrange("b j p k -> p b j k")
        block = ctx.enter_context(nc.Block())

        def chunk(u):
            return flat(group(A, u))

        @block.sync
        def _(sp):
            sp.dma_start(A[0:CK, :, :], d["ctx_t"].rearrange("b c k -> c b k")).then_inc(s_in, 16)
            sp.dma_start(Bv[:, :], d["b_d2v_b"]).then_inc(s_b, 16)
            sp.dma_start(Bi[:, :], d["b_img_b"]).then_inc(s_b, 16)
            sp.dma_start(Ba[:, :], d["b_att_b"]).then_inc(s_b, 16)

            def out(u, p):
                sp.wait_ge(s_out[2], u + 1)
                for j in range(2):
                    dst = keys[:, u * GB:(u + 1) * GB, j, :] if isinstance(u, int) else keys[:, bass.ds(u * GB, GB), j, :]
                    sp.dma_start(dst, ko[:, p, j, :].rearrange("p (a k) -> p a k", a=GB)).then_inc(s_kout[p], 16)
            ticks(sp, NG, 2, lambda t, p: stage(t, p, 1, NG, out))
            for s in s_kout:
                sp.wait_ge(s, 16 * NG)

        @block.gpsimd
        def _(pool):
            for r in range(3):
                pool.wait_ge(s_top, r + 1)
                n = CK if r == 0 else 128
                if r == 0:
                    nc.gpsimd.memset(most[:, :], 0.0).then_inc(s_avg, 1)
                    pool.wait_ge(s_avg, 1)
                nc.gpsimd.partition_all_reduce(most[:, :], one[:, :], 128, RMAX).then_inc(s_all, 1)

        @block.vector
        def _(dve):
            link = Link(dve, s_link, 1000)
            link(nc.vector.memset(A[96:128, :, :], 0.0))
            dve.wait_ge(s_in, 16)
            link(nc.vector.tensor_reduce(one[:, :], flat(A[:, :, :]), AX.X, ALU.max, apply_absolute_value=True))
            for r, (name, outs) in enumerate(rounds):
                if r:
                    link(nc.vector.tensor_reduce(one[:, :], tops[:, :], AX.X, ALU.max))
                dve.nop().then_inc(s_top, 1)
                dve.wait_ge(s_all, r + 1)
                quant_scale(nc, dve, link, None, most[:, 0:1], scale, 1e-8, 127.0)
                for j, w in enumerate(outs):
                    i = BIT_AT[w]
                    link(nc.vector.tensor_tensor(cs[:, j:j + 1], g.ws[:, i:i + 1], scale[:, 0:1], ALU.mult))
                dve.nop().then_inc(s_ready, 1)
                if r == 2:
                    link(nc.vector.tensor_reduce(g.avg[:, :], A[:, :, :], AX.X, ALU.add))
                    link(nc.vector.tensor_scalar(g.avg[:, :], g.avg[:, :], 1.0 / NK, None, ALU.mult))

                def quantise(u, p):
                    after(dve, s_mm[r], u - 1)
                    nc.vector.tensor_scalar(qf[:, p, :], chunk(u), scale[:, 1:2], MAGIC, ALU.mult, ALU.add).then_inc(s_qf[r], 1)
                    dve.wait_ge(s_qf[r], u + 1)
                    nc.vector.tensor_scalar(qb[:, p, :], qf[:, p, :], MAGIC, None, ALU.subtract).then_inc(s_q[r], 1)

                def largest(u, p):
                    dve.wait_ge(s_out[r], u + 1)
                    top = tops[:, u:u + 1] if isinstance(u, int) else tops[:, bass.ds(u, 1)]
                    nc.vector.tensor_reduce(top, chunk(u), AX.X, ALU.max, apply_absolute_value=True).then_inc(s_max[r], 1)

                def tick(t, p):
                    stage(t, p, 0, NG, quantise)
                    if r < 2:
                        stage(t, p, 2, NG, largest)
                ticks(dve, NG, 2, tick)
                if r < 2:
                    dve.wait_ge(s_max[r], NG)

        @block.tensor
        def _(pe):
            for r, (name, outs) in enumerate(rounds):
                def product(u, p):
                    pe.wait_ge(s_q[r], u + 1)
                    after(pe, s_out[r], u - 1)
                    for j, w in enumerate(outs):
                        a, z = BIT_COLS[w]
                        i = nc.tensor.matmul(ps[:, 2 * p + j, 0:CH], g.qw[:, a:z], qb[:, p, :], start=True, stop=True)
                    i.then_inc(s_mm[r], 1)
                ticks(pe, NG, 2, lambda t, p: stage(t, p, 0, NG, product))
                if r < 2:
                    pe.wait_ge(s_out[r], NG)

        @block.scalar
        def _(act):
            act.wait_ge(s_b, 48)
            for r, (name, outs) in enumerate(rounds):
                act.wait_ge(s_ready, r + 1)

                def feature(u, p):
                    act.wait_ge(s_mm[r], u + 1)
                    if r < 2:
                        nc.scalar.activation(chunk(u), ps[:, 2 * p, 0:CH], ACT.Identity, bias=(Bv, Bi)[r][:, 0:1],
                                             scale=cs[:, 0:1]).then_inc(s_out[r], 1)
                        return
                    if not isinstance(u, int) or u >= 2:
                        act.wait_ge(s_kout[p], (u - p) * 16)
                    for j in range(2):
                        i = nc.scalar.activation(ko[:, p, j, :], ps[:, 2 * p + j, 0:CH], ACT.Identity, bias=Ba[:, j:j + 1],
                                                 scale=cs[:, j:j + 1])
                    i.then_inc(s_out[2], 1)
                ticks(act, NG, 2, lambda t, p: stage(t, p, 0, NG, feature))


def layer_fused(nc, g, d):
    D2 = 64
    with ExitStack() as ctx:
        L = Layer(nc, ctx, "fu")
        s_w, s_part, s_all, s_link, s_scale = L.sem("weights"), L.sem("part"), L.sem("largest"), L.sem("link"), L.sem("scale_ready")
        s_qf, s_q, s_f, s_fu = L.sem("shifted"), L.sem("quantised"), L.sem("text"), L.sem("fused0")
        s_end, s_endc, s_topd = L.sem("end_turned"), L.sem("end_stored"), L.sem("top")
        s_kd = [[L.sem(f"keys{a}_{n}") for n in ("even", "odd")] for a in range(2)]
        names = ("turned", "copied", "keys_turned", "keys_copied", "scores", "max", "shifted", "exp", "probs_turned",
                 "probs_copied", "outputs", "inverse", "normed", "fused_lo", "fused")
        s = [{n: L.sem(f"a{a}_{n}") for n in names} for a in range(2)]
        BT = L.sb("b_txt", [128, F])
        one, most, scale, cs = L.sb("one", [128, 1]), L.sb("most", [128, 1]), L.sb("scale", [128, 2]), L.sb("product_scale", [128, 1])
        qf = L.sb("shifted", [F, GB * T])
        qb = L.sb("quantised", [F, 2, GB * T], BF16)
        fu = [L.sb(f"fused{i}", [T, 2, GB, F]) for i in range(3)]
        fT = [L.sb(f"fusedT{a}", [F, GB, T]) for a in range(2)]
        kd = [L.sb(f"keys{a}", [128, 2, GB, NK]) for a in range(2)]
        kt = [L.sb(f"keys_turned{a}", [NK, GB, D2 + 1]) for a in range(2)]
        P = [L.sb(f"probs{a}", [T, GB, NK]) for a in range(2)]
        PT = [L.sb(f"probsT{a}", [NK, GB, T]) for a in range(2)]
        mx = [L.sb(f"max{a}", [T, GB]) for a in range(2)]
        rec = [L.sb(f"inverse{a}", [T, GB]) for a in range(2)]
        o = [L.sb(f"normed{a}", [T, GB, D2]) for a in range(2)]
        psF, psE = L.psum("F", [128, 512]), L.psum("E", [128, 512])
        psA = [L.psum(f"A{a}", [128, 512]) for a in range(2)]
        psB = [L.psum(f"B{a}", [128, 512]) for a in range(2)]
        psK = [L.psum(f"K{a}", [128, 512]) for a in range(2)]
        LAGS = 4
        keys = d["keys"].rearrange("b j p k -> p b j k")
        block = ctx.enter_context(nc.Block())

        @block.sync
        def _(sp):
            sp.dma_start(BT[:, :], d["b_txt_b"].partition_broadcast(128)).then_inc(s_w, 16)

            def load(u, p, a):
                after(sp, s[a]["scores"], u - 1)
                src = keys[:, u * GB:(u + 1) * GB, a, :] if isinstance(u, int) else keys[:, bass.ds(u * GB, GB), a, :]
                sp.dma_start(kd[a][:, p, :, :], src).then_inc(s_kd[a][p], 16)

            def tick(t, p):
                stage(t, p, 1, NG, lambda u, q: load(u, q, 1))
                stage(t, p, 0, NG, lambda u, q: load(u, q, 0))
            ticks(sp, NG, LAGS, tick)

        @block.gpsimd
        def _(pool):
            pool.wait_ge(s_part, 1)
            nc.gpsimd.partition_all_reduce(most[:, :], one[:, :], 128, RMAX).then_inc(s_all, 1)

        @block.vector
        def _(dve):
            link = Link(dve, s_link, 1000)
            nc.vector.tensor_reduce(one[:, :], g.top[:, 0:g.tops], AX.X, ALU.max).then_inc(s_part, 1)
            dve.wait_ge(s_all, 1)
            quant_scale(nc, dve, link, None, most[:, 0:1], scale, 1e-8, 127.0)
            i = BIT_AT["txt"]
            link(nc.vector.tensor_tensor(cs[:, :], g.ws[:, i:i + 1], scale[:, 0:1], ALU.mult))
            for a in range(2):
                link(nc.vector.memset(kt[a][:, :, :], 1.0))
            dve.nop().then_inc(s_scale, 1)
            dve.wait_ge(s_w, 16)

            def quantise(u, p):
                after(dve, s_q, u)
                nc.vector.tensor_scalar(qf[:, :], flat(group(g.XT, u)), scale[:, 1:2], MAGIC, ALU.mult, ALU.add).then_inc(s_qf, 1)
                dve.wait_ge(s_qf, u + 1)
                after(dve, s_f, u - 1)
                nc.vector.tensor_scalar(qb[:, p, :], qf[:, :], MAGIC, None, ALU.subtract).then_inc(s_q, 1)

            def text(u, p):
                dve.wait_ge(s_f, u + 1)
                after(dve, s[0]["fused"], u - 1)
                nc.vector.scalar_tensor_tensor(fu[0][:, p, :, :], psF[:, :].rearrange("p (a f) -> p a f", a=GB), cs[:, 0:1],
                                               BT[:, :].unsqueeze(1).broadcast_to([128, GB, F]), ALU.mult, ALU.add).then_inc(s_fu, 1)

            def shift(u, p, a):
                dve.wait_ge(s[a]["scores"], u + 1)
                x = psB[a][:, 0:GB * NK].rearrange("p (a k) -> p a k", a=GB)
                after(dve, s[a]["shifted"], u)
                nc.vector.tensor_reduce(mx[a][:, :], x, AX.X, ALU.max).then_inc(s[a]["max"], 1)
                dve.wait_ge(s[a]["max"], u + 1)
                after(dve, s[a]["probs_turned"], u)
                nc.vector.tensor_tensor(P[a][:, :, :], x, mx[a][:, :].unsqueeze(2).broadcast_to([128, GB, NK]),
                                        ALU.subtract).then_inc(s[a]["shifted"], 1)

            def attend(u, p, a):
                dve.wait_ge(s[a]["outputs"], u + 1)
                x = psB[a][:, 0:GB * (D2 + 1)].rearrange("p (a e) -> p a e", a=GB)
                after(dve, s[a]["normed"], u)
                nc.vector.reciprocal(rec[a][:, :], x[:, :, D2]).then_inc(s[a]["inverse"], 1)
                dve.wait_ge(s[a]["inverse"], u + 1)
                after(dve, s[a]["fused"], u)
                nc.vector.tensor_tensor(o[a][:, :, :], x[:, :, 0:D2], rec[a][:, :].unsqueeze(2).broadcast_to([128, GB, D2]),
                                        ALU.mult).then_inc(s[a]["normed"], 1)
                dve.wait_ge(s[a]["normed"], u + 1)
                if a == 0:
                    after(dve, s[1]["fused"], u - 1)
                else:
                    after(dve, s_end, u - 1)
                    after(dve, s_topd, u - 1)
                for k, n in ((0, "fused_lo"), (1, "fused")):
                    nc.vector.scalar_tensor_tensor(fu[a + 1][:, p, :, k * D2:(k + 1) * D2], o[a][:, :, :], 0.1,
                                                   fu[a][:, p, :, k * D2:(k + 1) * D2], ALU.mult, ALU.add).then_inc(s[a][n], 1)

            def largest(u, p):
                dve.wait_ge(s[1]["fused"], u + 1)
                dve.wait_ge(s[1]["fused_lo"], u + 1)
                top = g.top[:, u:u + 1] if isinstance(u, int) else g.top[:, bass.ds(u, 1)]
                nc.vector.tensor_reduce(top, flat(fu[2][:, p, :, :]), AX.X, ALU.max, apply_absolute_value=True).then_inc(s_topd, 1)

            def tick(t, p):
                stage(t, p, 0, NG, quantise)
                stage(t, p, 0, NG, text)
                for a in (1, 0):
                    stage(t, p, a + 1, NG, lambda u, q: shift(u, q, a))
                stage(t, p, 3, NG, largest)
                for a in (1, 0):
                    stage(t, p, a + 1, NG, lambda u, q: attend(u, q, a))
            ticks(dve, NG, LAGS, tick)

        @block.tensor
        def _(pe):
            pe.wait_ge(s_scale, 1)

            def text(u, p):
                pe.wait_ge(s_q, u + 1)
                after(pe, s_fu, u)
                a, z = BIT_COLS["txt"]
                for k in range(GB):
                    i = nc.tensor.matmul(psF[:, k * F:(k + 1) * F], qb[:, p, k * T:(k + 1) * T], g.qw[:, a:z], start=True, stop=True)
                i.then_inc(s_f, 1)

            def turn(u, p, a):
                if a == 0:
                    pe.wait_ge(s_fu, u + 1)
                else:
                    pe.wait_ge(s[0]["fused"], u + 1)
                    pe.wait_ge(s[0]["fused_lo"], u + 1)
                after(pe, s[a]["probs_copied"], u)
                for k in range(GB):
                    i = nc.tensor.transpose(psA[a][:, k * T:(k + 1) * T], fu[a][:, p, k, :], g.ident[:, :])
                i.then_inc(s[a]["turned"], 1)

            def turn_keys(u, p, a):
                apart(pe, g,
                      (s_kd[a][p], (u - p) * 8 + 16),
                      (s[a]["keys_copied"], u))
                for k in range(GB):
                    i = nc.tensor.transpose(psK[a][0:NK, k * D2:(k + 1) * D2], kd[a][0:D2, p, k, :], g.ident[0:D2, 0:D2])
                i.then_inc(s[a]["keys_turned"], 1)

            def scores(u, p, a):
                pe.wait_ge(s[a]["copied"], u + 1)
                after(pe, s[a]["normed"], u)
                for k in range(GB):
                    i = nc.tensor.matmul(psB[a][:, k * NK:(k + 1) * NK], fT[a][:, k, :], kd[a][:, p, k, :], start=True, stop=True)
                i.then_inc(s[a]["scores"], 1)

            def turn_probs(u, p, a):
                pe.wait_ge(s[a]["exp"], u + 1)
                for k in range(GB):
                    i = nc.tensor.transpose(psA[a][0:NK, k * T:(k + 1) * T], P[a][:, k, :], g.ident[:, :])
                i.then_inc(s[a]["probs_turned"], 1)

            def outputs(u, p, a):
                pe.wait_ge(s[a]["probs_copied"], u + 1)
                pe.wait_ge(s[a]["keys_copied"], u + 1)
                for k in range(GB):
                    i = nc.tensor.matmul(psB[a][:, k * (D2 + 1):(k + 1) * (D2 + 1)], PT[a][:, k, :], kt[a][:, k, :], start=True, stop=True)
                i.then_inc(s[a]["outputs"], 1)

            def end(u, p):
                pe.wait_ge(s[1]["fused"], u + 1)
                pe.wait_ge(s[1]["fused_lo"], u + 1)
                after(pe, s_endc, u)
                for k in range(GB):
                    i = nc.tensor.transpose(psE[:, k * T:(k + 1) * T], fu[2][:, p, k, :], g.ident[:, :])
                i.then_inc(s_end, 1)

            def tick(t, p):
                for a in (1, 0):
                    stage(t, p, a + 1, NG, lambda u, q: turn(u, q, a))
                for a in (1, 0):
                    stage(t, p, a + 1, NG, lambda u, q: turn_keys(u, q, a))
                stage(t, p, 0, NG, text)
                for a in (1, 0):
                    stage(t, p, a + 1, NG, lambda u, q: scores(u, q, a))
                stage(t, p, 3, NG, end)
                for a in (1, 0):
                    stage(t, p, a + 1, NG, lambda u, q: turn_probs(u, q, a))
                for a in (1, 0):
                    stage(t, p, a + 1, NG, lambda u, q: outputs(u, q, a))
            ticks(pe, NG, LAGS, tick)

        @block.scalar
        def _(act):
            act.wait_ge(s_scale, 1)

            def copy(u, p, a):
                act.wait_ge(s[a]["turned"], u + 1)
                after(act, s[a]["scores"], u)
                nc.scalar.copy(flat(fT[a][:, :, :]), psA[a][:, :]).then_inc(s[a]["copied"], 1)

            def copy_keys(u, p, a):
                act.wait_ge(s[a]["keys_turned"], u + 1)
                after(act, s[a]["outputs"], u)
                nc.scalar.copy(kt[a][:, :, 0:D2], psK[a][0:NK, 0:GB * D2].rearrange("p (a e) -> p a e", a=GB)).then_inc(s[a]["keys_copied"], 1)

            def exp(u, p, a):
                act.wait_ge(s[a]["shifted"], u + 1)
                nc.scalar.activation(P[a][:, :, :], P[a][:, :, :], ACT.Exp, scale=float(F) ** -0.5).then_inc(s[a]["exp"], 1)

            def copy_probs(u, p, a):
                act.wait_ge(s[a]["probs_turned"], u + 1)
                after(act, s[a]["outputs"], u)
                nc.scalar.copy(flat(PT[a][:, :, :]), psA[a][0:NK, :]).then_inc(s[a]["probs_copied"], 1)

            def end(u, p):
                act.wait_ge(s_end, u + 1)
                nc.scalar.copy(group(g.XT, u), psE[:, :].rearrange("p (a t) -> p a t", a=GB)).then_inc(s_endc, 1)

            def tick(t, p):
                for a in (1, 0):
                    stage(t, p, a + 1, NG, lambda u, q: copy(u, q, a))
                for a in (1, 0):
                    stage(t, p, a + 1, NG, lambda u, q: copy_keys(u, q, a))
                for a in (1, 0):
                    stage(t, p, a + 1, NG, lambda u, q: exp(u, q, a))
                stage(t, p, 3, NG, end)
                for a in (1, 0):
                    stage(t, p, a + 1, NG, lambda u, q: copy_probs(u, q, a))
            ticks(act, NG, LAGS, tick)


def layer_bit_ffn(nc, g, d):
    M = 4
    with ExitStack() as ctx:
        L = Layer(nc, ctx, "bf")
        s_w, s_part, s_all, s_link = L.sem("weights"), L.sem("part"), L.sem("largest"), L.sem("link")
        s_setup, s_ready = L.sem("inputs_ready"), L.sem("hidden_scale_ready")
        s_qf, s_q = L.sem("shifted"), L.sem("quantised")
        s_h1, s_m = L.sem("hidden_first"), L.sem("max")
        s_h2, s_relu, s_hq, s_y, s_o, s_x = (L.sem(n) for n in ("hidden", "relu", "hidden_quantised", "out", "out_scaled", "x_done"))
        B1, B2 = L.sb("b1", [128, M]), L.sb("b2", [128, F])
        one, most, scale, cs = L.sb("one", [128, 2]), L.sb("most", [128, 1]), L.sb("scale", [128, 2]), L.sb("product_scale", [128, 1])
        scale2, cs2, hc, hb = L.sb("scale2", [128, 2]), L.sb("product_scale2", [128, 1]), L.sb("hidden_scale", [128, 1]), L.sb("hidden_bias", [128, M])
        qa = L.sb("mean_shifted", [128, NB])
        qab = L.sb("mean_quantised", [128, NB], BF16)
        qf = L.sb("shifted", [F, GB * T])
        qb = L.sb("quantised", [F, NB, T], BF16)
        mx = L.sb("maxima", [128, NG, M])
        hs = L.sb("relu", [128, M, GB * T])
        hq = L.sb("hidden", [128, 2, M, GB * T], BF16)
        ys = L.sb("out", [T, 2, GB * F])
        psH = L.psum("H", [128, M, 512])
        psY, psN = L.psum("Y", [128, 2, 512]), L.psum("N", [128, 512])
        N = Norm(L, g, GB, s_x, psN)
        a1 = BIT_COLS["f1"][0]
        a2 = BIT_COLS["f2"][0]
        LAGS = 4
        block = ctx.enter_context(nc.Block())

        def mean_cols(u):
            m = qab[:, u * GB:(u + 1) * GB] if isinstance(u, int) else qab[:, bass.ds(u * GB, GB)]
            return m.unsqueeze(2).broadcast_to([128, GB, T])

        @block.sync
        def _(sp):
            sp.dma_start(B1[:, :], d["b_f1_b"]).then_inc(s_w, 16)
            sp.dma_start(B2[:, :], d["b_f2_b"].partition_broadcast(128)).then_inc(s_w, 16)

        @block.tensor
        def _(pe):
            pe.wait_ge(s_setup, 1)

            def hidden(u, m):
                nc.tensor.matmul(psH[:, m, :], g.qw[:, a1 + m * 128:a1 + (m + 1) * 128], flat(group(qb, u)), start=True, stop=False)
                return nc.tensor.matmul(psH[:, m, :], g.qw[:, a1 + 512 + m * 128:a1 + 512 + (m + 1) * 128], mean_cols(u),
                                        start=False, stop=True)

            def first(u, p):
                pe.wait_ge(s_q, u + 1)
                for m in range(M):
                    after(pe, s_m, u * M + m - M + 1)
                    hidden(u, m).then_inc(s_h1, 1)
            ticks(pe, NG, 2, lambda t, p: stage(t, p, 0, NG, first))
            pe.wait_ge(s_m, NG * M)

            def second(u, p):
                for m in range(M):
                    after(pe, s_relu, u * M + m - M + 1)
                    hidden(u, m).then_inc(s_h2, 1)

            def out(u, p):
                pe.wait_ge(s_hq, (u + 1) * M)
                after(pe, s_o, u - 1)
                for k in range(GB):
                    for m in range(M):
                        i = nc.tensor.matmul(psY[:, p, k * F:(k + 1) * F], hq[:, p, m, k * T:(k + 1) * T],
                                             g.qw[:, a2 + m * F:a2 + (m + 1) * F], start=(m == 0), stop=(m == M - 1))
                i.then_inc(s_y, 1)

            def tick(t, p):
                stage(t, p, 0, NG, second)
                stage(t, p, 1, NG, out)
                stage(t, p, 3, NG, lambda u, q: N.pe_turn(pe, u, q))
            ticks(pe, NG, LAGS, tick)

        @block.scalar
        def _(act):
            act.wait_ge(s_ready, 1)

            def relu(u, p):
                for m in range(M):
                    act.wait_ge(s_h2, u * M + m + 1)
                    after(act, s_hq, u * M + m - M + 1)
                    nc.scalar.activation(hs[:, m, :], psH[:, m, :], ACT.Relu, bias=hb[:, m:m + 1], scale=hc[:, 0:1]).then_inc(s_relu, 1)

            def tick(t, p):
                stage(t, p, 0, NG, relu)
                stage(t, p, 3, NG, lambda u, q: N.act_store(act, u, q))
            ticks(act, NG, LAGS, tick)

        @block.gpsimd
        def _(pool):
            for r in range(2):
                pool.wait_ge(s_part, r + 1)
                nc.gpsimd.partition_all_reduce(most[:, :], one[:, r:r + 1], 128, RMAX).then_inc(s_all, 1)

            def update(u, p):
                apart(pool, g, (s_o, u + 1))
                x = flat(group(g.X, u))
                nc.gpsimd.tensor_tensor(x, x, ys[:, p, :], ALU.add).then_inc(s_x, 1)

            def tick(t, p):
                stage(t, p, 2, NG, lambda u, q: N.pool_rstd(pool, u, q))
                stage(t, p, 1, NG, update)
            ticks(pool, NG, LAGS, tick)

        @block.vector
        def _(dve):
            link = Link(dve, s_link, 1000)
            dve.wait_ge(s_w, 32)
            link(nc.vector.tensor_reduce(one[:, 0:1], g.top[:, 0:g.tops], AX.X, ALU.max))
            link(nc.vector.tensor_reduce(one[:, 1:2], g.avg[:, :], AX.X, ALU.max, apply_absolute_value=True))
            nc.vector.tensor_tensor(one[:, 0:1], one[:, 0:1], one[:, 1:2], ALU.max).then_inc(s_part, 1)
            dve.wait_ge(s_all, 1)
            quant_scale(nc, dve, link, None, most[:, 0:1], scale, 1e-8, 127.0)
            i = BIT_AT["f1"]
            link(nc.vector.tensor_tensor(cs[:, :], g.ws[:, i:i + 1], scale[:, 0:1], ALU.mult))
            link(nc.vector.tensor_scalar(qa[:, :], g.avg[:, :], scale[:, 1:2], MAGIC, ALU.mult, ALU.add))
            nc.vector.tensor_scalar(qab[:, :], qa[:, :], MAGIC, None, ALU.subtract).then_inc(s_setup, 1)

            def quantise(u, p):
                after(dve, s_q, u)
                nc.vector.tensor_scalar(qf[:, :], flat(group(g.XT, u)), scale[:, 1:2], MAGIC, ALU.mult, ALU.add).then_inc(s_qf, 1)
                dve.wait_ge(s_qf, u + 1)
                nc.vector.tensor_scalar(flat(group(qb, u)), qf[:, :], MAGIC, None, ALU.subtract).then_inc(s_q, 1)

            def largest(u, p):
                for m in range(M):
                    dve.wait_ge(s_h1, u * M + m + 1)
                    top = mx[:, u, m:m + 1] if isinstance(u, int) else mx[:, bass.ds(u, 1), m]
                    nc.vector.tensor_reduce(top, psH[:, m, :], AX.X, ALU.max).then_inc(s_m, 1)

            def tick1(t, p):
                stage(t, p, 0, NG, quantise)
                stage(t, p, 1, NG, largest)
            ticks(dve, NG, 2, tick1)
            dve.wait_ge(s_m, NG * M)
            link(nc.vector.tensor_reduce(hb[:, :], mx[:, :, :].rearrange("p u m -> p m u"), AX.X, ALU.max))
            link(nc.vector.scalar_tensor_tensor(hb[:, :], hb[:, :], cs[:, 0:1], B1[:, :], ALU.mult, ALU.add))
            nc.vector.tensor_reduce(one[:, 1:2], hb[:, :], AX.X, ALU.max).then_inc(s_part, 1)
            dve.wait_ge(s_all, 2)
            link(nc.vector.tensor_scalar(most[:, :], most[:, :], 0.0, None, ALU.max))
            quant_scale(nc, dve, link, None, most[:, 0:1], scale2, 1e-8, 127.0)
            i = BIT_AT["f2"]
            link(nc.vector.tensor_tensor(cs2[:, :], g.ws[:, i:i + 1], scale2[:, 0:1], ALU.mult))
            link(nc.vector.tensor_tensor(hc[:, :], cs[:, :], scale2[:, 1:2], ALU.mult))
            link(nc.vector.tensor_scalar(hb[:, :], B1[:, :], scale2[:, 1:2], None, ALU.mult))
            dve.nop().then_inc(s_ready, 1)

            def quantise2(u, p):
                for m in range(M):
                    dve.wait_ge(s_relu, u * M + m + 1)
                    after(dve, s_y, u - 1)
                    nc.vector.tensor_scalar(hq[:, p, m, :], hs[:, m, :], MAGIC, MAGIC, ALU.add, ALU.subtract).then_inc(s_hq, 1)

            def outputs(u, p):
                dve.wait_ge(s_y, u + 1)
                after(dve, s_x, u - 1)
                nc.vector.scalar_tensor_tensor(ys[:, p, :].rearrange("p (a f) -> p a f", a=GB), psY[:, p, :].rearrange("p (a f) -> p a f", a=GB),
                                               cs2[:, 0:1], B2[:, :].unsqueeze(1).broadcast_to([128, GB, F]), ALU.mult, ALU.add).then_inc(s_o, 1)

            def tick(t, p):
                stage(t, p, 1, NG, outputs)
                stage(t, p, 2, NG, lambda u, q: N.dve_mean(dve, u, q))
                stage(t, p, 0, NG, quantise2)
                stage(t, p, 2, NG, lambda u, q: N.dve_xn(dve, u, q))
            ticks(dve, NG, LAGS, tick)



def layer_gated_experts(nc, g, d):
    E, M = 8, 4
    with ExitStack() as ctx:
        L = Layer(nc, ctx, "ge")
        s_w, s_gs, s_gt, s_gc = L.sem("weights"), L.sem("gates"), L.sem("gates_turned"), L.sem("gates_copied")
        s_h, s_act, s_g, s_mul, s_y, s_x = (L.sem(n) for n in ("hidden", "gelu", "spread", "gated", "out", "x_done"))
        Wf, Wp, sel = L.sb("fc", [F, M * 128]), L.sb("proj", [128, M, F]), L.sb("spread", [E, M, 128])
        gs, gT = L.sb("gates", [T, GB, E]), L.sb("gatesT", [E, GB * T])
        hs = L.sb("hidden", [128, 2, M, GB * T])
        psH, psG = L.psum("H", [128, 2, 512]), L.psum("G", [128, 2, 512])
        psT, psY, psN = L.psum("T", [128, 512]), L.psum("Y", [128, 512]), L.psum("N", [128, 512])
        N = Norm(L, g, GB, s_x, psN)
        LAGS = 4
        block = ctx.enter_context(nc.Block())

        @block.sync
        def _(sp):
            for t, k in ((Wf, "m2_fc"), (Wp, "m2_proj"), (sel, "c_spread")):
                sp.dma_start(t[:], d[k]).then_inc(s_w, 16)

        @block.tensor
        def _(pe):
            pe.wait_ge(s_w, 48)

            def turn_gates(u, p):
                pe.wait_ge(s_gs, u + 1)
                after(pe, s_gc, u)
                for k in range(GB):
                    i = nc.tensor.transpose(psT[0:E, k * T:(k + 1) * T], gs[:, k, :], g.ident[:, :])
                i.then_inc(s_gt, 1)

            def hidden(u, p):
                for m in range(M):
                    after(pe, s_act, u * M + m - 1)
                    nc.tensor.matmul(psH[:, m % 2, :], Wf[:, m * 128:(m + 1) * 128], flat(group(g.XT, u)),
                                     start=True, stop=True).then_inc(s_h, 1)
                pe.wait_ge(s_gc, u + 1)
                for m in range(M):
                    after(pe, s_mul, u * M + m - 1)
                    nc.tensor.matmul(psG[:, m % 2, :], sel[:, m, :], gT[:, :], start=True, stop=True).then_inc(s_g, 1)

            def out(u, p):
                pe.wait_ge(s_mul, (u + 1) * M)
                after(pe, s_x, u)
                for k in range(GB):
                    for m in range(M):
                        i = nc.tensor.matmul(psY[:, k * F:(k + 1) * F], hs[:, p, m, k * T:(k + 1) * T], Wp[:, m, :],
                                             start=(m == 0), stop=(m == M - 1))
                i.then_inc(s_y, 1)

            def tick(t, p):
                stage(t, p, 0, NG, turn_gates)
                stage(t, p, 0, NG, hidden)
                stage(t, p, 1, NG, out)
                stage(t, p, 3, NG, lambda u, q: N.pe_turn(pe, u, q))
            ticks(pe, NG, LAGS, tick)

        @block.scalar
        def _(act):
            def gates(u, p):
                act.wait_ge(s_gt, u + 1)
                after(act, s_g, u * M)
                nc.scalar.copy(gT[:, :], psT[0:E, :]).then_inc(s_gc, 1)

            def gelu(u, p):
                after(act, s_y, u - 1)
                for m in range(M):
                    act.wait_ge(s_h, u * M + m + 1)
                    nc.scalar.activation(hs[:, p, m, :], psH[:, m % 2, :], ACT.Gelu).then_inc(s_act, 1)

            def tick(t, p):
                stage(t, p, 0, NG, gates)
                stage(t, p, 0, NG, gelu)
                stage(t, p, 3, NG, lambda u, q: N.act_store(act, u, q))
            ticks(act, NG, LAGS, tick)

        @block.gpsimd
        def _(pool):
            def gates(u, p):
                after(pool, s_gt, u)
                nc.gpsimd.tensor_copy(gs[:, :, :], group(g.gate, u)).then_inc(s_gs, 1)

            def tick(t, p):
                stage(t, p, 0, NG, gates)
                stage(t, p, 2, NG, lambda u, q: N.pool_rstd(pool, u, q))
            ticks(pool, NG, LAGS, tick)

        @block.vector
        def _(dve):
            def gate(u, p):
                for m in range(M):
                    dve.wait_ge(s_act, u * M + m + 1)
                    dve.wait_ge(s_g, u * M + m + 1)
                    nc.vector.tensor_tensor(hs[:, p, m, :], psG[:, m % 2, :], hs[:, p, m, :], ALU.mult).then_inc(s_mul, 1)

            def update(u, p):
                dve.wait_ge(s_y, u + 1)
                x = flat(group(g.X, u))
                nc.vector.tensor_tensor(x, psY[:, :], x, ALU.add).then_inc(s_x, 1)

            def tick(t, p):
                stage(t, p, 0, NG, gate)
                stage(t, p, 1, NG, update)
                stage(t, p, 2, NG, lambda u, q: N.dve_mean(dve, u, q))
                stage(t, p, 3, NG, lambda u, q: N.dve_xn(dve, u, q))
            ticks(dve, NG, LAGS, tick)


def layer_gated_mlp(nc, g, d):
    M = 3
    BL = 32
    Q = 32767.0
    with ExitStack() as ctx:
        L = Layer(nc, ctx, "gm")
        names = """weights link part largest w_rounded w_turned w_ready x_shifted x_rounded first first_max scales
            second up_shifted gate_shifted up_rounded gate_rounded tanh sig_shifted sig_rounded product product_max
            tanh3 sig_shifted3 sig_rounded3 product3 p_shifted p_rounded o o_max o4 o_shifted o_rounded out x_done""".split()
        s = {n: L.sem(n) for n in names}
        s_out = [L.sem("out_even"), L.sem("out_odd")]
        HT = M * GB * T
        buf = L.sb("buf", [128, 5, HT])
        raw, wq = buf[:, 0, 0:9 * 128], buf[:, 1, 0:9 * 128]
        bs, bi = L.sb("block_scales", [128, 36]), L.sb("block_inverses", [128, 36])
        W = L.sb("weightsT", [128, 9, 128])
        tops = L.sb("tops", [128, 4, NG])
        one, most = L.sb("one", [128, 2]), L.sb("most", [128, 2])
        sx, su, sg, sp3, so, c = (L.sb(n, [128, 2]) for n in ("scale_x", "scale_up", "scale_gate", "scale_p", "scale_o", "factors"))
        U, G = L.sb("up", [128, M, NB * T], I16), L.sb("gate_then_p", [128, M, NB * T], I16)
        ps = L.psum("ps", [128, 6, 512])
        psY = L.psum("Y", [128, 2, 512])
        up, gate = ps[:, 0:3, :], ps[:, 3:6, :]
        old = flat(g.XT[:, :, :])
        spare = [old[:, i * HT:(i + 1) * HT].rearrange("p (m t) -> p m t", m=M) for i in range(5)]
        mem = [buf[:, i, :].rearrange("p (m t) -> p m t", m=M) for i in range(5)]
        magic = L.sb("magic", [128, 2])
        block = ctx.enter_context(nc.Block())

        def cols(t, u):
            return t[:, :, u * GB * T:(u + 1) * GB * T] if isinstance(u, int) else t[:, :, bass.ds(u * GB * T, GB * T)]

        @block.sync
        def _(sp):
            sp.dma_start(raw, d["m3_w"]).then_inc(s["weights"], 16)

            def out(u, p):
                sp.wait_ge(s["x_done"], u + 1)
                o = d["out"]
                dst = o[u * GB:(u + 1) * GB] if isinstance(u, int) else o[bass.ds(u * GB, GB)]
                sp.dma_start(dst.rearrange("b t f -> t b f"), group(g.X, u)).then_inc(s_out[p], 16)
            ticks(sp, NG, 2, lambda t, p: stage(t, p, 0, NG, out))
            for x in s_out:
                sp.wait_ge(x, 8 * NG)

        @block.gpsimd
        def _(pool):
            for r, w in enumerate((1, 2, 1, 1)):
                pool.wait_ge(s["part"], r + 1)
                nc.gpsimd.partition_all_reduce(most[:, 0:w], one[:, 0:w], 128, RMAX).then_inc(s["largest"], 1)

        @block.tensor
        def _(pe):
            pe.wait_ge(s["w_rounded"], 1)
            for i in range(9):
                k = nc.tensor.transpose(ps[:, i // 4, (i % 4) * 128:(i % 4 + 1) * 128], wq[:, i * 128:(i + 1) * 128], g.ident[:, :])
            k.then_inc(s["w_turned"], 1)
            pe.wait_ge(s["w_ready"], 1)

            def products(u, done, read):
                for j in range(2):
                    after(pe, s[read], 2 * u + j - 1)
                    for m in range(M):
                        i = nc.tensor.matmul(ps[:, j * M + m, :], W[:, j * M + m, :], flat(group(g.XT, u)), start=True, stop=True)
                    i.then_inc(s[done], 1)

            def first(u, p):
                pe.wait_ge(s["x_rounded"], u + 1)
                products(u, "first", "first_max")
            ticks(pe, NG, 1, lambda t, p: stage(t, p, 0, NG, first))
            pe.wait_ge(s["first_max"], 2 * NG)

            def second(u, p):
                for j, read in enumerate(("up_shifted", "gate_shifted")):
                    after(pe, s[read], u)
                    for m in range(M):
                        i = nc.tensor.matmul(ps[:, j * M + m, :], W[:, j * M + m, :], flat(group(g.XT, u)), start=True, stop=True)
                    i.then_inc(s["second"], 1)
            ticks(pe, NG, 1, lambda t, p: stage(t, p, 0, NG, second))

            def out(u, p):
                pe.wait_ge(s["o_rounded"], u + 1)
                after(pe, s["x_done"], u - 1)
                for k in range(GB):
                    for m in range(M):
                        i = nc.tensor.matmul(psY[:, p, k * F:(k + 1) * F], mem[2 + p][:, m, k * T:(k + 1) * T], W[:, 6 + m, :],
                                             start=(m == 0), stop=(m == M - 1))
                i.then_inc(s["out"], 1)
            ticks(pe, NG, 2, lambda t, p: stage(t, p, 1, NG, out))

        @block.scalar
        def _(act):
            act.wait_ge(s["w_turned"], 1)
            for b in range(3):
                n = min(4, 9 - 4 * b)
                i = nc.scalar.copy(flat(W[:, 4 * b:4 * b + n, :]), ps[:, b, 0:n * 128])
            i.then_inc(s["w_ready"], 1)
            act.wait_ge(s["scales"], 2)

            def shift(u, p):
                act.wait_ge(s["second"], 2 * u + 1)
                after(act, s["up_rounded"], u)
                nc.scalar.activation(mem[0], up, ACT.Identity, bias=magic[:, 0:1], scale=su[:, 1:2]).then_inc(s["up_shifted"], 1)
                act.wait_ge(s["second"], 2 * u + 2)
                after(act, s["gate_rounded"], u)
                nc.scalar.activation(mem[1], gate, ACT.Identity, bias=magic[:, 0:1], scale=sg[:, 1:2]).then_inc(s["gate_shifted"], 1)

            def sigmoid(u, buffer, rounded, freed, tanh, shifted):
                if rounded is not None:
                    act.wait_ge(s[rounded], u + 1)
                after(act, s[freed], u - 1)
                nc.scalar.activation(buffer, cols(G, u), ACT.Tanh, scale=c[:, 0:1]).then_inc(s[tanh], 1)
                act.wait_ge(s[tanh], u + 1)
                nc.scalar.activation(buffer, buffer, ACT.Identity, bias=magic[:, 1:2], scale=32768.0).then_inc(s[shifted], 1)

            def tick(t, p):
                stage(t, p, 0, NG, shift)
                stage(t, p, 1, NG, lambda u, q: sigmoid(u, mem[2 + q], "gate_rounded", "product_max", "tanh", "sig_shifted"))
            ticks(act, NG, 2, tick)
            act.wait_ge(s["scales"], 3)

            def shift_p(u, p):
                act.wait_ge(s["product3"], u + 1)
                nc.scalar.activation(spare[2 + p], spare[2 + p], ACT.Identity, bias=magic[:, 0:1], scale=c[:, 1:2]).then_inc(s["p_shifted"], 1)

            def tick3(t, p):
                stage(t, p, 0, NG, lambda u, q: sigmoid(u, spare[q], None, "product3", "tanh3", "sig_shifted3"))
                stage(t, p, 1, NG, shift_p)
            ticks(act, NG, 2, tick3)
            act.wait_ge(s["scales"], 4)

            def shift_o(u, p):
                act.wait_ge(s["o4"], u + 1)
                nc.scalar.activation(mem[p], mem[p], ACT.Identity, bias=magic[:, 0:1], scale=so[:, 1:2]).then_inc(s["o_shifted"], 1)
            ticks(act, NG, 2, lambda t, p: stage(t, p, 0, NG, shift_o))

        @block.vector
        def _(dve):
            link = Link(dve, s["link"], 1000)
            link(nc.vector.memset(magic[:, 0:1], MAGIC))
            link(nc.vector.memset(magic[:, 1:2], MAGIC + 32768.0))
            dve.wait_ge(s["weights"], 16)
            blocks = raw.rearrange("p (b i) -> p b i", i=BL)
            rounded = wq.rearrange("p (b i) -> p b i", i=BL)
            spread = lambda t: t[:, :].unsqueeze(2).broadcast_to([128, 36, BL])
            link(nc.vector.tensor_reduce(bs[:, :], blocks, AX.X, ALU.max, apply_absolute_value=True))
            link(nc.vector.tensor_scalar(bs[:, :], bs[:, :], 1.0 / 7.0, 1e-12, ALU.mult, ALU.max))
            link(nc.vector.reciprocal(bi[:, :], bs[:, :]))
            link(nc.vector.tensor_tensor(rounded, blocks, spread(bi), ALU.mult))
            link(nc.vector.tensor_scalar(raw, wq, MAGIC, MAGIC, ALU.add, ALU.subtract))
            nc.vector.tensor_tensor(rounded, blocks, spread(bs), ALU.mult).then_inc(s["w_rounded"], 1)

            def scale_of(out, n, r):
                link(nc.vector.tensor_scalar(out[:, 0:1], most[:, n:n + 1], 1.0 / Q, 1e-12, ALU.mult, ALU.max))
                link(nc.vector.reciprocal(out[:, 1:2], out[:, 0:1]))

            nc.vector.tensor_reduce(one[:, 0:1], g.top[:, 0:g.tops], AX.X, ALU.max).then_inc(s["part"], 1)
            dve.wait_ge(s["largest"], 1)
            scale_of(sx, 0, 1)
            dve.nop().then_inc(s["scales"], 1)
            dve.wait_ge(s["w_turned"], 1)

            def round_x(u, p):
                x = group(g.XT, u)
                t = buf[:, p, 0:GB * T].rearrange("p (a t) -> p a t", a=GB)
                nc.vector.tensor_scalar(t, x, sx[:, 1:2], MAGIC, ALU.mult, ALU.add).then_inc(s["x_shifted"], 1)
                dve.wait_ge(s["x_shifted"], u + 1)
                nc.vector.tensor_scalar(x, t, MAGIC, sx[:, 0:1], ALU.subtract, ALU.mult).then_inc(s["x_rounded"], 1)

            def at(t, r, u):
                return t[:, r, u:u + 1] if isinstance(u, int) else t[:, r, bass.ds(u, 1)]

            def first_max(u, p):
                for j, x in enumerate((up, gate)):
                    dve.wait_ge(s["first"], 2 * u + j + 1)
                    nc.vector.tensor_reduce(at(tops, j, u), x, AX.XY, ALU.max, apply_absolute_value=True).then_inc(s["first_max"], 1)

            def tick1(t, p):
                stage(t, p, 0, NG, round_x)
                stage(t, p, 1, NG, first_max)
            ticks(dve, NG, 1, tick1)
            dve.wait_ge(s["first_max"], 2 * NG)
            nc.vector.tensor_reduce(one[:, :], tops[:, 0:2, :], AX.X, ALU.max).then_inc(s["part"], 1)
            dve.wait_ge(s["largest"], 2)
            scale_of(su, 0, 2)
            scale_of(sg, 1, 2)
            link(nc.vector.tensor_scalar(c[:, 0:1], sg[:, 0:1], 0.5, None, ALU.mult))
            dve.nop().then_inc(s["scales"], 1)

            def round_both(u, p):
                dve.wait_ge(s["up_shifted"], u + 1)
                nc.vector.tensor_scalar(cols(U, u), mem[0], MAGIC, None, ALU.subtract).then_inc(s["up_rounded"], 1)
                dve.wait_ge(s["gate_shifted"], u + 1)
                nc.vector.tensor_scalar(cols(G, u), mem[1], MAGIC, None, ALU.subtract).then_inc(s["gate_rounded"], 1)

            def gate_sigmoid(u, sig, out, shifted, rounded, product):
                dve.wait_ge(s[shifted], u + 1)
                nc.vector.tensor_scalar(sig, sig, MAGIC, 65535.0, ALU.subtract, ALU.min).then_inc(s[rounded], 1)
                dve.wait_ge(s[rounded], u + 1)
                nc.vector.tensor_tensor(out, cols(G, u), sig, ALU.mult).then_inc(s[product], 1)

            def product(u, p):
                after(dve, s["product_max"], u)
                gate_sigmoid(u, mem[2 + p], mem[4], "sig_shifted", "sig_rounded", "product")
                dve.wait_ge(s["product"], u + 1)
                nc.vector.tensor_reduce(at(tops, 2, u), mem[4], AX.XY, ALU.max, apply_absolute_value=True).then_inc(s["product_max"], 1)

            def tick2(t, p):
                stage(t, p, 0, NG, round_both)
                stage(t, p, 1, NG, product)
            ticks(dve, NG, 2, tick2)
            dve.wait_ge(s["product_max"], NG)
            link(nc.vector.tensor_reduce(one[:, 0:1], tops[:, 2, :], AX.X, ALU.max))
            link(nc.vector.tensor_scalar(sg[:, 0:1], sg[:, 0:1], 2.0 ** -16, None, ALU.mult))
            nc.vector.tensor_scalar(one[:, 0:1], one[:, 0:1], sg[:, 0:1], None, ALU.mult).then_inc(s["part"], 1)
            dve.wait_ge(s["largest"], 3)
            scale_of(sp3, 0, 3)
            link(nc.vector.tensor_tensor(c[:, 1:2], sg[:, 0:1], sp3[:, 1:2], ALU.mult))
            dve.nop().then_inc(s["scales"], 1)

            def product3(u, p):
                after(dve, s["p_rounded"], u - 1)
                gate_sigmoid(u, spare[p], spare[2 + p], "sig_shifted3", "sig_rounded3", "product3")

            def round_p(u, p):
                dve.wait_ge(s["p_shifted"], u + 1)
                nc.vector.tensor_scalar(cols(G, u), spare[2 + p], MAGIC, None, ALU.subtract).then_inc(s["p_rounded"], 1)
                dve.wait_ge(s["p_rounded"], u + 1)
                after(dve, s["o_max"], u)
                nc.vector.tensor_tensor(spare[4], cols(G, u), cols(U, u), ALU.mult).then_inc(s["o"], 1)
                dve.wait_ge(s["o"], u + 1)
                nc.vector.tensor_reduce(at(tops, 3, u), spare[4], AX.XY, ALU.max, apply_absolute_value=True).then_inc(s["o_max"], 1)

            def tick3(t, p):
                stage(t, p, 0, NG, product3)
                stage(t, p, 1, NG, round_p)
            ticks(dve, NG, 2, tick3)
            dve.wait_ge(s["o_max"], NG)
            link(nc.vector.tensor_reduce(one[:, 0:1], tops[:, 3, :], AX.X, ALU.max))
            link(nc.vector.tensor_tensor(sp3[:, 1:2], sp3[:, 0:1], su[:, 0:1], ALU.mult))
            nc.vector.tensor_scalar(one[:, 0:1], one[:, 0:1], sp3[:, 1:2], None, ALU.mult).then_inc(s["part"], 1)
            dve.wait_ge(s["largest"], 4)
            scale_of(so, 0, 4)
            link(nc.vector.tensor_tensor(so[:, 1:2], so[:, 1:2], sp3[:, 1:2], ALU.mult))
            dve.nop().then_inc(s["scales"], 1)

            def o4(u, p):
                after(dve, s["o_rounded"], u - 1)
                nc.vector.tensor_tensor(mem[p], cols(G, u), cols(U, u), ALU.mult).then_inc(s["o4"], 1)

            def round_o(u, p):
                dve.wait_ge(s["o_shifted"], u + 1)
                after(dve, s["out"], u - 1)
                nc.vector.tensor_scalar(mem[2 + p], mem[p], MAGIC, so[:, 0:1], ALU.subtract, ALU.mult).then_inc(s["o_rounded"], 1)

            def update(u, p):
                dve.wait_ge(s["out"], u + 1)
                x = flat(group(g.X, u))
                nc.vector.tensor_tensor(x, psY[:, p, :], x, ALU.add).then_inc(s["x_done"], 1)

            def tick4(t, p):
                stage(t, p, 0, NG, o4)
                stage(t, p, 2, NG, update)
                stage(t, p, 1, NG, round_o)
            ticks(dve, NG, 2, tick4)


def layer_store(nc, g, d):
    with ExitStack() as ctx:
        L = Layer(nc, ctx, "st")
        s_out = L.sem("stored")
        block = ctx.enter_context(nc.Block())

        @block.sync
        def _(sp):
            for i in range(4):
                b = NB // 4 * i
                sp.dma_start(d["out"][b:b + NB // 4].rearrange("b t f -> t b f"), g.X[:, b:b + NB // 4, :]).then_inc(s_out, 16)
            sp.wait_ge(s_out, 64)


def build(nc, d, layers=tuple(range(8))):
    with ExitStack() as ctx:
        g = Resident()
        sb = lambda n, s, t=F32: ctx.enter_context(nc.sbuf_tensor(n, s, t))
        g.X = sb("X", [T, NB, F])
        g.XT = sb("XT", [F, NB, T])
        g.ident = sb("ident", [128, 128])
        g.headmask = sb("headmask", [128, 4])
        g.rank = sb("rank", [128, 8])
        g.keep = sb("keep", [T, NB])
        g.minus_half = sb("minus_half", [T, GB])
        g.s_constants = ctx.enter_context(nc.semaphore("constants"))
        g.gate = sb("gate", [T, NB, 8])
        g.top = sb("top", [128, NB])
        g.tops = NG
        layer_load(nc, g, d, layers[0] == 2, layers[0] in (4, 7))
        if 0 in layers:
            layer_heads(nc, g, d, "a0", 8, True, d["a0_wq"], d["a0_wk"], d["a0_wv"], d["a0_wo"], None, None, None,
                        d["a0_bo"], 64 ** -0.5, False)
        if 1 in layers:
            layer_router(nc, g, d, "r0", d["m0_wg"], d["m0_bg"], True)
            layer_experts(nc, g, d)
        if 2 in layers:
            layer_heads(nc, g, d, "a1", 16, False, d["a1_wq"], d["a1_wk"], d["a1_wv"], None, None, None, None, None,
                        8 ** -0.5, False)
        if 3 in layers:
            layer_channel_mix(nc, g, d)
        if 4 in layers:
            with ExitStack() as own:
                g.qw = own.enter_context(nc.sbuf_tensor("ternary", [128, 2176], BF16))
                g.ws = own.enter_context(nc.sbuf_tensor("ternary_scales", [128, len(BIT_COLS)], F32))
                g.avg = own.enter_context(nc.sbuf_tensor("mean_image", [128, NB], F32))
                layer_bit_weights(nc, g, d)
                layer_image(nc, g, d)
                layer_fused(nc, g, d)
                layer_bit_ffn(nc, g, d)
        if 5 in layers:
            layer_router(nc, g, d, "r2", d["m2_wg"], None, False)
            layer_gated_experts(nc, g, d)
        if 6 in layers:
            layer_heads(nc, g, d, "a3", 16, False, d["a3_wq"], d["a3_wk"], d["a3_wv"], d["a3_wo"], d["a3_bq"], d["a3_bk"], d["a3_bv"],
                        d["a3_bo"], 8 ** -0.5, False, g.top)
            g.tops = NB
        if 7 in layers:
            layer_gated_mlp(nc, g, d)
            return
        layer_store(nc, g, d)


def layouts(i):
    import numpy as np
    a = {k: np.asarray(v) for k, v in i.items()}
    c = np.ascontiguousarray
    p = np.arange(128)
    wkv3 = a["L3_xattn_Wkv"].reshape(16, 2, 8, CK)
    bkv3 = a["L3_xattn_bkv"].reshape(16, 2, 8)
    return {
        "c_ident": np.eye(128, dtype=np.float32),
        "c_headmask": ((p % 32) // 8 == np.arange(4)[:, None]).T.astype(np.float32).copy(),
        "c_rank": np.tile(np.arange(8, 0, -1, dtype=np.float32), (128, 1)),
        "mask_t": c(a["mask_BxS_bk0"].T),
        "x": a["x"],
        "ctx_t": c(a["ctx_768"].transpose(0, 2, 1)),
        "a0_wq": a["L0_xattn_Wq"], "a0_wk": a["L0_xattn_Wk"], "a0_wv": a["L0_xattn_Wv"],
        "a0_wo": c(a["L0_xattn_Wo"].reshape(4, 128, F).transpose(1, 0, 2)), "a0_bo": a["L0_xattn_bo"],
        "a1_wq": c(a["L1_xattn_Wq"].T), "a1_wk": c(a["L1_xattn_Wkv"][:128].T), "a1_wv": c(a["L1_xattn_Wkv"][128:].T),
        "m0_wg": a["L0_ffn_Wg"], "m0_bg": c(a["L0_ffn_bg"][:, None]),
        "m0_w1": c(a["L0_ffn_W1"].transpose(1, 0, 2)), "m0_b1": c(a["L0_ffn_b1"].reshape(8, 4, 128).transpose(2, 0, 1)),
        "m0_w2": c(a["L0_ffn_W2"].reshape(8, 4, 128, F).transpose(2, 0, 1, 3)), "m0_b2": a["L0_ffn_b2"],
        "m1_wr": c(a["L1_ffn_W_r"].T), "m1_wk": c(a["L1_ffn_W_k"].T), "m1_wv": c(a["L1_ffn_W_v"].T),
        "c_bit_inverse_counts": np.tile(np.float32(1) / np.float32([96 * 128, 128 * 128, 128 * 128, 128 * 128, 128 * 128, 256 * 512, 512 * 128]), (128, 1)),
        "b_d2v_w": c(a["L2_xattn_W_d2v"].T),
        "b_rest_w": c(np.concatenate([a["L2_xattn_W_img"].T, a["L2_xattn_W_txt"].T] + [a["L2_xattn_W_att0"].T] * 2
                                     + [a["L2_xattn_W_att1"].T] * 2
                                     + [a["L2_xattn_W_f1"].T[:128], a["L2_xattn_W_f1"].T[128:],
                                        a["L2_xattn_W_f2"].T.reshape(4, 128, F).transpose(1, 0, 2).reshape(128, 512)], axis=1)),
        "b_d2v_b": c(a["L2_xattn_b_d2v"][:, None]), "b_img_b": c(a["L2_xattn_b_img"][:, None]),
        "b_att_b": c(np.stack([np.tile(a["L2_xattn_b_att0"], 2), np.tile(a["L2_xattn_b_att1"], 2)], 1)),
        "b_txt_b": a["L2_xattn_b_txt"], "b_f1_b": c(a["L2_xattn_b_f1"].reshape(4, 128).T), "b_f2_b": a["L2_xattn_b_f2"],
        "m2_wg": c(a["L2_ffn_w_gate"].T), "m2_fc": c(a["L2_ffn_w_fc"].reshape(512, F).T),
        "m2_proj": c(a["L2_ffn_w_proj"].transpose(0, 2, 1).reshape(4, 128, F).transpose(1, 0, 2)),
        "c_spread": (np.arange(8)[:, None, None] == 2 * np.arange(4)[None, :, None] + p[None, None, :] // 64).astype(np.float32),
        "a3_wq": c(a["L3_xattn_Wq"].T), "a3_wk": c(wkv3[:, 0].reshape(128, CK).T), "a3_wv": c(wkv3[:, 1].reshape(128, CK).T),
        "a3_wo": c(a["L3_xattn_Wo"].T[:, None, :]), "a3_bq": c(a["L3_xattn_bq"][:, None]), "a3_bk": c(bkv3[:, 0].reshape(128, 1)),
        "a3_bv": c(bkv3[:, 1].reshape(128)), "a3_bo": a["L3_xattn_bo"],
        "m3_w": c(np.concatenate([a["L3_ffn_w_up"].reshape(3, 128, F).transpose(1, 0, 2).reshape(128, 384),
                                  a["L3_ffn_w_gate"].reshape(3, 128, F).transpose(1, 0, 2).reshape(128, 384),
                                  a["L3_ffn_w_down"]], axis=1)),
        "m1_mu": c(np.stack([a["L1_ffn_mu_r"], a["L1_ffn_mu_k"]], 1)),
    }


def program(nc, inputs, layers=tuple(range(8))):
    arrays = {f"in_{k}": v for k, v in layouts(inputs).items()}
    d = {k[3:]: nc.dram_tensor(k, v.shape, mybir.dt.from_np(v.dtype), kind="ExternalInput").ap() for k, v in arrays.items()}
    d["out"] = nc.dram_tensor("out", (NB, T, F), F32, kind="ExternalOutput").ap()
    d["keys"] = nc.dram_tensor("keys", (NB, 2, 128, NK), F32, kind="Internal").ap()
    build(nc, d, layers)
    return arrays


def kernel(**inputs):
    import concourse.bacc as bacc
    from concourse.bass_utils import run_bass_kernel_spmd

    nc = bacc.Bacc("TRN2", target_bir_lowering=False, num_devices=1)
    arrays = program(nc, inputs)
    return run_bass_kernel_spmd(nc, [arrays], core_ids=[0]).results[0]["out"]
```

```python
from contextlib import ExitStack

import concourse.bass as bass
from concourse import mybir

F32 = mybir.dt.float32
F32R = mybir.dt.float32r
BF16 = mybir.dt.bfloat16
I16 = mybir.dt.int16
U8 = mybir.dt.uint8
ALU = mybir.AluOpType
ACT = mybir.ActivationFunctionType
AX = mybir.AxisListType
RMAX = bass.bass_isa.ReduceOp.max
RADD = bass.bass_isa.ReduceOp.add

NB, T, F = 64, 128, 128
NK, CK = 120, 96
LN_EPS = 1e-5
MAGIC = 1.5 * 2.0 ** 23
GB = 4
NG = NB // GB


def after(eng, sem, n):
    if isinstance(n, int) and n <= 0:
        return
    eng.wait_ge(sem, n)


def apart(eng, g, *waits):
    counts = [n if isinstance(n, int) else eng.to_reg(n) for _, n in waits]
    eng.wait_ge(g.s_constants, 1)
    for (sem, _), n in zip(waits, counts):
        after(eng, sem, n)


def ticks(eng, n, lag, tick):
    head = lag + 2 + (lag % 2)
    head = min(head, n)
    for t in range(head):
        tick(t, t % 2)
    if head < n:
        with eng.Fori(head // 2, n // 2) as j:
            tick(j * 2, 0)
            tick(j * 2 + 1, 1)
    for t in range(n, n + lag):
        tick(t, t % 2)


def stage(t, par, lag, n, fn):
    b = t - lag
    if isinstance(b, int) and not 0 <= b < n:
        return
    fn(b, (par - lag) % 2)


class Resident:
    pass


class Link:

    def __init__(self, eng, sem, per, g=None):
        self.eng, self.sem, self.per, self.g, self.k, self.b = eng, sem, per, g, 0, 0

    def unit(self, b):
        assert self.k in (0, self.per), (self.k, self.per)
        self.b, self.k = b, 0

    def __call__(self, ins):
        self.k += 1
        ins.then_inc(self.sem, 1)
        if self.g is None:
            self.eng.wait_ge(self.sem, self.b * self.per + self.k)
        else:
            apart(self.eng, self.g, (self.sem, self.b * self.per + self.k))


class Layer:

    def __init__(self, nc, ctx, name):
        self.nc, self.ctx, self.name, self.sems = nc, ctx, name, []
        ctx.callback(self.release)

    def release(self):
        self.nc.clear_and_free_semaphores(self.sems)
        self.nc.all_engine_barrier()

    def sem(self, name):
        self.sems.append(self.nc.alloc_semaphore(f"{self.name}_{name}"))
        return self.sems[-1]

    def sb(self, name, shape, dt=F32):
        return self.ctx.enter_context(self.nc.sbuf_tensor(f"{self.name}_{name}", shape, dt))

    def psum(self, name, shape, dt=F32):
        return self.ctx.enter_context(self.nc.psum_tensor(f"{self.name}_{name}", shape, dt))


class Norm:

    def __init__(self, L, g, G, x_done, psum, masked=False, top=None):
        self.nc, self.g, self.G, self.x_done, self.psum = L.nc, g, G, x_done, psum
        self.masked, self.top = masked, top
        self.stats = L.sb("stats", [T, 2, G, 6])
        self.mv = L.sb("meanvar", [T, 2, G, 2])
        self.rstd = L.sb("rstd", [T, 2, G])
        self.xn = L.sb("xn", [T, 2, G * F])
        self.s_stats = L.sem("ln_stats")
        self.s_mean = L.sem("ln_mean")
        self.s_var = L.sem("ln_var")
        self.s_pow = L.sem("ln_pow")
        self.s_rstd = L.sem("ln_rstd")
        self.s_xn = L.sem("ln_xn")
        self.s_turned = L.sem("ln_turned")
        self.s_stored = L.sem("ln_stored")

    def batches(self, t, u):
        if self.G == 1:
            return t[:, bass.ds(u, 1), :] if not isinstance(u, int) else t[:, u:u + 1, :]
        if isinstance(u, int):
            return t[:, u * self.G:(u + 1) * self.G, :]
        return t[:, bass.ds(u * self.G, self.G), :]

    def one(self, t, u, k):
        b = u * self.G + k
        return t[:, b, :] if isinstance(b, int) else t[:, bass.ds(b, 1), :].rearrange("p a f -> p (a f)")

    def dve_mean(self, dve, u, p):
        apart(dve, self.g, (self.x_done, u + 1))
        for k in range(self.G):
            i = self.nc.vector.bn_stats(self.stats[:, p, k, :], self.one(self.g.X, u, k))
        i.then_inc(self.s_stats, 1)
        apart(dve, self.g,
              (self.s_rstd, u - 1),
              (self.s_stats, u + 1))
        for k in range(self.G):
            i = self.nc.vector.bn_aggr(self.mv[:, p, k, :], self.stats[:, p, k, :])
        i.then_inc(self.s_mean, 1)

    def pool_rstd(self, pool, u, p):
        apart(pool, self.g,
              (self.s_mean, u + 1),
              (self.s_xn, u - 1))
        self.nc.gpsimd.tensor_scalar(self.rstd[:, p, :], self.mv[:, p, :, 1], LN_EPS, 1.0, ALU.add, ALU.mult).then_inc(self.s_var, 1)
        pool.wait_ge(self.s_var, u + 1)
        i = self.nc.gpsimd.tensor_tensor(self.rstd[:, p, :], self.rstd[:, p, :], self.g.minus_half[:, 0:self.G], ALU.pow)
        if self.masked:
            i.then_inc(self.s_pow, 1)
            apart(pool, self.g, (self.s_pow, u + 1))
            if isinstance(u, int):
                keep = self.g.keep[:, u * self.G:(u + 1) * self.G]
            else:
                keep = self.g.keep[:, bass.ds(u * self.G, self.G)]
            i = self.nc.gpsimd.tensor_tensor(self.rstd[:, p, :], self.rstd[:, p, :], keep, ALU.mult)
        i.then_inc(self.s_rstd, 1)

    def dve_xn(self, dve, u, p):
        dve.wait_ge(self.s_rstd, u + 1)
        after(dve, self.s_turned, u - 1)
        for k in range(self.G):
            i = self.nc.vector.tensor_scalar(self.xn[:, p, k * F:(k + 1) * F], self.one(self.g.X, u, k),
                                             self.mv[:, p, k, 0:1], self.rstd[:, p, k:k + 1], ALU.subtract, ALU.mult)
        i.then_inc(self.s_xn, 1)
        if self.top is not None:
            dve.wait_ge(self.s_xn, u + 1)
            top = self.top[:, u:u + 1] if isinstance(u, int) else self.top[:, bass.ds(u, 1)]
            self.nc.vector.tensor_reduce(top, self.xn[:, p, :], AX.X, ALU.max, apply_absolute_value=True).then_inc(self.s_top, 1)

    def pe_turn(self, pe, u, p):
        pe.wait_ge(self.s_xn, u + 1)
        after(pe, self.s_stored, u)
        for k in range(self.G):
            i = self.nc.tensor.transpose(self.psum[:, k * F:(k + 1) * F], self.xn[:, p, k * F:(k + 1) * F], self.g.ident[:, :])
        i.then_inc(self.s_turned, 1)

    def act_store(self, act, u, p):
        act.wait_ge(self.s_turned, u + 1)
        self.nc.scalar.copy(self.batches(self.g.XT, u),
                            self.psum[:, 0:self.G * F].rearrange("p (a f) -> p a f", a=self.G)).then_inc(self.s_stored, 1)


def layer_load(nc, g, d, masked, top):
    with ExitStack() as ctx:
        L = Layer(nc, ctx, "ld")
        s_const = L.sem("const")
        PARTS = 8
        s_x = [L.sem(f"x{i}") for i in range(PARTS)]
        s_keep = L.sem("keep")
        s_xd, s_kept = L.sem("x_done"), L.sem("mask")
        ps = [L.psum(f"turn{i}", [128, 512]) for i in range(2)]
        mask8 = L.sb("mask8", [T, NB], U8)
        N = Norm(L, g, GB, s_xd, ps[0], masked=masked, top=g.top if top else None)
        N.s_top = L.sem('top')
        block = ctx.enter_context(nc.Block())

        def constants_in(sp):
            sp.dma_start(g.ident[:, :], d["c_ident"]).then_inc(s_const, 16)
            sp.dma_start(g.headmask[:, :], d["c_headmask"]).then_inc(s_const, 16)
            sp.dma_start(mask8[:, :], d["mask_t"]).then_inc(s_const, 16)
            sp.dma_start(g.rank[:, :], d["c_rank"]).then_inc(s_const, 16)
            sp.dma_start(g.pick[:, :], d["c_pick"]).then_inc(s_const, 16)

        @block.sync
        def _(sp):
            for i in range(PARTS):
                b = NB // PARTS * i
                sp.dma_start(g.X[:, b:b + NB // PARTS, :], d["x"][b:b + NB // PARTS].rearrange("b t f -> t b f")).then_inc(s_x[i], 16)
                if i == 0:
                    constants_in(sp)
            for i in range(PARTS):
                sp.wait_ge(s_x[i], 16)
                sp.nop().then_inc(s_xd, NG // PARTS)

        @block.gpsimd
        def _(pool):
            nc.gpsimd.memset(g.minus_half[:, :], -0.5).then_inc(s_keep, 1)
            pool.wait_ge(s_keep, 1)
            pool.wait_ge(s_kept, 1)
            ticks(pool, NG, 2, lambda t, p: stage(t, p, 0, NG, lambda u, q: N.pool_rstd(pool, u, q)))

        @block.vector
        def _(dve):
            dve.wait_ge(s_const, 80)
            dve.nop().then_inc(g.s_constants, 1)
            nc.vector.tensor_copy(g.keep[:, :], mask8[:, :]).then_inc(s_kept, 1)

            def tick(t, p):
                stage(t, p, 0, NG, lambda u, q: N.dve_mean(dve, u, q))
                stage(t, p, 1, NG, lambda u, q: N.dve_xn(dve, u, q))
            ticks(dve, NG, 2, tick)

        @block.tensor
        def _(pe):
            pe.wait_ge(s_const, 80)
            ticks(pe, NG, 2, lambda t, p: stage(t, p, 1, NG, lambda u, q: N.pe_turn(pe, u, q)))

        @block.scalar
        def _(act):
            ticks(act, NG, 2, lambda t, p: stage(t, p, 1, NG, lambda u, q: N.act_store(act, u, q)))


def layer_heads(nc, g, d, name, H, wide, wq, wk, wv, wo, bq, bk, bv, bo, scale, masked_next, top=None):
    D = 64 if wide else 8
    I = H * D
    NT = I // 128
    HB = 4
    SB = H // HB
    DV = D + 1
    O_CUT = 3 if wide else H
    HALVES = H // 8

    def head_at(at):
        return 2 * (at % HB) + at // HB if wide else at

    with ExitStack() as ctx:
        L = Layer(nc, ctx, name)
        s_w = L.sem("weights")
        s_ctx = [L.sem("ctx_in_even"), L.sem("ctx_in_odd")]
        s_setup = L.sem("setup")
        s_q, s_kv = L.sem("q_projected"), L.sem("kv_projected")
        s_qc, s_kc, s_vc = L.sem("q_copied"), L.sem("k_copied"), L.sem("v_copied")
        s_S, s_max, s_sub, s_P = L.sem("scores"), L.sem("max"), L.sem("shifted"), L.sem("probs")
        s_PT, s_PTc, s_O = L.sem("probs_turned"), L.sem("probs_copied"), L.sem("outputs")
        s_Oc, s_tok = L.sem("outputs_copied"), L.sem("token_major")
        s_rec, s_on = L.sem("sum_inverse"), L.sem("normed")
        s_oT, s_oTc, s_wo, s_x = L.sem("out_turned"), L.sem("out_copied"), L.sem("projected"), L.sem("x_done")
        s_woc, s_xb = L.sem("projected_copied"), L.sem("x_part")
        Wq = L.sb("wq", [F, I])
        Wk = L.sb("wk", [CK, I])
        Wv = L.sb("wv", [CK, I])
        s_wn = 3
        if wo is not None:
            Wo = L.sb("wo", [128, NT, F])
            BO = L.sb("bo", [128, F])
            s_wn += 2
        if bq is not None:
            BQ, BK, BV = L.sb("bq", [128, 1]), L.sb("bk", [128, 1]), L.sb("bv", [NK, I])
            s_wn += 3
        cs = L.sb("ctx", [CK, 2, NK])
        qT = L.sb("qT", [128, 2, NT if wide else SB, T])
        kT = L.sb("kT", [128, 2, NT if wide else HB, NK])
        va = L.sb("values", [NK, 2, H, DV if wide else 32])
        Sx = L.sb("probs", [T, 2, H, NK])
        mx = L.sb("max", [T, 8])
        PTs = L.sb("probsT", [NK, H, T])
        rec = L.sb("sum_inv", [T, H])
        if not wide:
            OT = L.sb("outputs", [128, SB, T])
        on = L.sb("out", [T, 2, H, D])
        if wo is not None:
            oTs = L.sb("outT", [128, NT, T])
            ws = L.sb("projected", [T, F])
        if wide:
            psS = L.psum("S", [128, 2, 512])
            psPT = L.psum("PT", [128, 2, 512])
            psQ = L.psum("Q", [128, 512])
            psK = L.psum("K", [128, 512])
            psV = L.psum("V", [128, 512])
            psO = L.psum("O", [128, 512])
            pq, pk, pv = psQ[:, 0:512], psK[:, 0:NT * NK], psV[0:NK, 0:512]
            pO = [psO[:, 0:O_CUT * DV], psV[:, 0:(H - O_CUT) * DV]]
        else:
            psS = L.psum("S", [128, 4, 512])
            psPT = L.psum("PT", [128, 2, 512])
            psQ = L.psum("Q", [128, 512])
            psO = L.psum("KVO", [128, 512])
            pq, pk, pv = psQ[:, 0:128], psO[:, 0:NK], psO[0:NK, 128:256]
            pO = [psO[:, 256:256 + H * DV]]
            pOT = psPT[:, 0, :]
        poT, pWo = psQ[:, 0:NT * T], psQ[:, 0:F]
        N = Norm(L, g, 1, s_x, psQ)
        N.masked, N.top = masked_next, top
        N.s_top = L.sem("top")
        LAG_O = 3 if wide else 4
        LAG_X, LAG_T = 5, 6
        LAGS = LAG_T
        block = ctx.enter_context(nc.Block())

        @block.sync
        def _(sp):
            sp.dma_start(Wq[:, :], wq).then_inc(s_w, 16)
            sp.dma_start(Wk[:, :], wk).then_inc(s_w, 16)
            sp.dma_start(Wv[:, :], wv).then_inc(s_w, 16)
            if wo is not None:
                sp.dma_start(Wo[:, :, :], wo).then_inc(s_w, 16)
                sp.dma_start(BO[:, :], bo.partition_broadcast(128)).then_inc(s_w, 16)
            if bq is not None:
                sp.dma_start(BQ[:, :], bq).then_inc(s_w, 16)
                sp.dma_start(BK[:, :], bk).then_inc(s_w, 16)
                sp.dma_start(BV[:, :], bv.partition_broadcast(NK)).then_inc(s_w, 16)

            def load(b, p):
                after(sp, s_kv, b)
                if isinstance(b, int):
                    src = d["ctx_t"][b]
                else:
                    src = d["ctx_t"][bass.ds(b, 1)].rearrange("a c k -> (a c) k")
                sp.dma_start(cs[:, p, :], src).then_inc(s_ctx[p], 16)
            ticks(sp, NB, LAGS, lambda t, p: stage(t, p, 0, NB, load))

        @block.tensor
        def _(pe):
            pe.wait_ge(s_w, 16 * s_wn)

            def queries(b, p):
                if wo is not None:
                    after(pe, s_woc, b - 3 if wide else b - 4)
                if wide or wo is None:
                    after(pe, N.s_stored, b - LAG_T + 1 if wide else b - LAG_T)
                after(pe, s_qc, b)
                x = g.XT[:, b, :] if isinstance(b, int) else g.XT[:, bass.ds(b, 1), :].rearrange("p a t -> p (a t)")
                for i in range(NT):
                    m = nc.tensor.matmul(pq[:, i * T:(i + 1) * T], Wq[:, i * 128:(i + 1) * 128], x, start=True, stop=True)
                m.then_inc(s_q, 1)

            def keys_values(t, p):
                after(pe, s_kc, t)
                after(pe, s_vc, t - 1)
                after(pe, s_on, t - 2 if wide else t - 3)
                if not isinstance(t, int) or t < NB:
                    pe.wait_ge(s_ctx[p], (t - p) * 8 + 16)
                    for i in range(NT):
                        m = nc.tensor.matmul(pk[:, i * NK:(i + 1) * NK], Wk[:, i * 128:(i + 1) * 128], cs[:, p, :], start=True, stop=True)
                if not isinstance(t, int) or t >= 1:
                    m = nc.tensor.matmul(pv, cs[:, 1 - p, :], Wv[:, :], start=True, stop=True)
                m.then_inc(s_kv, 1)

            def scores(b, p, half):
                if half == 0:
                    pe.wait_ge(s_qc, b + 1)
                    pe.wait_ge(s_kc, b + 1)
                after(pe, s_sub, (b - 1) * HALVES + half + 1)
                if wide:
                    for h in range(H):
                        r = 64 * (h % 2)
                        m = nc.tensor.matmul(psS[:, h % 2, (h // 2) * NK:(h // 2 + 1) * NK], qT[r:r + 64, p, h // 2, :],
                                             kT[r:r + 64, p, h // 2, :], start=True, stop=True)
                else:
                    for i in (2 * half, 2 * half + 1):
                        m = nc.tensor.matmul(psS[:, i, 0:HB * NK], qT[:, p, i, :],
                                             kT[:, p, :, :].rearrange("p h k -> p (h k)"), start=True, stop=True)
                m.then_inc(s_S, 1)

            def turn(b, p, half):
                pe.wait_ge(s_P, b * HALVES + half + 1)
                after(pe, s_PTc, b * HALVES + half)
                if half == 0 and not wide:
                    after(pe, s_Oc, b)
                for h in range(8):
                    m = nc.tensor.transpose(psPT[0:NK, h // 4, (h % 4) * T:(h % 4 + 1) * T], Sx[:, p, 8 * half + h, :], g.ident[:, :])
                m.then_inc(s_PT, 1)

            def values(b, p):
                pe.wait_ge(s_PTc, (b + 1) * HALVES)
                if not wide:
                    for h in range(H):
                        j, c = h % HB, h // HB * T
                        m = nc.tensor.matmul(pOT[32 * j:32 * j + 32, c:c + T], va[:, p, h, :], PTs[:, h, :], start=True, stop=True)
                    m.then_inc(s_O, 1)
                    return
                bank_of_outputs(b)
                for at in range(H):
                    h = head_at(at)
                    k = 0 if h < O_CUT else 1
                    c = (h - k * O_CUT) * DV
                    m = nc.tensor.matmul(pO[k][:, c:c + DV], PTs[:, at, :], va[:, p, h, :], start=True, stop=True)
                m.then_inc(s_O, 1)

            def bank_of_outputs(b):
                after(pe, s_on, b)
                t = b + 2 if wide else b + 3
                if not wide:
                    pe.wait_ge(s_kc, min(t + 1, NB) if isinstance(t, int) else t + 1)
                pe.wait_ge(s_vc, min(t, NB) if isinstance(t, int) else t)

            def token_major(b, p):
                pe.wait_ge(s_Oc, b + 1)
                bank_of_outputs(b)
                for i in range(SB):
                    c = i * HB * DV
                    m = nc.tensor.matmul(pO[0][:, c:c + HB * DV], OT[:, i, :], g.pick[:, :], start=True, stop=True)
                m.then_inc(s_tok, 1)

            def turn_out(b, p):
                pe.wait_ge(s_on, b + 1)
                after(pe, N.s_stored, b + LAG_O - LAG_T + 1)
                pe.wait_ge(s_qc, b + LAG_O + 1 if not isinstance(b, int) else min(b + LAG_O + 1, NB))
                o = on[:, p, :, :].rearrange("p h e -> p (h e)")
                for i in range(NT):
                    m = nc.tensor.transpose(poT[:, i * T:(i + 1) * T], o[:, i * 128:(i + 1) * 128], g.ident[:, :])
                m.then_inc(s_oT, 1)

            def project_out(b, p):
                pe.wait_ge(s_oTc, b + 1)
                for i in range(NT):
                    m = nc.tensor.matmul(pWo, oTs[:, i, :], Wo[:, i, :], start=(i == 0), stop=(i == NT - 1))
                m.then_inc(s_wo, 1)

            def turn_xn(b, p):
                before = LAG_T if wide else LAG_T + 1
                pe.wait_ge(s_qc, b + before if not isinstance(b, int) else min(b + before, NB))
                if wo is not None:
                    before = LAG_T - 3 if wide else LAG_T - 4
                    pe.wait_ge(s_woc, b + before if not isinstance(b, int) else min(b + before, NB))
                N.pe_turn(pe, b, p)

            def wide_tick(t, p):
                stage(t, p, 1, NB, lambda b, q: scores(b, q, 0))
                stage(t, p, 4, NB, project_out)
                stage(t, p, 0, NB + 1, keys_values)
                stage(t, p, LAG_T, NB, turn_xn)
                stage(t, p, 2, NB, lambda b, q: turn(b, q, 0))
                stage(t, p, 0, NB, queries)
                stage(t, p, 2, NB, values)
                stage(t, p, LAG_O, NB, turn_out)

            def narrow_tick(t, p):
                stage(t, p, 1, NB, lambda b, q: scores(b, q, 0))
                stage(t, p, 0, NB + 1, keys_values)
                stage(t, p, 2, NB, lambda b, q: turn(b, q, 0))
                stage(t, p, 0, NB, queries)
                stage(t, p, 1, NB, lambda b, q: scores(b, q, 1))
                stage(t, p, 2, NB, lambda b, q: turn(b, q, 1))
                stage(t, p, LAG_T, NB, turn_xn)
                stage(t, p, 3, NB, token_major)
                if wo is not None:
                    stage(t, p, LAG_O, NB, turn_out)
                stage(t, p, 2, NB, values)
                if wo is not None:
                    stage(t, p, LAG_O, NB, project_out)
            ticks(pe, NB, LAGS, wide_tick if wide else narrow_tick)

        @block.scalar
        def _(act):
            act.wait_ge(s_w, 16 * s_wn)
            act.wait_ge(s_setup, 1 if wide else 3)

            def queries(b, p):
                act.wait_ge(s_q, b + 1)
                after(act, s_S, (b - 1) * HALVES)
                if wide:
                    m = nc.scalar.copy(qT[:, p, :, :], pq.rearrange("p (n t) -> p n t", n=NT))
                else:
                    for i in range(SB):
                        r = slice(32 * i, 32 * i + 32)
                        if bq is None:
                            m = nc.scalar.copy(qT[r, p, i, :], pq[r, :])
                        else:
                            m = nc.scalar.activation(qT[r, p, i, :], pq[r, :], ACT.Identity, bias=BQ[r, 0:1])
                m.then_inc(s_qc, 1)

            def probs(b, p, half):
                act.wait_ge(s_sub, b * HALVES + half + 1)
                x = Sx[:, p, 8 * half:8 * half + 8, :]
                nc.scalar.activation(x, x, ACT.Exp, scale=scale).then_inc(s_P, 1)

            def copy_turned(b, p, half):
                act.wait_ge(s_PT, b * HALVES + half + 1)
                after(act, s_O, b)
                nc.scalar.copy(PTs[:, 8 * half:8 * half + 8, :],
                               psPT[0:NK, :, :].rearrange("p a (h t) -> p (a h) t", h=4)).then_inc(s_PTc, 1)

            def outputs_copy(b, p):
                act.wait_ge(s_O, b + 1)
                after(act, s_tok, b)
                nc.scalar.copy(OT[:, :, :], pOT.rearrange("p (s t) -> p s t", s=SB)).then_inc(s_Oc, 1)

            def out_copy(b, p):
                act.wait_ge(s_oT, b + 1)
                after(act, s_wo, b)
                nc.scalar.copy(oTs[:, :, :], poT.rearrange("p (n t) -> p n t", n=NT)).then_inc(s_oTc, 1)

            def projected_copy(b, p):
                act.wait_ge(s_wo, b + 1)
                after(act, s_xb, b)
                nc.scalar.copy(ws[:, :], pWo).then_inc(s_woc, 1)

            def wide_tick(t, p):
                stage(t, p, 4, NB, projected_copy)
                stage(t, p, LAG_T, NB, lambda b, q: N.act_store(act, b, q))
                stage(t, p, 2, NB, lambda b, q: copy_turned(b, q, 0))
                stage(t, p, 0, NB, queries)
                stage(t, p, 1, NB, lambda b, q: probs(b, q, 0))
                stage(t, p, LAG_O, NB, out_copy)

            def narrow_tick(t, p):
                stage(t, p, 3, NB, outputs_copy)
                stage(t, p, 2, NB, lambda b, q: copy_turned(b, q, 0))
                stage(t, p, 0, NB, queries)
                stage(t, p, 1, NB, lambda b, q: probs(b, q, 0))
                stage(t, p, 2, NB, lambda b, q: copy_turned(b, q, 1))
                stage(t, p, LAG_T, NB, lambda b, q: N.act_store(act, b, q))
                if wo is not None:
                    stage(t, p, LAG_O, NB, out_copy)
                stage(t, p, 1, NB, lambda b, q: probs(b, q, 1))
                if wo is not None:
                    stage(t, p, LAG_O, NB, projected_copy)
            ticks(act, NB, LAGS, wide_tick if wide else narrow_tick)

        @block.gpsimd
        def _(pool):
            def update(b, p):
                x = N.one(g.X, b, 0)
                if wo is None:
                    apart(pool, g, (s_on, b + 1))
                    nc.gpsimd.tensor_tensor(x, x, on[:, p, :, :].rearrange("p h e -> p (h e)"), ALU.add).then_inc(s_x, 1)
                else:
                    apart(pool, g, (s_woc, b + 1))
                    nc.gpsimd.tensor_tensor(x, x, ws[:, :], ALU.add).then_inc(s_xb, 1)
                    apart(pool, g, (s_xb, b + 1))
                    nc.gpsimd.tensor_tensor(x, x, BO[:, :], ALU.add).then_inc(s_x, 1)

            pool.wait_ge(s_w, 16 * s_wn)

            def tick(t, p):
                stage(t, p, LAG_X, NB, lambda b, q: N.pool_rstd(pool, b, q))
                stage(t, p, 4, NB, update)
            ticks(pool, NB, LAGS, tick)

        @block.vector
        def _(dve):
            if wide:
                nc.vector.memset(va[:, :, :, :], 1.0).then_inc(s_setup, 1)
            else:
                nc.vector.memset(va[:, :, :, :], 0.0).then_inc(s_setup, 1)
                dve.wait_ge(s_setup, 1)
                nc.vector.memset(va[:, :, :, D:DV], 1.0).then_inc(s_setup, 1)
                nc.vector.memset(qT[:, :, :, :], 0.0).then_inc(s_setup, 1)
            dve.wait_ge(s_setup, 1 if wide else 3)
            dve.wait_ge(s_w, 16 * s_wn)

            def keys(b, p):
                dve.wait_ge(s_kv, b + 1)
                after(dve, s_S, (b - 1) * HALVES)
                if wide:
                    m = nc.vector.tensor_copy(kT[:, p, :, :], pk.rearrange("p (n k) -> p n k", n=NT))
                else:
                    k4 = pk.unsqueeze(1).broadcast_to([128, HB, NK])
                    m4 = g.headmask[:, :].unsqueeze(2).broadcast_to([128, HB, NK])
                    if bk is None:
                        m = nc.vector.tensor_tensor(kT[:, p, :, :], k4, m4, ALU.mult)
                    else:
                        m = nc.vector.scalar_tensor_tensor(kT[:, p, :, :], k4, BK[:, 0:1], m4, ALU.add, ALU.mult)
                m.then_inc(s_kc, 1)

            def values(b, p):
                dve.wait_ge(s_kv, b + 2)
                after(dve, s_O, b - 1)
                v = pv.rearrange("p (h e) -> p h e", h=H)
                if bv is None:
                    m = nc.vector.tensor_copy(va[:, p, :, 0:D], v)
                else:
                    m = nc.vector.tensor_tensor(va[:, p, :, 0:D], v, BV[:, :].rearrange("p (h e) -> p h e", h=H), ALU.add)
                m.then_inc(s_vc, 1)

            def shift(b, p, half):
                n = b * HALVES + half
                dve.wait_ge(s_S, n + 1)
                after(dve, s_sub, n)
                scored = psS[:, 2 * half:2 * half + 2, 0:HB * NK].rearrange("p a (h k) -> p a h k", h=HB)
                nc.vector.tensor_reduce(mx[:, :].rearrange("p (a h) -> p a h", a=2), scored, AX.X, ALU.max).then_inc(s_max, 1)
                dve.wait_ge(s_max, n + 1)
                after(dve, s_PT, (b - 2) * HALVES + half + 1)
                nc.vector.tensor_tensor(Sx[:, p, 8 * half:8 * half + 8, :].rearrange("p (a h) k -> p a h k", a=2), scored,
                                        mx[:, :].rearrange("p (a h) -> p a h", a=2).unsqueeze(3).broadcast_to([128, 2, HB, NK]),
                                        ALU.subtract).then_inc(s_sub, 1)

            parts = [(0, O_CUT)] + ([(O_CUT, H)] if wide else [])

            def normalise(b, p):
                dve.wait_ge(s_O if wide else s_tok, b + 1)
                after(dve, s_on, b)
                for k, (a, z) in enumerate(parts):
                    o = pO[k].rearrange("p (h e) -> p h e", e=DV)
                    i = nc.vector.reciprocal(rec[:, a:z], o[:, :, D])
                i.then_inc(s_rec, 1)
                dve.wait_ge(s_rec, b + 1)
                if wo is not None:
                    after(dve, s_oT, b - 1)
                else:
                    after(dve, s_x, b - 1)
                for k, (a, z) in enumerate(parts):
                    o = pO[k].rearrange("p (h e) -> p h e", e=DV)
                    i = nc.vector.tensor_tensor(on[:, p, a:z, :], o[:, :, 0:D],
                                                rec[:, a:z].unsqueeze(2).broadcast_to([128, z - a, D]), ALU.mult)
                i.then_inc(s_on, 1)

            def tick(t, p):
                if wide:
                    stage(t, p, 3, NB, normalise)
                stage(t, p, 1, NB, lambda b, q: shift(b, q, 0))
                stage(t, p, 1, NB, values)
                stage(t, p, 0, NB, keys)
                stage(t, p, LAG_X, NB, lambda b, q: N.dve_mean(dve, b, q))
                if not wide:
                    stage(t, p, 1, NB, lambda b, q: shift(b, q, 1))
                    stage(t, p, 3, NB, normalise)
                stage(t, p, LAG_X, NB, lambda b, q: N.dve_xn(dve, b, q))
            ticks(dve, NB, LAGS, tick)



def group(t, u, n=GB):
    return t[:, u * n:(u + 1) * n, :] if isinstance(u, int) else t[:, bass.ds(u * n, n), :]


def flat(t):
    return t.rearrange("p a f -> p (a f)")


def layer_router(nc, g, d, name, wg, bg, softmax_all):
    E = 8
    with ExitStack() as ctx:
        L = Layer(nc, ctx, name)
        s_w, s_logit, s_sb = L.sem("weights"), L.sem("logits"), L.sem("logits_copied")
        s_turned, s_kept, s_exp, s_arg, s_link = L.sem("turned"), L.sem("kept"), L.sem("exp"), L.sem("exp_in"), L.sem("link")
        Wg = L.sb("wg", [F, E])
        Bg = L.sb("bg", [E, 1])
        ls = L.sb("logits", [E, 2, GB * T])
        V = L.sb("values", [T, NB, E])
        first, second = L.sb("first", [T, NB, E]), L.sb("second", [T, NB, E])
        top, low, rank = L.sb("top", [T, NB]), L.sb("low", [T, NB]), L.sb("rank_top", [T, NB])
        psL = L.psum("L", [128, 2, 512])
        psT = L.psum("T", [128, 2, 512])
        block = ctx.enter_context(nc.Block())

        @block.sync
        def _(sp):
            sp.dma_start(Wg[:, :], wg).then_inc(s_w, 16)
            if bg is not None:
                sp.dma_start(Bg[:, :], bg).then_inc(s_w, 16)

        @block.tensor
        def _(pe):
            pe.wait_ge(s_w, 16 if bg is None else 32)

            def logits(u, p):
                after(pe, s_sb, u - 1)
                nc.tensor.matmul(psL[0:E, p, :], Wg[:, :], flat(group(g.XT, u)), start=True, stop=True).then_inc(s_logit, 1)

            def turn(u, p):
                apart(pe, g,
                      (s_sb, u + 1),
                      (s_kept, u - 1))
                for k in range(GB):
                    i = nc.tensor.transpose(psT[:, p, k * E:(k + 1) * E], ls[:, p, k * T:(k + 1) * T], g.ident[0:E, 0:E])
                i.then_inc(s_turned, 1)

            def tick(t, p):
                stage(t, p, 0, NG, logits)
                stage(t, p, 1, NG, turn)
            ticks(pe, NG, 2, tick)

        @block.scalar
        def _(act):
            act.wait_ge(s_w, 16 if bg is None else 32)

            def copy(u, p):
                act.wait_ge(s_logit, u + 1)
                after(act, s_turned, u - 1)
                if bg is None:
                    i = nc.scalar.copy(ls[:, p, :], psL[0:E, p, :])
                else:
                    i = nc.scalar.activation(ls[:, p, :], psL[0:E, p, :], ACT.Identity, bias=Bg[:, 0:1])
                i.then_inc(s_sb, 1)
            ticks(act, NG, 2, lambda t, p: stage(t, p, 0, NG, copy))
            act.wait_ge(s_arg, 1)
            if softmax_all:
                nc.scalar.activation(V[:, :, :], V[:, :, :], ACT.Exp).then_inc(s_exp, 1)
            else:
                nc.scalar.activation(low[:, :], low[:, :], ACT.Exp).then_inc(s_exp, 1)

        @block.vector
        def _(dve):
            def keep(u, p):
                dve.wait_ge(s_turned, u + 1)
                nc.vector.tensor_copy(group(V, u), psT[:, p, 0:GB * E].rearrange("p (a e) -> p a e", a=GB)).then_inc(s_kept, 1)
            ticks(dve, NG, 2, lambda t, p: stage(t, p, 1, NG, keep))
            dve.wait_ge(s_kept, NG)
            link = Link(dve, s_link, 0)
            link.per = 1000
            wide = lambda t: t[:, :].unsqueeze(2).broadcast_to([T, NB, E])
            ranks = g.rank[:, :].unsqueeze(1).broadcast_to([T, NB, E])
            if softmax_all:
                link(nc.vector.tensor_reduce(top[:, :], V[:, :, :], AX.X, ALU.max))
                nc.vector.tensor_tensor(V[:, :, :], V[:, :, :], wide(top), ALU.subtract).then_inc(s_arg, 1)
                dve.wait_ge(s_exp, 1)
                link(nc.vector.tensor_reduce(top[:, :], V[:, :, :], AX.X, ALU.add))
                link(nc.vector.reciprocal(low[:, :], top[:, :]))
                link(nc.vector.tensor_tensor(V[:, :, :], V[:, :, :], wide(low), ALU.mult))

            def choose(one, best):
                link(nc.vector.tensor_reduce(best[:, :], V[:, :, :], AX.X, ALU.max))
                link(nc.vector.tensor_tensor(one[:, :, :], V[:, :, :], wide(best), ALU.is_equal))
                link(nc.vector.tensor_tensor(one[:, :, :], one[:, :, :], ranks, ALU.mult))
                link(nc.vector.tensor_reduce(rank[:, :], one[:, :, :], AX.X, ALU.max))
                link(nc.vector.tensor_tensor(one[:, :, :], one[:, :, :], wide(rank), ALU.is_equal))

            choose(first, top)
            if softmax_all:
                link(nc.vector.tensor_tensor(g.gate[:, :, :], V[:, :, :], first[:, :, :], ALU.mult))
            link(nc.vector.scalar_tensor_tensor(flat(V[:, :, :]), flat(first[:, :, :]), -3e38, flat(V[:, :, :]), ALU.mult, ALU.add))
            choose(second, low)
            if softmax_all:
                link(nc.vector.tensor_tensor(second[:, :, :], second[:, :, :], wide(low), ALU.mult))
                link(nc.vector.tensor_tensor(g.gate[:, :, :], g.gate[:, :, :], second[:, :, :], ALU.add))
                link(nc.vector.tensor_tensor(top[:, :], top[:, :], low[:, :], ALU.add))
                link(nc.vector.tensor_scalar(top[:, :], top[:, :], 1e-8, None, ALU.add))
                link(nc.vector.reciprocal(low[:, :], top[:, :]))
                link(nc.vector.tensor_tensor(g.gate[:, :, :], g.gate[:, :, :], wide(low), ALU.mult))
            else:
                nc.vector.tensor_tensor(low[:, :], low[:, :], top[:, :], ALU.subtract).then_inc(s_arg, 1)
                dve.wait_ge(s_exp, 1)
                link(nc.vector.tensor_scalar(top[:, :], low[:, :], 1.0, None, ALU.add))
                link(nc.vector.reciprocal(rank[:, :], top[:, :]))
                link(nc.vector.tensor_tensor(low[:, :], low[:, :], rank[:, :], ALU.mult))
                link(nc.vector.tensor_tensor(g.gate[:, :, :], first[:, :, :], wide(rank), ALU.mult))
                link(nc.vector.tensor_tensor(second[:, :, :], second[:, :, :], wide(low), ALU.mult))
                link(nc.vector.tensor_tensor(g.gate[:, :, :], g.gate[:, :, :], second[:, :, :], ALU.add))


def layer_experts(nc, g, d):
    E, M, P3 = 8, 4, 3
    GT = GB * T
    with ExitStack() as ctx:
        L = Layer(nc, ctx, "moe")
        s_b, s_sel, s_wh, s_wl = L.sem("biases_in"), L.sem("spread_ready"), L.sem("weights_hi"), L.sem("weights_lo")
        CH = 4
        s_w = [L.sem(f"weights_in{i}") for i in range(2 * CH)]
        s_link, s_xh, s_xl = L.sem("link"), L.sem("x_hi"), L.sem("x_lo")
        s_h, s_act, s_hh, s_hl, s_y = L.sem("hidden"), L.sem("gelu"), L.sem("hidden_hi"), L.sem("hidden_lo"), L.sem("outputs")
        s_gs, s_gt, s_gc, s_sp = L.sem("gates"), L.sem("gates_turned"), L.sem("gates_copied"), L.sem("gates_spread")
        s_gsb = L.sem("spread_copied")
        s_mul, s_add, s_at, s_x = L.sem("gated"), L.sem("added"), L.sem("sum_turned"), L.sem("x_done")
        W1l, W1h = L.sb("w1_lo", [F, E, M * 128], F32R), L.sb("w1_hi", [F, E, M * 128], F32R)
        W2l, W2h = L.sb("w2_lo", [128, E, M, F], F32R), L.sb("w2_hi", [128, E, M, F], F32R)
        B1, B2 = L.sb("b1", [128, E, M]), L.sb("b2", [F, E])
        sel = L.sb("spread", [P3 * E, E, 128], BF16)
        part, rest = L.sb("part", [T, GB, E], BF16), L.sb("rest", [T, GB, E])
        hr = L.sb("hidden", [128, M, GT])
        xs = L.sb("x_parts", [F, 2, 2, GT], F32R)
        hl, hh = L.sb("hidden_lo", [128, 2, M, GT], F32R), L.sb("hidden_hi", [128, 2, M, GT], F32R)
        gs, gT = L.sb("gates", [T, GB, P3 * E]), L.sb("gatesT", [P3 * E, GT], BF16)
        gsb = L.sb("gates_spread", [F, 2, GT])
        tmp, acc = L.sb("gated", [F, 2, GT]), L.sb("sum", [F, 2, GT])
        psH, psY, psG = L.psum("H", [128, 3, 512]), L.psum("Y", [128, 2, 512]), L.psum("G", [128, 512])
        bank = (0, 1, 2, 0)
        psT, psN = L.psum("T", [128, 512]), L.psum("N", [128, 512])
        N = Norm(L, g, GB, s_x, psN, masked=True)
        LAGS = 4
        block = ctx.enter_context(nc.Block())

        sel32 = flat(tmp[0:P3 * E, :, :])
        places = [flat(hr[:, 0:2, :]), flat(hr[:, 2:4, :]), flat(gsb[:, :, :]), flat(acc[:, :, :]), flat(N.xn[:, :, :])]
        PL = len(places)

        def chunk(w1, w2, i):
            e = slice(i % CH * E // CH, (i % CH + 1) * E // CH)
            return w1[:, e, :].rearrange("p e h -> p (e h)") if i < CH else w2[:, e, :, :].rearrange("p e m f -> p (e m f)")

        def f32(ap):
            return ap.bitcast(F32)

        def steps(t, p, fn_now, fn_before, extra):
            for e in range(E):
                stage(t, p, 1, NG, lambda u, q: fn_now(u, q, e))
                if e:
                    stage(t, p, 1, NG, lambda u, q: fn_before(u, q, e - 1))
                else:
                    stage(t, p, 2, NG, lambda u, q: fn_before(u, q, E - 1))
                extra(e)

        @block.sync
        def _(sp):
            def load(i):
                sp.dma_start(places[i % PL], chunk(d["m0_w1"], d["m0_w2"], i)).then_inc(s_w[i], 16)

            load(0)
            for t, k in ((B1[:], "m0_b1"), (B2[:], "m0_b2"), (sel32, "c_spread1")):
                sp.dma_start(t, d[k]).then_inc(s_b, 16)
            for i in range(1, 2 * CH):
                if i >= PL:
                    sp.wait_ge(s_wl, i - PL + 1)
                load(i)

        @block.tensor
        def _(pe):
            pe.wait_ge(s_sel, 1)

            def hidden(u, p, e):
                if isinstance(u, int) and u == 0 and e % (E // CH) == 0:
                    pe.wait_ge(s_wl, e * CH // E + 1)
                if e == 0:
                    pe.wait_ge(s_xl, u + 1)
                for m in range(M):
                    h = psH[:, bank[m], :]
                    if m == 0:
                        after(pe, s_act, (u * E + e) * M)
                    if m == 3:
                        pe.wait_ge(s_act, (u * E + e) * M + 1)
                    c = slice(m * 128, (m + 1) * 128)
                    nc.tensor.matmul(h, W1h[:, e, c], xs[:, p, 0, :], start=True, stop=False)
                    nc.tensor.matmul(h, W1h[:, e, c], xs[:, p, 1, :], start=False, stop=False)
                    nc.tensor.matmul(h, W1l[:, e, c], xs[:, p, 0, :], start=False, stop=True).then_inc(s_h, 1)

            def outputs(u, p, e):
                n = u * E + e
                if e == 0:
                    pe.wait_ge(s_gc, u + 1)
                after(pe, s_gsb, n)
                after(pe, s_mul, n - 1)
                nc.tensor.matmul(psG[:, :], sel[:, e, :], gT[:, :], start=True, stop=True).then_inc(s_sp, 1)
                pe.wait_ge(s_hl, (n + 1) * M)
                if isinstance(u, int) and u == 0 and e % (E // CH) == 0:
                    pe.wait_ge(s_wl, CH + e * CH // E + 1)
                for m in range(M):
                    y = psY[:, e % 2, :]
                    nc.tensor.matmul(y, W2h[:, e, m, :], hh[:, e % 2, m, :], start=(m == 0), stop=False)
                    nc.tensor.matmul(y, W2h[:, e, m, :], hl[:, e % 2, m, :], start=False, stop=False)
                    i = nc.tensor.matmul(y, W2l[:, e, m, :], hh[:, e % 2, m, :], start=False, stop=(m == M - 1))
                i.then_inc(s_y, 1)

            def turn_gates(u, p):
                pe.wait_ge(s_gs, u + 1)
                after(pe, s_x, u - 1)
                after(pe, s_gc, u)
                for k in range(GB):
                    i = nc.tensor.transpose(psT[0:P3 * E, k * T:(k + 1) * T], gs[:, k, :], g.ident[:, :])
                i.then_inc(s_gt, 1)

            def turn_sum(u, p):
                pe.wait_ge(s_add, (u + 1) * (E - 1))
                pe.wait_ge(s_gc, u + 2 if not isinstance(u, int) else min(u + 2, NG))
                after(pe, s_x, u)
                for k in range(GB):
                    i = nc.tensor.transpose(psT[:, k * F:(k + 1) * F], acc[:, p, k * T:(k + 1) * T], g.ident[:, :])
                i.then_inc(s_at, 1)

            def tick(t, p):
                def extra(e):
                    if e == 0:
                        stage(t, p, 1, NG, turn_gates)
                    if e == 3:
                        stage(t, p, 2, NG, turn_sum)
                    if e == 5:
                        stage(t, p, 3, NG, lambda u, q: N.pe_turn(pe, u, q))
                steps(t, p, hidden, outputs, extra)
            ticks(pe, NG, LAGS, tick)

        @block.scalar
        def _(act):

            def x_hi(u, p):
                after(act, s_h, (u - 1) * E * M)
                nc.scalar.copy(xs[:, p, 0, :], flat(group(g.XT, u))).then_inc(s_xh, 1)

            def gelu(u, p, e):
                n = (u * E + e) * M

                def hi(m):
                    act.wait_ge(s_act, n + m + 1)
                    nc.scalar.copy(hh[:, e % 2, m, :], hr[:, m, :]).then_inc(s_hh, 1)

                for m in range(M):
                    act.wait_ge(s_h, n + m + 1)
                    after(act, s_hl, n - M + m + 1)
                    if m == 0:
                        after(act, s_y, u * E + e - 1)
                    nc.scalar.activation(hr[:, m, :], psH[:, bank[m], :], ACT.Gelu_apprx_tanh, bias=B1[:, e, m:m + 1]).then_inc(s_act, 1)
                    if m:
                        hi(m - 1)
                hi(M - 1)

            def spread(u, p, e):
                n = u * E + e
                act.wait_ge(s_sp, n + 1)
                after(act, s_mul, n - 1)
                nc.scalar.copy(gsb[:, e % 2, :], psG[:, :]).then_inc(s_gsb, 1)

            def gates(u, p):
                act.wait_ge(s_gt, u + 1)
                after(act, s_sp, u * E)
                nc.scalar.copy(gT[:, :], psT[0:P3 * E, :]).then_inc(s_gc, 1)

            def tick(t, p):
                if isinstance(t, int) and t == 0:
                    x_hi(0, 0)
                    act.wait_ge(s_b, 48)
                    nc.scalar.copy(sel[:, :, :].rearrange("p e f -> p (e f)"), sel32).then_inc(s_sel, 1)
                    for i in range(2 * CH):
                        act.wait_ge(s_w[i], 16)
                        nc.scalar.copy(chunk(W1h, W2h, i), places[i % PL]).then_inc(s_wh, 1)
                    act.wait_ge(s_wl, 2 * CH)
                    return

                def extra(e):
                    if e == 0:
                        stage(t, p, 1, NG, gates)
                    if e == 4:
                        stage(t, p, 0, NG, x_hi)
                    if e == 5:
                        stage(t, p, 3, NG, lambda u, q: N.act_store(act, u, q))
                steps(t, p, gelu, spread, extra)
            ticks(act, NG, LAGS, tick)

        @block.gpsimd
        def _(pool):
            link = Link(pool, s_link, 3 * P3 - 1, g)

            def gates(u, p):
                link.unit(u)
                after(pool, s_gt, u)
                link(nc.gpsimd.tensor_copy(rest[:, :, :], group(g.gate, u)))
                for k in range(P3):
                    at = gs[:, :, k * E:(k + 1) * E]
                    link(nc.gpsimd.tensor_copy(part[:, :, :], rest[:, :, :]))
                    i = nc.gpsimd.tensor_copy(at, part[:, :, :])
                    if k < P3 - 1:
                        link(i)
                        link(nc.gpsimd.tensor_tensor(rest[:, :, :], rest[:, :, :], at, ALU.subtract))
                i.then_inc(s_gs, 1)

            def add(u, p, e):
                if e == 0:
                    return
                pool.wait_ge(s_mul, u * E + e + 1)
                after(pool, s_add, u * (E - 1) + e - 1)
                nc.gpsimd.tensor_tensor(acc[:, p, :], acc[:, p, :], tmp[:, e % 2, :], ALU.add).then_inc(s_add, 1)

            def tick(t, p):
                def extra(e):
                    if e == 3:
                        stage(t, p, 3, NG, lambda u, q: N.pool_rstd(pool, u, q))
                    if e == 5:
                        stage(t, p, 0, NG, gates)
                steps(t, p, lambda u, q, e: None, add, extra)
            ticks(pool, NG, LAGS, tick)

        @block.vector
        def _(dve):
            def x_lo(u, p):
                dve.wait_ge(s_xh, u + 1)
                nc.vector.tensor_tensor(xs[:, p, 1, :], flat(group(g.XT, u)), f32(xs[:, p, 0, :]), ALU.subtract).then_inc(s_xl, 1)

            def lo(u, p, e):
                for m in range(M):
                    dve.wait_ge(s_hh, (u * E + e) * M + m + 1)
                    nc.vector.tensor_tensor(hl[:, e % 2, m, :], hr[:, m, :], f32(hh[:, e % 2, m, :]), ALU.subtract).then_inc(s_hl, 1)

            def gated(u, p, e):
                n = u * E + e
                dve.wait_ge(s_gsb, n + 1)
                dve.wait_ge(s_y, n + 1)
                if e == 0:
                    after(dve, s_at, u - 1)
                    out = acc[:, p, :]
                else:
                    after(dve, s_add, u * (E - 1) + max(0, e - 2))
                    out = tmp[:, e % 2, :]
                nc.vector.scalar_tensor_tensor(out, psY[:, e % 2, :], B2[:, e:e + 1], gsb[:, e % 2, :], ALU.add, ALU.mult).then_inc(s_mul, 1)

            def update(u, p):
                dve.wait_ge(s_at, u + 1)
                x = flat(group(g.X, u))
                nc.vector.tensor_tensor(x, psT[:, :], x, ALU.add).then_inc(s_x, 1)

            def tick(t, p):
                if isinstance(t, int) and t == 0:
                    x_lo(0, 0)
                    for i in range(2 * CH):
                        dve.wait_ge(s_wh, i + 1)
                        nc.vector.tensor_tensor(chunk(W1l, W2l, i), places[i % PL], f32(chunk(W1h, W2h, i)),
                                                ALU.subtract).then_inc(s_wl, 1)
                    dve.wait_ge(s_sel, 1)
                    return

                def extra(e):
                    if e == 2:
                        stage(t, p, 3, NG, lambda u, q: N.dve_mean(dve, u, q))
                    if e == 3:
                        stage(t, p, 2, NG, update)
                    if e == 4:
                        stage(t, p, 0, NG, x_lo)
                        stage(t, p, 3, NG, lambda u, q: N.dve_xn(dve, u, q))
                steps(t, p, lo, gated, extra)
            ticks(dve, NG, LAGS, tick)


def layer_channel_mix(nc, g, d):
    with ExitStack() as ctx:
        L = Layer(nc, ctx, "mix")
        s_w, s_omu = L.sem("weights"), L.sem("one_minus_mu")
        s_r0, s_k0, s_xr, s_xk = L.sem("r_part"), L.sem("k_part"), L.sem("xr"), L.sem("xk")
        s_zr, s_zk, s_tanh, s_relu, s_sq = L.sem("zr"), L.sem("zk"), L.sem("tanh"), L.sem("relu"), L.sem("squared")
        s_v, s_rv, s_x = L.sem("v"), L.sem("rv"), L.sem("x_done")
        Wr, Wk, Wv = (L.sb(n, [F, F]) for n in ("wr", "wk", "wv"))
        mu = L.sb("mu", [F, 2])
        omu = L.sb("one_minus_mu", [F, 2])
        xm = L.sb("mixed", [F, 2, GB, T])
        rs = L.sb("tanh", [T, 2, GB * F])
        ks = L.sb("kact", [F, 2, GB * T])
        rv = L.sb("rv", [T, GB * F])
        psR, psK, psV, psN = (L.psum(n, [128, 512]) for n in ("R", "K", "V", "N"))
        N = Norm(L, g, GB, s_x, psN, top=g.top)
        N.s_top = L.sem("top")
        LAGS = 4
        block = ctx.enter_context(nc.Block())

        @block.sync
        def _(sp):
            for t, k in ((Wr, "m1_wr"), (Wk, "m1_wk"), (Wv, "m1_wv"), (mu, "m1_mu")):
                sp.dma_start(t[:], d[k]).then_inc(s_w, 16)

        @block.tensor
        def _(pe):
            pe.wait_ge(s_w, 64)

            def inner(u, p):
                pe.wait_ge(s_xr, u + 1)
                after(pe, s_tanh, u)
                for k in range(GB):
                    i = nc.tensor.matmul(psR[:, k * F:(k + 1) * F], xm[:, 0, k, :], Wr[:, :], start=True, stop=True)
                i.then_inc(s_zr, 1)
                pe.wait_ge(s_xk, u + 1)
                after(pe, s_relu, u)
                nc.tensor.matmul(psK[:, :], Wk[:, :], flat(xm[:, 1, :, :]), start=True, stop=True).then_inc(s_zk, 1)

            def outer(u, p):
                pe.wait_ge(s_sq, u + 1)
                after(pe, s_rv, u)
                for k in range(GB):
                    i = nc.tensor.matmul(psV[:, k * F:(k + 1) * F], ks[:, p, k * T:(k + 1) * T], Wv[:, :], start=True, stop=True)
                i.then_inc(s_v, 1)

            def tick(t, p):
                stage(t, p, 0, NG, inner)
                stage(t, p, 1, NG, outer)
                stage(t, p, 3, NG, lambda u, q: N.pe_turn(pe, u, q))
            ticks(pe, NG, LAGS, tick)

        @block.scalar
        def _(act):
            def inner(u, p):
                act.wait_ge(s_zr, u + 1)
                after(act, s_rv, u - 1)
                nc.scalar.activation(rs[:, p, :], psR[:, :], ACT.Tanh, scale=0.5).then_inc(s_tanh, 1)
                act.wait_ge(s_zk, u + 1)
                after(act, s_v, u - 1)
                nc.scalar.activation(ks[:, p, :], psK[:, :], ACT.Relu).then_inc(s_relu, 1)
                act.wait_ge(s_relu, u + 1)
                nc.scalar.activation(ks[:, p, :], ks[:, p, :], ACT.Square).then_inc(s_sq, 1)

            def tick(t, p):
                stage(t, p, 0, NG, inner)
                stage(t, p, 3, NG, lambda u, q: N.act_store(act, u, q))
            ticks(act, NG, LAGS, tick)

        @block.gpsimd
        def _(pool):
            ticks(pool, NG, LAGS, lambda t, p: stage(t, p, 2, NG, lambda u, q: N.pool_rstd(pool, u, q)))

        @block.vector
        def _(dve):
            dve.wait_ge(s_w, 64)
            nc.vector.tensor_scalar(omu[:, :], mu[:, :], -1.0, 1.0, ALU.mult, ALU.add).then_inc(s_omu, 1)
            dve.wait_ge(s_omu, 1)

            def mix(u, p):
                x = group(g.XT, u)
                for j, (part, done, used) in enumerate(((s_r0, s_xr, s_zr), (s_k0, s_xk, s_zk))):
                    after(dve, used, u)
                    nc.vector.tensor_scalar(xm[:, j, :, :], x, mu[:, j:j + 1], None, ALU.mult).then_inc(part, 1)
                for j, (part, done, used) in enumerate(((s_r0, s_xr, s_zr), (s_k0, s_xk, s_zk))):
                    dve.wait_ge(part, u + 1)
                    m = xm[:, j, :, 1:T]
                    nc.vector.scalar_tensor_tensor(m, x[:, :, 0:T - 1], omu[:, j:j + 1], m, ALU.mult, ALU.add).then_inc(done, 1)

            def update(u, p):
                dve.wait_ge(s_v, u + 1)
                dve.wait_ge(s_tanh, u + 1)
                after(dve, s_x, u)
                nc.vector.scalar_tensor_tensor(rv[:, :], rs[:, p, :], 1.0, psV[:, :], ALU.add, ALU.mult).then_inc(s_rv, 1)
                dve.wait_ge(s_rv, u + 1)
                x = flat(group(g.X, u))
                nc.vector.scalar_tensor_tensor(x, rv[:, :], 0.5, x, ALU.mult, ALU.add).then_inc(s_x, 1)

            def tick(t, p):
                stage(t, p, 0, NG, mix)
                stage(t, p, 2, NG, update)
                stage(t, p, 2, NG, lambda u, q: N.dve_mean(dve, u, q))
                stage(t, p, 3, NG, lambda u, q: N.dve_xn(dve, u, q))
            ticks(dve, NG, LAGS, tick)




BIT_COLS = {"d2v": (0, 128), "img": (128, 256), "txt": (256, 384), "att0": (384, 512), "att1": (512, 640),
            "f1": (640, 1664), "f2": (1664, 2176)}
BIT_AT = {k: i for i, k in enumerate(BIT_COLS)}


def quant_scale(nc, dve, link, tops, one, out, floor, levels):
    link(nc.vector.tensor_scalar(out[:, 0:1], one, floor, 1.0 / levels, ALU.max, ALU.mult))
    link(nc.vector.reciprocal(out[:, 1:2], out[:, 0:1]))


def layer_bit_weights(nc, g, d):
    n = len(BIT_COLS)
    with ExitStack() as ctx:
        L = Layer(nc, ctx, "bw")
        s_w, s_part, s_all, s_link = L.sem("weights"), L.sem("sums"), L.sem("totals"), L.sem("link")
        raw = L.sb("raw", [128, 2176])
        neg = L.sb("negative", [128, 1024])
        count = L.sb("inverse_counts", [128, n])
        sums, total, cut = L.sb("sums", [128, n]), L.sb("totals", [128, n]), L.sb("cuts", [128, 2, n])
        block = ctx.enter_context(nc.Block())

        @block.sync
        def _(sp):
            sp.dma_start(raw[0:CK, 0:128], d["b_d2v_w"]).then_inc(s_w, 16)
            sp.dma_start(raw[:, 128:2176], d["b_rest_w"]).then_inc(s_w, 16)
            sp.dma_start(count[:, :], d["c_bit_inverse_counts"]).then_inc(s_w, 16)

        @block.gpsimd
        def _(pool):
            pool.wait_ge(s_part, 1)
            nc.gpsimd.partition_all_reduce(total[:, :], sums[:, :], 128, RADD).then_inc(s_all, 1)

        @block.vector
        def _(dve):
            link = Link(dve, s_link, 1000)
            link(nc.vector.memset(raw[96:128, 0:128], 0.0))
            dve.wait_ge(s_w, 48)
            for i, (a, z) in enumerate(BIT_COLS.values()):
                k = nc.vector.tensor_reduce(sums[:, i:i + 1], raw[:, a:z], AX.X, ALU.add, apply_absolute_value=True)
            k.then_inc(s_part, 1)
            dve.wait_ge(s_all, 1)
            link(nc.vector.tensor_tensor(total[:, :], total[:, :], count[:, :], ALU.mult))
            link(nc.vector.tensor_scalar(g.ws[:, :], total[:, :], 1e-5, None, ALU.max))
            link(nc.vector.tensor_scalar(cut[:, 0, :], g.ws[:, :], 0.5, None, ALU.mult))
            link(nc.vector.tensor_scalar(cut[:, 1, :], g.ws[:, :], -0.5, None, ALU.mult))
            for i, (a, z) in enumerate(BIT_COLS.values()):
                link(nc.vector.tensor_scalar(neg[:, 0:z - a], raw[:, a:z], cut[:, 1, i:i + 1], None, ALU.is_lt))
                link(nc.vector.scalar_tensor_tensor(g.qw[:, a:z], raw[:, a:z], cut[:, 0, i:i + 1], neg[:, 0:z - a],
                                                    ALU.is_gt, ALU.subtract))


def layer_image(nc, g, d):
    CH = GB * NK
    with ExitStack() as ctx:
        L = Layer(nc, ctx, "im")
        s_in, s_b, s_link = L.sem("ctx_in"), L.sem("biases"), L.sem("link")
        s_top, s_all = L.sem("top"), L.sem("largest")
        s_avg = L.sem("average")
        A = L.sb("features", [128, NB, NK])
        qf = L.sb("shifted", [128, 2, CH])
        qb = L.sb("quantised", [128, 2, CH], BF16)
        ko = L.sb("keys", [128, 2, 2, CH])
        tops, one, most = L.sb("tops", [128, NG]), L.sb("one", [128, 1]), L.sb("most", [128, 1])
        scale, cs = L.sb("scale", [128, 2]), L.sb("product_scale", [128, 2])
        Bv, Bi, Ba = L.sb("b_d2v", [128, 1]), L.sb("b_img", [128, 1]), L.sb("b_att", [128, 2])
        ps = L.psum("out", [128, 4, 512])
        rounds = [("vis", ["d2v"]), ("img", ["img"]), ("key", ["att0", "att1"])]
        s_q, s_qf, s_mm, s_out, s_max = ([L.sem(f"{r}_{n}") for r, _ in rounds]
                                         for n in ("quantised", "shifted", "product", "features", "max"))
        s_ready = L.sem("scales_ready")
        s_kout = [L.sem("keys_out_even"), L.sem("keys_out_odd")]
        keys = d["keys"].rearrange("b j p k -> p b j k")
        block = ctx.enter_context(nc.Block())

        def chunk(u):
            return flat(group(A, u))

        @block.sync
        def _(sp):
            sp.dma_start(A[0:CK, :, :], d["ctx_t"].rearrange("b c k -> c b k")).then_inc(s_in, 16)
            sp.dma_start(Bv[:, :], d["b_d2v_b"]).then_inc(s_b, 16)
            sp.dma_start(Bi[:, :], d["b_img_b"]).then_inc(s_b, 16)
            sp.dma_start(Ba[:, :], d["b_att_b"]).then_inc(s_b, 16)

            def out(u, p):
                sp.wait_ge(s_out[2], u + 1)
                for j in range(2):
                    dst = keys[:, u * GB:(u + 1) * GB, j, :] if isinstance(u, int) else keys[:, bass.ds(u * GB, GB), j, :]
                    sp.dma_start(dst, ko[:, p, j, :].rearrange("p (a k) -> p a k", a=GB)).then_inc(s_kout[p], 16)
            ticks(sp, NG, 2, lambda t, p: stage(t, p, 1, NG, out))
            for s in s_kout:
                sp.wait_ge(s, 16 * NG)

        @block.gpsimd
        def _(pool):
            for r in range(3):
                pool.wait_ge(s_top, r + 1)
                n = CK if r == 0 else 128
                if r == 0:
                    nc.gpsimd.memset(most[:, :], 0.0).then_inc(s_avg, 1)
                    pool.wait_ge(s_avg, 1)
                nc.gpsimd.partition_all_reduce(most[:, :], one[:, :], 128, RMAX).then_inc(s_all, 1)

        @block.vector
        def _(dve):
            link = Link(dve, s_link, 1000)
            link(nc.vector.memset(A[96:128, :, :], 0.0))
            dve.wait_ge(s_in, 16)
            link(nc.vector.tensor_reduce(one[:, :], flat(A[:, :, :]), AX.X, ALU.max, apply_absolute_value=True))
            for r, (name, outs) in enumerate(rounds):
                if r:
                    link(nc.vector.tensor_reduce(one[:, :], tops[:, :], AX.X, ALU.max))
                dve.nop().then_inc(s_top, 1)
                dve.wait_ge(s_all, r + 1)
                quant_scale(nc, dve, link, None, most[:, 0:1], scale, 1e-8, 127.0)
                for j, w in enumerate(outs):
                    i = BIT_AT[w]
                    link(nc.vector.tensor_tensor(cs[:, j:j + 1], g.ws[:, i:i + 1], scale[:, 0:1], ALU.mult))
                dve.nop().then_inc(s_ready, 1)
                if r == 2:
                    link(nc.vector.tensor_reduce(g.avg[:, :], A[:, :, :], AX.X, ALU.add))
                    link(nc.vector.tensor_scalar(g.avg[:, :], g.avg[:, :], 1.0 / NK, None, ALU.mult))

                def quantise(u, p):
                    after(dve, s_mm[r], u - 1)
                    nc.vector.tensor_scalar(qf[:, p, :], chunk(u), scale[:, 1:2], MAGIC, ALU.mult, ALU.add).then_inc(s_qf[r], 1)
                    dve.wait_ge(s_qf[r], u + 1)
                    nc.vector.tensor_scalar(qb[:, p, :], qf[:, p, :], MAGIC, None, ALU.subtract).then_inc(s_q[r], 1)

                def largest(u, p):
                    dve.wait_ge(s_out[r], u + 1)
                    top = tops[:, u:u + 1] if isinstance(u, int) else tops[:, bass.ds(u, 1)]
                    nc.vector.tensor_reduce(top, chunk(u), AX.X, ALU.max, apply_absolute_value=True).then_inc(s_max[r], 1)

                def tick(t, p):
                    stage(t, p, 0, NG, quantise)
                    if r < 2:
                        stage(t, p, 2, NG, largest)
                ticks(dve, NG, 2, tick)
                if r < 2:
                    dve.wait_ge(s_max[r], NG)

        @block.tensor
        def _(pe):
            for r, (name, outs) in enumerate(rounds):
                def product(u, p):
                    pe.wait_ge(s_q[r], u + 1)
                    after(pe, s_out[r], u - 1)
                    for j, w in enumerate(outs):
                        a, z = BIT_COLS[w]
                        i = nc.tensor.matmul(ps[:, 2 * p + j, 0:CH], g.qw[:, a:z], qb[:, p, :], start=True, stop=True)
                    i.then_inc(s_mm[r], 1)
                ticks(pe, NG, 2, lambda t, p: stage(t, p, 0, NG, product))
                if r < 2:
                    pe.wait_ge(s_out[r], NG)

        @block.scalar
        def _(act):
            act.wait_ge(s_b, 48)
            for r, (name, outs) in enumerate(rounds):
                act.wait_ge(s_ready, r + 1)

                def feature(u, p):
                    act.wait_ge(s_mm[r], u + 1)
                    if r < 2:
                        nc.scalar.activation(chunk(u), ps[:, 2 * p, 0:CH], ACT.Identity, bias=(Bv, Bi)[r][:, 0:1],
                                             scale=cs[:, 0:1]).then_inc(s_out[r], 1)
                        return
                    if not isinstance(u, int) or u >= 2:
                        act.wait_ge(s_kout[p], (u - p) * 16)
                    for j in range(2):
                        i = nc.scalar.activation(ko[:, p, j, :], ps[:, 2 * p + j, 0:CH], ACT.Identity, bias=Ba[:, j:j + 1],
                                                 scale=cs[:, j:j + 1])
                    i.then_inc(s_out[2], 1)
                ticks(act, NG, 2, lambda t, p: stage(t, p, 0, NG, feature))


def layer_fused(nc, g, d):
    D2 = 64
    with ExitStack() as ctx:
        L = Layer(nc, ctx, "fu")
        s_w, s_part, s_all, s_link, s_scale = L.sem("weights"), L.sem("part"), L.sem("largest"), L.sem("link"), L.sem("scale_ready")
        s_qf, s_q, s_f, s_fu = L.sem("shifted"), L.sem("quantised"), L.sem("text"), L.sem("fused0")
        s_end, s_endc, s_topd = L.sem("end_turned"), L.sem("end_stored"), L.sem("top")
        s_kd = [[L.sem(f"keys{a}_{n}") for n in ("even", "odd")] for a in range(2)]
        names = ("turned", "copied", "keys_turned", "keys_copied", "scores", "max", "shifted", "exp", "probs_turned",
                 "probs_copied", "outputs", "inverse", "normed", "fused_lo", "fused")
        s = [{n: L.sem(f"a{a}_{n}") for n in names} for a in range(2)]
        BT = L.sb("b_txt", [128, F])
        one, most, scale, cs = L.sb("one", [128, 1]), L.sb("most", [128, 1]), L.sb("scale", [128, 2]), L.sb("product_scale", [128, 1])
        qf = L.sb("shifted", [F, GB * T])
        qb = L.sb("quantised", [F, 2, GB * T], BF16)
        fu = [L.sb(f"fused{i}", [T, 2, GB, F]) for i in range(3)]
        fT = [L.sb(f"fusedT{a}", [F, GB, T]) for a in range(2)]
        kd = [L.sb(f"keys{a}", [128, 2, GB, NK]) for a in range(2)]
        kt = [L.sb(f"keys_turned{a}", [NK, 2, GB, D2 + 1]) for a in range(2)]
        P = [L.sb(f"probs{a}", [T, GB, NK]) for a in range(2)]
        PT = [L.sb(f"probsT{a}", [NK, GB, T]) for a in range(2)]
        mx = [L.sb(f"max{a}", [T, GB]) for a in range(2)]
        rec = [L.sb(f"inverse{a}", [T, GB]) for a in range(2)]
        o = [L.sb(f"normed{a}", [T, GB, D2]) for a in range(2)]
        psF, psE = L.psum("F", [128, 512]), L.psum("E", [128, 512])
        psA = [L.psum(f"A{a}", [128, 512]) for a in range(2)]
        psB = [L.psum(f"B{a}", [128, 512]) for a in range(2)]
        psK = [L.psum(f"K{a}", [128, 512]) for a in range(2)]
        LAGS = 4
        keys = d["keys"].rearrange("b j p k -> p b j k")
        block = ctx.enter_context(nc.Block())

        @block.sync
        def _(sp):
            sp.dma_start(BT[:, :], d["b_txt_b"].partition_broadcast(128)).then_inc(s_w, 16)

            def load(u, p, a):
                after(sp, s[a]["scores"], u - 1)
                after(sp, s[a]["keys_turned"], u - 1)
                src = keys[:, u * GB:(u + 1) * GB, a, :] if isinstance(u, int) else keys[:, bass.ds(u * GB, GB), a, :]
                sp.dma_start(kd[a][:, p, :, :], src).then_inc(s_kd[a][p], 16)

            def tick(t, p):
                stage(t, p, 2, NG, lambda u, q: load(u, q, 1))
                stage(t, p, 0, NG, lambda u, q: load(u, q, 0))
            ticks(sp, NG, LAGS, tick)

        @block.gpsimd
        def _(pool):
            pool.wait_ge(s_part, 1)
            nc.gpsimd.partition_all_reduce(most[:, :], one[:, :], 128, RMAX).then_inc(s_all, 1)

        @block.vector
        def _(dve):
            link = Link(dve, s_link, 1000)
            nc.vector.tensor_reduce(one[:, :], g.top[:, 0:g.tops], AX.X, ALU.max).then_inc(s_part, 1)
            dve.wait_ge(s_all, 1)
            quant_scale(nc, dve, link, None, most[:, 0:1], scale, 1e-8, 127.0)
            i = BIT_AT["txt"]
            link(nc.vector.tensor_tensor(cs[:, :], g.ws[:, i:i + 1], scale[:, 0:1], ALU.mult))
            for a in range(2):
                link(nc.vector.memset(kt[a][:, :, :, :], 1.0))
            dve.nop().then_inc(s_scale, 1)
            dve.wait_ge(s_w, 16)

            def quantise(u, p):
                after(dve, s_q, u)
                nc.vector.tensor_scalar(qf[:, :], flat(group(g.XT, u)), scale[:, 1:2], MAGIC, ALU.mult, ALU.add).then_inc(s_qf, 1)
                dve.wait_ge(s_qf, u + 1)
                after(dve, s_f, u - 1)
                nc.vector.tensor_scalar(qb[:, p, :], qf[:, :], MAGIC, None, ALU.subtract).then_inc(s_q, 1)

            def text(u, p):
                dve.wait_ge(s_f, u + 1)
                after(dve, s[0]["fused"], u - 1)
                nc.vector.scalar_tensor_tensor(fu[0][:, p, :, :], psF[:, :].rearrange("p (a f) -> p a f", a=GB), cs[:, 0:1],
                                               BT[:, :].unsqueeze(1).broadcast_to([128, GB, F]), ALU.mult, ALU.add).then_inc(s_fu, 1)

            def shift(u, p, a):
                dve.wait_ge(s[a]["scores"], u + 1)
                x = psB[a][:, 0:GB * NK].rearrange("p (a k) -> p a k", a=GB)
                after(dve, s[a]["shifted"], u)
                nc.vector.tensor_reduce(mx[a][:, :], x, AX.X, ALU.max).then_inc(s[a]["max"], 1)
                dve.wait_ge(s[a]["max"], u + 1)
                after(dve, s[a]["probs_turned"], u)
                nc.vector.tensor_tensor(P[a][:, :, :], x, mx[a][:, :].unsqueeze(2).broadcast_to([128, GB, NK]),
                                        ALU.subtract).then_inc(s[a]["shifted"], 1)

            def attend(u, p, a):
                dve.wait_ge(s[a]["outputs"], u + 1)
                x = psB[a][:, 0:GB * (D2 + 1)].rearrange("p (a e) -> p a e", a=GB)
                after(dve, s[a]["normed"], u)
                nc.vector.reciprocal(rec[a][:, :], x[:, :, D2]).then_inc(s[a]["inverse"], 1)
                dve.wait_ge(s[a]["inverse"], u + 1)
                after(dve, s[a]["fused"], u)
                nc.vector.tensor_tensor(o[a][:, :, :], x[:, :, 0:D2], rec[a][:, :].unsqueeze(2).broadcast_to([128, GB, D2]),
                                        ALU.mult).then_inc(s[a]["normed"], 1)
                dve.wait_ge(s[a]["normed"], u + 1)
                if a == 0:
                    after(dve, s[1]["fused"], u - 1)
                else:
                    after(dve, s_end, u - 1)
                    after(dve, s_topd, u - 1)
                for k, n in ((0, "fused_lo"), (1, "fused")):
                    nc.vector.scalar_tensor_tensor(fu[a + 1][:, p, :, k * D2:(k + 1) * D2], o[a][:, :, :], 0.1,
                                                   fu[a][:, p, :, k * D2:(k + 1) * D2], ALU.mult, ALU.add).then_inc(s[a][n], 1)

            def largest(u, p):
                dve.wait_ge(s[1]["fused"], u + 1)
                dve.wait_ge(s[1]["fused_lo"], u + 1)
                top = g.top[:, u:u + 1] if isinstance(u, int) else g.top[:, bass.ds(u, 1)]
                nc.vector.tensor_reduce(top, flat(fu[2][:, p, :, :]), AX.X, ALU.max, apply_absolute_value=True).then_inc(s_topd, 1)

            def tick(t, p):
                stage(t, p, 0, NG, quantise)
                stage(t, p, 3, NG, lambda u, q: shift(u, q, 1))
                stage(t, p, 2, NG, lambda u, q: attend(u, q, 0))
                stage(t, p, 0, NG, text)
                stage(t, p, 1, NG, lambda u, q: shift(u, q, 0))
                stage(t, p, 3, NG, lambda u, q: attend(u, q, 1))
                stage(t, p, 3, NG, largest)
            ticks(dve, NG, LAGS, tick)

        @block.tensor
        def _(pe):
            pe.wait_ge(s_scale, 1)

            def text(u, p):
                pe.wait_ge(s_q, u + 1)
                after(pe, s_fu, u)
                a, z = BIT_COLS["txt"]
                for k in range(GB):
                    i = nc.tensor.matmul(psF[:, k * F:(k + 1) * F], qb[:, p, k * T:(k + 1) * T], g.qw[:, a:z], start=True, stop=True)
                i.then_inc(s_f, 1)

            def turn(u, p, a):
                if a == 0:
                    pe.wait_ge(s_fu, u + 1)
                else:
                    pe.wait_ge(s[0]["fused"], u + 1)
                    pe.wait_ge(s[0]["fused_lo"], u + 1)
                after(pe, s[a]["probs_copied"], u)
                for k in range(GB):
                    i = nc.tensor.transpose(psA[a][:, k * T:(k + 1) * T], fu[a][:, p, k, :], g.ident[:, :])
                i.then_inc(s[a]["turned"], 1)

            def turn_keys(u, p, a):
                apart(pe, g,
                      (s_kd[a][p], (u - p) * 8 + 16),
                      (s[a]["keys_copied"], u))
                for k in range(GB):
                    i = nc.tensor.transpose(psK[a][0:NK, k * D2:(k + 1) * D2], kd[a][0:D2, p, k, :], g.ident[0:D2, 0:D2])
                i.then_inc(s[a]["keys_turned"], 1)

            def scores(u, p, a):
                pe.wait_ge(s[a]["copied"], u + 1)
                after(pe, s[a]["normed"], u)
                pe.wait_ge(s_kd[a][p], (u - p) * 8 + 16)
                for k in range(GB):
                    i = nc.tensor.matmul(psB[a][:, k * NK:(k + 1) * NK], fT[a][:, k, :], kd[a][:, p, k, :], start=True, stop=True)
                i.then_inc(s[a]["scores"], 1)

            def turn_probs(u, p, a):
                pe.wait_ge(s[a]["exp"], u + 1)
                for k in range(GB):
                    i = nc.tensor.transpose(psA[a][0:NK, k * T:(k + 1) * T], P[a][:, k, :], g.ident[:, :])
                i.then_inc(s[a]["probs_turned"], 1)

            def outputs(u, p, a):
                pe.wait_ge(s[a]["probs_copied"], u + 1)
                pe.wait_ge(s[a]["keys_copied"], u + 1)
                for k in range(GB):
                    i = nc.tensor.matmul(psB[a][:, k * (D2 + 1):(k + 1) * (D2 + 1)], PT[a][:, k, :], kt[a][:, p, k, :], start=True, stop=True)
                i.then_inc(s[a]["outputs"], 1)

            def end(u, p):
                pe.wait_ge(s[1]["fused"], u + 1)
                pe.wait_ge(s[1]["fused_lo"], u + 1)
                after(pe, s_endc, u)
                for k in range(GB):
                    i = nc.tensor.transpose(psE[:, k * T:(k + 1) * T], fu[2][:, p, k, :], g.ident[:, :])
                i.then_inc(s_end, 1)

            def tick(t, p):
                stage(t, p, 2, NG, lambda u, q: turn_probs(u, q, 0))
                stage(t, p, 3, NG, lambda u, q: scores(u, q, 1))
                stage(t, p, 1, NG, lambda u, q: turn_keys(u, q, 0))
                stage(t, p, 2, NG, lambda u, q: outputs(u, q, 0))
                stage(t, p, 1, NG, lambda u, q: turn(u, q, 0))
                stage(t, p, 0, NG, text)
                stage(t, p, 4, NG, end)
                stage(t, p, 3, NG, lambda u, q: turn_probs(u, q, 1))
                stage(t, p, 1, NG, lambda u, q: scores(u, q, 0))
                stage(t, p, 3, NG, lambda u, q: turn_keys(u, q, 1))
                stage(t, p, 3, NG, lambda u, q: outputs(u, q, 1))
                stage(t, p, 2, NG, lambda u, q: turn(u, q, 1))
            ticks(pe, NG, LAGS, tick)

        @block.scalar
        def _(act):
            act.wait_ge(s_scale, 1)

            def copy(u, p, a):
                act.wait_ge(s[a]["turned"], u + 1)
                after(act, s[a]["scores"], u)
                nc.scalar.copy(flat(fT[a][:, :, :]), psA[a][:, :]).then_inc(s[a]["copied"], 1)

            def copy_keys(u, p, a):
                act.wait_ge(s[a]["keys_turned"], u + 1)
                after(act, s[a]["outputs"], u - 1)
                nc.scalar.copy(kt[a][:, p, :, 0:D2], psK[a][0:NK, 0:GB * D2].rearrange("p (a e) -> p a e", a=GB)).then_inc(s[a]["keys_copied"], 1)

            def exp(u, p, a):
                act.wait_ge(s[a]["shifted"], u + 1)
                nc.scalar.activation(P[a][:, :, :], P[a][:, :, :], ACT.Exp, scale=float(F) ** -0.5).then_inc(s[a]["exp"], 1)

            def copy_probs(u, p, a):
                act.wait_ge(s[a]["probs_turned"], u + 1)
                after(act, s[a]["outputs"], u)
                nc.scalar.copy(flat(PT[a][:, :, :]), psA[a][0:NK, :]).then_inc(s[a]["probs_copied"], 1)

            def end(u, p):
                act.wait_ge(s_end, u + 1)
                nc.scalar.copy(group(g.XT, u), psE[:, :].rearrange("p (a t) -> p a t", a=GB)).then_inc(s_endc, 1)

            def tick(t, p):
                stage(t, p, 2, NG, lambda u, q: copy_probs(u, q, 0))
                stage(t, p, 1, NG, lambda u, q: copy_keys(u, q, 0))
                stage(t, p, 3, NG, lambda u, q: exp(u, q, 1))
                stage(t, p, 1, NG, lambda u, q: copy(u, q, 0))
                stage(t, p, 4, NG, end)
                stage(t, p, 3, NG, lambda u, q: copy_probs(u, q, 1))
                stage(t, p, 3, NG, lambda u, q: copy_keys(u, q, 1))
                stage(t, p, 1, NG, lambda u, q: exp(u, q, 0))
                stage(t, p, 2, NG, lambda u, q: copy(u, q, 1))
            ticks(act, NG, LAGS, tick)


def layer_bit_ffn(nc, g, d):
    M = 4
    with ExitStack() as ctx:
        L = Layer(nc, ctx, "bf")
        s_w, s_part, s_all, s_link = L.sem("weights"), L.sem("part"), L.sem("largest"), L.sem("link")
        s_setup, s_ready = L.sem("inputs_ready"), L.sem("hidden_scale_ready")
        s_qf, s_q = L.sem("shifted"), L.sem("quantised")
        s_h1, s_m = L.sem("hidden_first"), L.sem("max")
        s_h2, s_relu, s_hq, s_y, s_o, s_x = (L.sem(n) for n in ("hidden", "relu", "hidden_quantised", "out", "out_scaled", "x_done"))
        B1, B2 = L.sb("b1", [128, M]), L.sb("b2", [128, F])
        one, most, scale, cs = L.sb("one", [128, 2]), L.sb("most", [128, 1]), L.sb("scale", [128, 2]), L.sb("product_scale", [128, 1])
        scale2, cs2, hc, hb = L.sb("scale2", [128, 2]), L.sb("product_scale2", [128, 1]), L.sb("hidden_scale", [128, 1]), L.sb("hidden_bias", [128, M])
        qa = L.sb("mean_shifted", [128, NB])
        qab = L.sb("mean_quantised", [128, NB], BF16)
        qf = L.sb("shifted", [F, GB * T])
        qb = L.sb("quantised", [F, NB, T], BF16)
        mx = L.sb("maxima", [128, NG, M])
        hs = L.sb("relu", [128, M, GB * T])
        hq = L.sb("hidden", [128, 2, M, GB * T], BF16)
        ys = L.sb("out", [T, 2, GB * F])
        psH = L.psum("H", [128, M, 512])
        psY, psN = L.psum("Y", [128, 2, 512]), L.psum("N", [128, 512])
        N = Norm(L, g, GB, s_x, psN)
        a1 = BIT_COLS["f1"][0]
        a2 = BIT_COLS["f2"][0]
        LAGS = 4
        block = ctx.enter_context(nc.Block())

        def mean_cols(u):
            m = qab[:, u * GB:(u + 1) * GB] if isinstance(u, int) else qab[:, bass.ds(u * GB, GB)]
            return m.unsqueeze(2).broadcast_to([128, GB, T])

        @block.sync
        def _(sp):
            sp.dma_start(B1[:, :], d["b_f1_b"]).then_inc(s_w, 16)
            sp.dma_start(B2[:, :], d["b_f2_b"].partition_broadcast(128)).then_inc(s_w, 16)

        @block.tensor
        def _(pe):
            pe.wait_ge(s_setup, 1)

            def hidden(u, m):
                nc.tensor.matmul(psH[:, m, :], g.qw[:, a1 + m * 128:a1 + (m + 1) * 128], flat(group(qb, u)), start=True, stop=False)
                return nc.tensor.matmul(psH[:, m, :], g.qw[:, a1 + 512 + m * 128:a1 + 512 + (m + 1) * 128], mean_cols(u),
                                        start=False, stop=True)

            def first(u, p):
                pe.wait_ge(s_q, u + 1)
                for m in range(M):
                    after(pe, s_m, u * M + m - M + 1)
                    hidden(u, m).then_inc(s_h1, 1)
            ticks(pe, NG, 2, lambda t, p: stage(t, p, 0, NG, first))
            pe.wait_ge(s_m, NG * M)

            def second(u, p):
                for m in range(M):
                    after(pe, s_relu, u * M + m - M + 1)
                    hidden(u, m).then_inc(s_h2, 1)

            def out(u, p):
                pe.wait_ge(s_hq, (u + 1) * M)
                after(pe, s_o, u - 1)
                for k in range(GB):
                    for m in range(M):
                        i = nc.tensor.matmul(psY[:, p, k * F:(k + 1) * F], hq[:, p, m, k * T:(k + 1) * T],
                                             g.qw[:, a2 + m * F:a2 + (m + 1) * F], start=(m == 0), stop=(m == M - 1))
                i.then_inc(s_y, 1)

            def tick(t, p):
                stage(t, p, 0, NG, second)
                stage(t, p, 1, NG, out)
                stage(t, p, 3, NG, lambda u, q: N.pe_turn(pe, u, q))
            ticks(pe, NG, LAGS, tick)

        @block.scalar
        def _(act):
            act.wait_ge(s_ready, 1)

            def relu(u, p):
                for m in range(M):
                    act.wait_ge(s_h2, u * M + m + 1)
                    after(act, s_hq, u * M + m - M + 1)
                    nc.scalar.activation(hs[:, m, :], psH[:, m, :], ACT.Relu, bias=hb[:, m:m + 1], scale=hc[:, 0:1]).then_inc(s_relu, 1)

            def tick(t, p):
                stage(t, p, 0, NG, relu)
                stage(t, p, 3, NG, lambda u, q: N.act_store(act, u, q))
            ticks(act, NG, LAGS, tick)

        @block.gpsimd
        def _(pool):
            for r in range(2):
                pool.wait_ge(s_part, r + 1)
                nc.gpsimd.partition_all_reduce(most[:, :], one[:, r:r + 1], 128, RMAX).then_inc(s_all, 1)

            def update(u, p):
                apart(pool, g, (s_o, u + 1))
                x = flat(group(g.X, u))
                nc.gpsimd.tensor_tensor(x, x, ys[:, p, :], ALU.add).then_inc(s_x, 1)

            def tick(t, p):
                stage(t, p, 2, NG, lambda u, q: N.pool_rstd(pool, u, q))
                stage(t, p, 1, NG, update)
            ticks(pool, NG, LAGS, tick)

        @block.vector
        def _(dve):
            link = Link(dve, s_link, 1000)
            dve.wait_ge(s_w, 32)
            link(nc.vector.tensor_reduce(one[:, 0:1], g.top[:, 0:g.tops], AX.X, ALU.max))
            link(nc.vector.tensor_reduce(one[:, 1:2], g.avg[:, :], AX.X, ALU.max, apply_absolute_value=True))
            nc.vector.tensor_tensor(one[:, 0:1], one[:, 0:1], one[:, 1:2], ALU.max).then_inc(s_part, 1)
            dve.wait_ge(s_all, 1)
            quant_scale(nc, dve, link, None, most[:, 0:1], scale, 1e-8, 127.0)
            i = BIT_AT["f1"]
            link(nc.vector.tensor_tensor(cs[:, :], g.ws[:, i:i + 1], scale[:, 0:1], ALU.mult))
            link(nc.vector.tensor_scalar(qa[:, :], g.avg[:, :], scale[:, 1:2], MAGIC, ALU.mult, ALU.add))
            nc.vector.tensor_scalar(qab[:, :], qa[:, :], MAGIC, None, ALU.subtract).then_inc(s_setup, 1)

            def quantise(u, p):
                after(dve, s_q, u)
                nc.vector.tensor_scalar(qf[:, :], flat(group(g.XT, u)), scale[:, 1:2], MAGIC, ALU.mult, ALU.add).then_inc(s_qf, 1)
                dve.wait_ge(s_qf, u + 1)
                nc.vector.tensor_scalar(flat(group(qb, u)), qf[:, :], MAGIC, None, ALU.subtract).then_inc(s_q, 1)

            def largest(u, p):
                for m in range(M):
                    dve.wait_ge(s_h1, u * M + m + 1)
                    top = mx[:, u, m:m + 1] if isinstance(u, int) else mx[:, bass.ds(u, 1), m]
                    nc.vector.tensor_reduce(top, psH[:, m, :], AX.X, ALU.max).then_inc(s_m, 1)

            def tick1(t, p):
                stage(t, p, 0, NG, quantise)
                stage(t, p, 1, NG, largest)
            ticks(dve, NG, 2, tick1)
            dve.wait_ge(s_m, NG * M)
            link(nc.vector.tensor_reduce(hb[:, :], mx[:, :, :].rearrange("p u m -> p m u"), AX.X, ALU.max))
            link(nc.vector.scalar_tensor_tensor(hb[:, :], hb[:, :], cs[:, 0:1], B1[:, :], ALU.mult, ALU.add))
            nc.vector.tensor_reduce(one[:, 1:2], hb[:, :], AX.X, ALU.max).then_inc(s_part, 1)
            dve.wait_ge(s_all, 2)
            link(nc.vector.tensor_scalar(most[:, :], most[:, :], 0.0, None, ALU.max))
            quant_scale(nc, dve, link, None, most[:, 0:1], scale2, 1e-8, 127.0)
            i = BIT_AT["f2"]
            link(nc.vector.tensor_tensor(cs2[:, :], g.ws[:, i:i + 1], scale2[:, 0:1], ALU.mult))
            link(nc.vector.tensor_tensor(hc[:, :], cs[:, :], scale2[:, 1:2], ALU.mult))
            link(nc.vector.tensor_scalar(hb[:, :], B1[:, :], scale2[:, 1:2], None, ALU.mult))
            dve.nop().then_inc(s_ready, 1)

            def quantise2(u, p):
                for m in range(M):
                    dve.wait_ge(s_relu, u * M + m + 1)
                    after(dve, s_y, u - 1)
                    nc.vector.tensor_scalar(hq[:, p, m, :], hs[:, m, :], MAGIC, MAGIC, ALU.add, ALU.subtract).then_inc(s_hq, 1)

            def outputs(u, p):
                dve.wait_ge(s_y, u + 1)
                after(dve, s_x, u - 1)
                nc.vector.scalar_tensor_tensor(ys[:, p, :].rearrange("p (a f) -> p a f", a=GB), psY[:, p, :].rearrange("p (a f) -> p a f", a=GB),
                                               cs2[:, 0:1], B2[:, :].unsqueeze(1).broadcast_to([128, GB, F]), ALU.mult, ALU.add).then_inc(s_o, 1)

            def tick(t, p):
                stage(t, p, 1, NG, outputs)
                stage(t, p, 2, NG, lambda u, q: N.dve_mean(dve, u, q))
                stage(t, p, 0, NG, quantise2)
                stage(t, p, 2, NG, lambda u, q: N.dve_xn(dve, u, q))
            ticks(dve, NG, LAGS, tick)



def layer_gated_experts(nc, g, d):
    E, M, P3 = 8, 4, 3
    with ExitStack() as ctx:
        L = Layer(nc, ctx, "ge")
        s_w, s_gs, s_gt, s_gc = L.sem("weights"), L.sem("gates"), L.sem("gates_turned"), L.sem("gates_copied")
        s_link, s_split = L.sem("link"), L.sem("gates_split")
        s_h, s_act, s_g, s_mul, s_y, s_x = (L.sem(n) for n in ("hidden", "gelu", "spread", "gated", "out", "x_done"))
        Wf, Wp, sel = L.sb("fc", [F, M * 128]), L.sb("proj", [128, M, F]), L.sb("spread", [P3 * E, M, 128], BF16)
        sel32 = L.sb("spread32", [P3 * E, M, 128])
        part, rest, parts = L.sb("part", [T, NB, E], BF16), L.sb("rest", [T, NB, E]), L.sb("parts", [T, NB, P3 * E])
        gs, gT = L.sb("gates", [T, GB, P3 * E]), L.sb("gatesT", [P3 * E, GB * T], BF16)
        hs = L.sb("hidden", [128, 2, M, GB * T])
        psH, psG = L.psum("H", [128, 2, 512]), L.psum("G", [128, 2, 512])
        psT, psY, psN = L.psum("T", [128, 512]), L.psum("Y", [128, 512]), L.psum("N", [128, 512])
        N = Norm(L, g, GB, s_x, psN)
        LAGS = 4
        block = ctx.enter_context(nc.Block())

        @block.sync
        def _(sp):
            for t, k in ((Wf, "m2_fc"), (Wp, "m2_proj"), (sel32, "c_spread")):
                sp.dma_start(t[:], d[k]).then_inc(s_w, 16)

        @block.tensor
        def _(pe):
            pe.wait_ge(s_w, 48)
            pe.wait_ge(s_split, 1)

            def turn_gates(u, p):
                pe.wait_ge(s_gs, u + 1)
                after(pe, s_gc, u)
                for k in range(GB):
                    i = nc.tensor.transpose(psT[0:P3 * E, k * T:(k + 1) * T], gs[:, k, :], g.ident[:, :])
                i.then_inc(s_gt, 1)

            def hidden(u, p):
                for m in range(M):
                    after(pe, s_act, u * M + m - 1)
                    nc.tensor.matmul(psH[:, m % 2, :], Wf[:, m * 128:(m + 1) * 128], flat(group(g.XT, u)),
                                     start=True, stop=True).then_inc(s_h, 1)

            def spread(u, p):
                pe.wait_ge(s_gc, u + 1)
                for m in range(M):
                    after(pe, s_mul, u * M + m - 1)
                    nc.tensor.matmul(psG[:, m % 2, :], sel[:, m, :], gT[:, :], start=True, stop=True).then_inc(s_g, 1)

            def out(u, p):
                pe.wait_ge(s_mul, (u + 1) * M)
                after(pe, s_x, u)
                for k in range(GB):
                    for m in range(M):
                        i = nc.tensor.matmul(psY[:, k * F:(k + 1) * F], hs[:, p, m, k * T:(k + 1) * T], Wp[:, m, :],
                                             start=(m == 0), stop=(m == M - 1))
                i.then_inc(s_y, 1)

            def tick(t, p):
                stage(t, p, 0, NG, hidden)
                stage(t, p, 0, NG, turn_gates)
                stage(t, p, 1, NG, out)
                stage(t, p, 0, NG, spread)
                stage(t, p, 3, NG, lambda u, q: N.pe_turn(pe, u, q))
            ticks(pe, NG, LAGS, tick)

        @block.scalar
        def _(act):
            def gates(u, p):
                act.wait_ge(s_gt, u + 1)
                after(act, s_g, u * M)
                nc.scalar.copy(gT[:, :], psT[0:P3 * E, :]).then_inc(s_gc, 1)

            def gelu(u, p):
                after(act, s_y, u - 1)
                for m in range(M):
                    act.wait_ge(s_h, u * M + m + 1)
                    nc.scalar.activation(hs[:, p, m, :], psH[:, m % 2, :], ACT.Gelu).then_inc(s_act, 1)

            def tick(t, p):
                stage(t, p, 0, NG, gelu)
                stage(t, p, 0, NG, gates)
                stage(t, p, 3, NG, lambda u, q: N.act_store(act, u, q))
            ticks(act, NG, LAGS, tick)

        @block.gpsimd
        def _(pool):
            def gates(u, p):
                after(pool, s_gt, u)
                nc.gpsimd.tensor_copy(gs[:, :, :], group(parts, u)).then_inc(s_gs, 1)

            pool.wait_ge(s_split, 1)

            def tick(t, p):
                stage(t, p, 0, NG, gates)
                stage(t, p, 2, NG, lambda u, q: N.pool_rstd(pool, u, q))
            ticks(pool, NG, LAGS, tick)

        @block.vector
        def _(dve):
            link = Link(dve, s_link, 1000)
            dve.wait_ge(s_w, 48)
            link(nc.vector.tensor_copy(sel[:, :, :], sel32[:, :, :]))
            for i in range(P3):
                at = parts[:, :, i * E:(i + 1) * E]
                left = rest if i else g.gate
                link(nc.vector.tensor_copy(part[:, :, :], left[:, :, :]))
                link(nc.vector.tensor_copy(at, part[:, :, :]))
                link(nc.vector.tensor_tensor(rest[:, :, :], left[:, :, :], at, ALU.subtract))
            dve.nop().then_inc(s_split, 1)

            def gate(u, p):
                for m in range(M):
                    dve.wait_ge(s_act, u * M + m + 1)
                    dve.wait_ge(s_g, u * M + m + 1)
                    nc.vector.tensor_tensor(hs[:, p, m, :], psG[:, m % 2, :], hs[:, p, m, :], ALU.mult).then_inc(s_mul, 1)

            def update(u, p):
                dve.wait_ge(s_y, u + 1)
                x = flat(group(g.X, u))
                nc.vector.tensor_tensor(x, psY[:, :], x, ALU.add).then_inc(s_x, 1)

            def tick(t, p):
                stage(t, p, 2, NG, lambda u, q: N.dve_mean(dve, u, q))
                stage(t, p, 3, NG, lambda u, q: N.dve_xn(dve, u, q))
                stage(t, p, 0, NG, gate)
                stage(t, p, 1, NG, update)
            ticks(dve, NG, LAGS, tick)


def layer_gated_mlp(nc, g, d):
    M = 3
    BL = 32
    Q = 32767.0
    with ExitStack() as ctx:
        L = Layer(nc, ctx, "gm")
        names = """weights link part largest w_rounded w_turned w_ready x_shifted x_rounded first first_max scales
            second up_shifted gate_shifted up_rounded gate_rounded tanh sig_shifted sig_rounded product product_max
            tanh3 sig_shifted3 sig_rounded3 product3 p_shifted p_rounded o o_max o4 o_shifted o_rounded out x_done""".split()
        s = {n: L.sem(n) for n in names}
        s_out = [L.sem("out_even"), L.sem("out_odd")]
        HT = M * GB * T
        buf = L.sb("buf", [128, 5, HT])
        raw, wq = buf[:, 0, 0:9 * 128], buf[:, 1, 0:9 * 128]
        bs, bi = L.sb("block_scales", [128, 36]), L.sb("block_inverses", [128, 36])
        W = L.sb("weightsT", [128, 9, 128])
        tops = L.sb("tops", [128, 4, NG])
        one, most = L.sb("one", [128, 2]), L.sb("most", [128, 2])
        sx, su, sg, sp3, so, c = (L.sb(n, [128, 2]) for n in ("scale_x", "scale_up", "scale_gate", "scale_p", "scale_o", "factors"))
        U, G = L.sb("up", [128, M, NB * T], I16), L.sb("gate_then_p", [128, M, NB * T], I16)
        ps = L.psum("ps", [128, 6, 512])
        psY = L.psum("Y", [128, 2, 512])
        up, gate = ps[:, 0:3, :], ps[:, 3:6, :]
        old = flat(g.XT[:, :, :])
        spare = [old[:, i * HT:(i + 1) * HT].rearrange("p (m t) -> p m t", m=M) for i in range(5)]
        mem = [buf[:, i, :].rearrange("p (m t) -> p m t", m=M) for i in range(5)]
        magic = L.sb("magic", [128, 2])
        block = ctx.enter_context(nc.Block())

        def cols(t, u):
            return t[:, :, u * GB * T:(u + 1) * GB * T] if isinstance(u, int) else t[:, :, bass.ds(u * GB * T, GB * T)]

        @block.sync
        def _(sp):
            sp.dma_start(raw, d["m3_w"]).then_inc(s["weights"], 16)

            def out(u, p):
                sp.wait_ge(s["x_done"], u + 1)
                o = d["out"]
                dst = o[u * GB:(u + 1) * GB] if isinstance(u, int) else o[bass.ds(u * GB, GB)]
                sp.dma_start(dst.rearrange("b t f -> t b f"), group(g.X, u)).then_inc(s_out[p], 16)
            ticks(sp, NG, 2, lambda t, p: stage(t, p, 0, NG, out))
            for x in s_out:
                sp.wait_ge(x, 8 * NG)

        @block.gpsimd
        def _(pool):
            for r, w in enumerate((1, 2, 1, 1)):
                pool.wait_ge(s["part"], r + 1)
                nc.gpsimd.partition_all_reduce(most[:, 0:w], one[:, 0:w], 128, RMAX).then_inc(s["largest"], 1)

        @block.tensor
        def _(pe):
            pe.wait_ge(s["w_rounded"], 1)
            for i in range(9):
                k = nc.tensor.transpose(ps[:, i // 4, (i % 4) * 128:(i % 4 + 1) * 128], wq[:, i * 128:(i + 1) * 128], g.ident[:, :])
            k.then_inc(s["w_turned"], 1)
            pe.wait_ge(s["w_ready"], 1)

            def products(u, done, read):
                for j in range(2):
                    after(pe, s[read], 2 * u + j - 1)
                    for m in range(M):
                        i = nc.tensor.matmul(ps[:, j * M + m, :], W[:, j * M + m, :], flat(group(g.XT, u)), start=True, stop=True)
                    i.then_inc(s[done], 1)

            def first(u, p):
                pe.wait_ge(s["x_rounded"], u + 1)
                products(u, "first", "first_max")
            ticks(pe, NG, 1, lambda t, p: stage(t, p, 0, NG, first))
            pe.wait_ge(s["first_max"], 2 * NG)

            def second(u, p):
                for j, read in enumerate(("up_shifted", "gate_shifted")):
                    after(pe, s[read], u)
                    for m in range(M):
                        i = nc.tensor.matmul(ps[:, j * M + m, :], W[:, j * M + m, :], flat(group(g.XT, u)), start=True, stop=True)
                    i.then_inc(s["second"], 1)
            ticks(pe, NG, 1, lambda t, p: stage(t, p, 0, NG, second))

            def out(u, p):
                pe.wait_ge(s["o_rounded"], u + 1)
                after(pe, s["x_done"], u - 1)
                for k in range(GB):
                    for m in range(M):
                        i = nc.tensor.matmul(psY[:, p, k * F:(k + 1) * F], mem[2 + p][:, m, k * T:(k + 1) * T], W[:, 6 + m, :],
                                             start=(m == 0), stop=(m == M - 1))
                i.then_inc(s["out"], 1)
            ticks(pe, NG, 2, lambda t, p: stage(t, p, 1, NG, out))

        @block.scalar
        def _(act):
            act.wait_ge(s["w_turned"], 1)
            for b in range(3):
                n = min(4, 9 - 4 * b)
                i = nc.scalar.copy(flat(W[:, 4 * b:4 * b + n, :]), ps[:, b, 0:n * 128])
            i.then_inc(s["w_ready"], 1)
            act.wait_ge(s["scales"], 2)

            def shift(u, p):
                act.wait_ge(s["second"], 2 * u + 1)
                after(act, s["up_rounded"], u)
                nc.scalar.activation(mem[0], up, ACT.Identity, bias=magic[:, 0:1], scale=su[:, 1:2]).then_inc(s["up_shifted"], 1)
                act.wait_ge(s["second"], 2 * u + 2)
                after(act, s["gate_rounded"], u)
                nc.scalar.activation(mem[1], gate, ACT.Identity, bias=magic[:, 0:1], scale=sg[:, 1:2]).then_inc(s["gate_shifted"], 1)

            def sigmoid(u, buffer, rounded, freed, tanh, shifted):
                if rounded is not None:
                    act.wait_ge(s[rounded], u + 1)
                after(act, s[freed], u - 1)
                nc.scalar.activation(buffer, cols(G, u), ACT.Tanh, scale=c[:, 0:1]).then_inc(s[tanh], 1)
                act.wait_ge(s[tanh], u + 1)
                nc.scalar.activation(buffer, buffer, ACT.Identity, bias=magic[:, 1:2], scale=32768.0).then_inc(s[shifted], 1)

            def tick(t, p):
                stage(t, p, 0, NG, shift)
                stage(t, p, 1, NG, lambda u, q: sigmoid(u, mem[2 + q], "gate_rounded", "product_max", "tanh", "sig_shifted"))
            ticks(act, NG, 2, tick)
            act.wait_ge(s["scales"], 3)

            def shift_p(u, p):
                act.wait_ge(s["product3"], u + 1)
                nc.scalar.activation(spare[2 + p], spare[2 + p], ACT.Identity, bias=magic[:, 0:1], scale=c[:, 1:2]).then_inc(s["p_shifted"], 1)

            def tick3(t, p):
                stage(t, p, 0, NG, lambda u, q: sigmoid(u, spare[q], None, "product3", "tanh3", "sig_shifted3"))
                stage(t, p, 1, NG, shift_p)
            ticks(act, NG, 2, tick3)
            act.wait_ge(s["scales"], 4)

            def shift_o(u, p):
                act.wait_ge(s["o4"], u + 1)
                nc.scalar.activation(mem[p], mem[p], ACT.Identity, bias=magic[:, 0:1], scale=so[:, 1:2]).then_inc(s["o_shifted"], 1)
            ticks(act, NG, 2, lambda t, p: stage(t, p, 0, NG, shift_o))

        @block.vector
        def _(dve):
            link = Link(dve, s["link"], 1000)
            link(nc.vector.memset(magic[:, 0:1], MAGIC))
            link(nc.vector.memset(magic[:, 1:2], MAGIC + 32768.0))
            dve.wait_ge(s["weights"], 16)
            blocks = raw.rearrange("p (b i) -> p b i", i=BL)
            rounded = wq.rearrange("p (b i) -> p b i", i=BL)
            spread = lambda t: t[:, :].unsqueeze(2).broadcast_to([128, 36, BL])
            link(nc.vector.tensor_reduce(bs[:, :], blocks, AX.X, ALU.max, apply_absolute_value=True))
            link(nc.vector.tensor_scalar(bs[:, :], bs[:, :], 1.0 / 7.0, 1e-12, ALU.mult, ALU.max))
            link(nc.vector.reciprocal(bi[:, :], bs[:, :]))
            link(nc.vector.tensor_tensor(rounded, blocks, spread(bi), ALU.mult))
            link(nc.vector.tensor_scalar(raw, wq, MAGIC, MAGIC, ALU.add, ALU.subtract))
            nc.vector.tensor_tensor(rounded, blocks, spread(bs), ALU.mult).then_inc(s["w_rounded"], 1)

            def scale_of(out, n, r):
                link(nc.vector.tensor_scalar(out[:, 0:1], most[:, n:n + 1], 1.0 / Q, 1e-12, ALU.mult, ALU.max))
                link(nc.vector.reciprocal(out[:, 1:2], out[:, 0:1]))

            nc.vector.tensor_reduce(one[:, 0:1], g.top[:, 0:g.tops], AX.X, ALU.max).then_inc(s["part"], 1)
            dve.wait_ge(s["largest"], 1)
            scale_of(sx, 0, 1)
            dve.nop().then_inc(s["scales"], 1)
            dve.wait_ge(s["w_turned"], 1)

            def round_x(u, p):
                x = group(g.XT, u)
                t = buf[:, p, 0:GB * T].rearrange("p (a t) -> p a t", a=GB)
                nc.vector.tensor_scalar(t, x, sx[:, 1:2], MAGIC, ALU.mult, ALU.add).then_inc(s["x_shifted"], 1)
                dve.wait_ge(s["x_shifted"], u + 1)
                nc.vector.tensor_scalar(x, t, MAGIC, sx[:, 0:1], ALU.subtract, ALU.mult).then_inc(s["x_rounded"], 1)

            def at(t, r, u):
                return t[:, r, u:u + 1] if isinstance(u, int) else t[:, r, bass.ds(u, 1)]

            def first_max(u, p):
                for j, x in enumerate((up, gate)):
                    dve.wait_ge(s["first"], 2 * u + j + 1)
                    nc.vector.tensor_reduce(at(tops, j, u), x, AX.XY, ALU.max, apply_absolute_value=True).then_inc(s["first_max"], 1)

            def tick1(t, p):
                stage(t, p, 0, NG, round_x)
                stage(t, p, 1, NG, first_max)
            ticks(dve, NG, 1, tick1)
            dve.wait_ge(s["first_max"], 2 * NG)
            nc.vector.tensor_reduce(one[:, :], tops[:, 0:2, :], AX.X, ALU.max).then_inc(s["part"], 1)
            dve.wait_ge(s["largest"], 2)
            scale_of(su, 0, 2)
            scale_of(sg, 1, 2)
            link(nc.vector.tensor_scalar(c[:, 0:1], sg[:, 0:1], 0.5, None, ALU.mult))
            dve.nop().then_inc(s["scales"], 1)

            def round_both(u, p):
                dve.wait_ge(s["up_shifted"], u + 1)
                nc.vector.tensor_scalar(cols(U, u), mem[0], MAGIC, None, ALU.subtract).then_inc(s["up_rounded"], 1)
                dve.wait_ge(s["gate_shifted"], u + 1)
                nc.vector.tensor_scalar(cols(G, u), mem[1], MAGIC, None, ALU.subtract).then_inc(s["gate_rounded"], 1)

            def gate_sigmoid(u, sig, out, shifted, rounded, product):
                dve.wait_ge(s[shifted], u + 1)
                nc.vector.tensor_scalar(sig, sig, MAGIC, 65535.0, ALU.subtract, ALU.min).then_inc(s[rounded], 1)
                dve.wait_ge(s[rounded], u + 1)
                nc.vector.tensor_tensor(out, cols(G, u), sig, ALU.mult).then_inc(s[product], 1)

            def product(u, p):
                after(dve, s["product_max"], u)
                gate_sigmoid(u, mem[2 + p], mem[4], "sig_shifted", "sig_rounded", "product")
                dve.wait_ge(s["product"], u + 1)
                nc.vector.tensor_reduce(at(tops, 2, u), mem[4], AX.XY, ALU.max, apply_absolute_value=True).then_inc(s["product_max"], 1)

            def tick2(t, p):
                stage(t, p, 0, NG, round_both)
                stage(t, p, 1, NG, product)
            ticks(dve, NG, 2, tick2)
            dve.wait_ge(s["product_max"], NG)
            link(nc.vector.tensor_reduce(one[:, 0:1], tops[:, 2, :], AX.X, ALU.max))
            link(nc.vector.tensor_scalar(sg[:, 0:1], sg[:, 0:1], 2.0 ** -16, None, ALU.mult))
            nc.vector.tensor_scalar(one[:, 0:1], one[:, 0:1], sg[:, 0:1], None, ALU.mult).then_inc(s["part"], 1)
            dve.wait_ge(s["largest"], 3)
            scale_of(sp3, 0, 3)
            link(nc.vector.tensor_tensor(c[:, 1:2], sg[:, 0:1], sp3[:, 1:2], ALU.mult))
            dve.nop().then_inc(s["scales"], 1)

            def product3(u, p):
                after(dve, s["p_rounded"], u - 1)
                gate_sigmoid(u, spare[p], spare[2 + p], "sig_shifted3", "sig_rounded3", "product3")

            def round_p(u, p):
                dve.wait_ge(s["p_shifted"], u + 1)
                nc.vector.tensor_scalar(cols(G, u), spare[2 + p], MAGIC, None, ALU.subtract).then_inc(s["p_rounded"], 1)
                dve.wait_ge(s["p_rounded"], u + 1)
                after(dve, s["o_max"], u)
                nc.vector.tensor_tensor(spare[4], cols(G, u), cols(U, u), ALU.mult).then_inc(s["o"], 1)
                dve.wait_ge(s["o"], u + 1)
                nc.vector.tensor_reduce(at(tops, 3, u), spare[4], AX.XY, ALU.max, apply_absolute_value=True).then_inc(s["o_max"], 1)

            def tick3(t, p):
                stage(t, p, 0, NG, product3)
                stage(t, p, 1, NG, round_p)
            ticks(dve, NG, 2, tick3)
            dve.wait_ge(s["o_max"], NG)
            link(nc.vector.tensor_reduce(one[:, 0:1], tops[:, 3, :], AX.X, ALU.max))
            link(nc.vector.tensor_tensor(sp3[:, 1:2], sp3[:, 0:1], su[:, 0:1], ALU.mult))
            nc.vector.tensor_scalar(one[:, 0:1], one[:, 0:1], sp3[:, 1:2], None, ALU.mult).then_inc(s["part"], 1)
            dve.wait_ge(s["largest"], 4)
            scale_of(so, 0, 4)
            link(nc.vector.tensor_tensor(so[:, 1:2], so[:, 1:2], sp3[:, 1:2], ALU.mult))
            dve.nop().then_inc(s["scales"], 1)

            def o4(u, p):
                after(dve, s["o_rounded"], u - 1)
                nc.vector.tensor_tensor(mem[p], cols(G, u), cols(U, u), ALU.mult).then_inc(s["o4"], 1)

            def round_o(u, p):
                dve.wait_ge(s["o_shifted"], u + 1)
                after(dve, s["out"], u - 1)
                nc.vector.tensor_scalar(mem[2 + p], mem[p], MAGIC, so[:, 0:1], ALU.subtract, ALU.mult).then_inc(s["o_rounded"], 1)

            def update(u, p):
                dve.wait_ge(s["out"], u + 1)
                x = flat(group(g.X, u))
                nc.vector.tensor_tensor(x, psY[:, p, :], x, ALU.add).then_inc(s["x_done"], 1)

            def tick4(t, p):
                stage(t, p, 0, NG, o4)
                stage(t, p, 2, NG, update)
                stage(t, p, 1, NG, round_o)
            ticks(dve, NG, 2, tick4)


def layer_store(nc, g, d):
    with ExitStack() as ctx:
        L = Layer(nc, ctx, "st")
        s_out = L.sem("stored")
        block = ctx.enter_context(nc.Block())

        @block.sync
        def _(sp):
            for i in range(4):
                b = NB // 4 * i
                sp.dma_start(d["out"][b:b + NB // 4].rearrange("b t f -> t b f"), g.X[:, b:b + NB // 4, :]).then_inc(s_out, 16)
            sp.wait_ge(s_out, 64)


def build(nc, d, layers=tuple(range(8))):
    with ExitStack() as ctx:
        g = Resident()
        sb = lambda n, s, t=F32: ctx.enter_context(nc.sbuf_tensor(n, s, t))
        g.X = sb("X", [T, NB, F])
        g.XT = sb("XT", [F, NB, T])
        g.ident = sb("ident", [128, 128])
        g.headmask = sb("headmask", [128, 4])
        g.rank = sb("rank", [128, 8])
        g.pick = sb("pick", [128, 36])
        g.keep = sb("keep", [T, NB])
        g.minus_half = sb("minus_half", [T, GB])
        g.s_constants = ctx.enter_context(nc.semaphore("constants"))
        g.gate = sb("gate", [T, NB, 8])
        g.top = sb("top", [128, NB])
        g.tops = NG
        layer_load(nc, g, d, layers[0] == 2, layers[0] in (4, 7))
        if 0 in layers:
            layer_heads(nc, g, d, "a0", 8, True, d["a0_wq"], d["a0_wk"], d["a0_wv"], d["a0_wo"], None, None, None,
                        d["a0_bo"], 64 ** -0.5, False)
        if 1 in layers:
            layer_router(nc, g, d, "r0", d["m0_wg"], d["m0_bg"], True)
            layer_experts(nc, g, d)
        if 2 in layers:
            layer_heads(nc, g, d, "a1", 16, False, d["a1_wq"], d["a1_wk"], d["a1_wv"], None, None, None, None, None,
                        8 ** -0.5, False)
        if 3 in layers:
            layer_channel_mix(nc, g, d)
        if 4 in layers:
            with ExitStack() as own:
                g.qw = own.enter_context(nc.sbuf_tensor("ternary", [128, 2176], BF16))
                g.ws = own.enter_context(nc.sbuf_tensor("ternary_scales", [128, len(BIT_COLS)], F32))
                g.avg = own.enter_context(nc.sbuf_tensor("mean_image", [128, NB], F32))
                layer_bit_weights(nc, g, d)
                layer_image(nc, g, d)
                layer_fused(nc, g, d)
                layer_bit_ffn(nc, g, d)
        if 5 in layers:
            layer_router(nc, g, d, "r2", d["m2_wg"], None, False)
            layer_gated_experts(nc, g, d)
        if 6 in layers:
            layer_heads(nc, g, d, "a3", 16, False, d["a3_wq"], d["a3_wk"], d["a3_wv"], d["a3_wo"], d["a3_bq"], d["a3_bk"], d["a3_bv"],
                        d["a3_bo"], 8 ** -0.5, False, g.top)
            g.tops = NB
        if 7 in layers:
            layer_gated_mlp(nc, g, d)
            return
        layer_store(nc, g, d)


def layouts(i):
    import numpy as np
    a = {k: np.asarray(v) for k, v in i.items()}
    c = np.ascontiguousarray
    p = np.arange(128)
    wkv3 = a["L3_xattn_Wkv"].reshape(16, 2, 8, CK)
    bkv3 = a["L3_xattn_bkv"].reshape(16, 2, 8)
    return {
        "c_ident": np.eye(128, dtype=np.float32),
        "c_headmask": ((p % 32) // 8 == np.arange(4)[:, None]).T.astype(np.float32).copy(),
        "c_pick": (p[:, None] == 32 * (np.arange(36) // 9) + np.arange(36) % 9).astype(np.float32),
        "c_rank": np.tile(np.arange(8, 0, -1, dtype=np.float32), (128, 1)),
        "mask_t": c(a["mask_BxS_bk0"].T),
        "x": a["x"],
        "ctx_t": c(a["ctx_768"].transpose(0, 2, 1)),
        "a0_wq": a["L0_xattn_Wq"], "a0_wk": a["L0_xattn_Wk"], "a0_wv": a["L0_xattn_Wv"],
        "a0_wo": c(a["L0_xattn_Wo"].reshape(4, 128, F).transpose(1, 0, 2)), "a0_bo": a["L0_xattn_bo"],
        "a1_wq": c(a["L1_xattn_Wq"].T), "a1_wk": c(a["L1_xattn_Wkv"][:128].T), "a1_wv": c(a["L1_xattn_Wkv"][128:].T),
        "m0_wg": a["L0_ffn_Wg"], "m0_bg": c(a["L0_ffn_bg"][:, None]),
        "m0_w1": c(a["L0_ffn_W1"].transpose(1, 0, 2)), "m0_b1": c(a["L0_ffn_b1"].reshape(8, 4, 128).transpose(2, 0, 1)),
        "m0_w2": c(a["L0_ffn_W2"].reshape(8, 4, 128, F).transpose(2, 0, 1, 3)), "m0_b2": c(a["L0_ffn_b2"].T),
        "c_spread1": np.tile(np.repeat(np.eye(8, dtype=np.float32), 128, axis=1), (3, 1)),
        "m1_wr": c(a["L1_ffn_W_r"].T), "m1_wk": c(a["L1_ffn_W_k"].T), "m1_wv": c(a["L1_ffn_W_v"].T),
        "c_bit_inverse_counts": np.tile(np.float32(1) / np.float32([96 * 128, 128 * 128, 128 * 128, 128 * 128, 128 * 128, 256 * 512, 512 * 128]), (128, 1)),
        "b_d2v_w": c(a["L2_xattn_W_d2v"].T),
        "b_rest_w": c(np.concatenate([a["L2_xattn_W_img"].T, a["L2_xattn_W_txt"].T] + [a["L2_xattn_W_att0"].T] * 2
                                     + [a["L2_xattn_W_att1"].T] * 2
                                     + [a["L2_xattn_W_f1"].T[:128], a["L2_xattn_W_f1"].T[128:],
                                        a["L2_xattn_W_f2"].T.reshape(4, 128, F).transpose(1, 0, 2).reshape(128, 512)], axis=1)),
        "b_d2v_b": c(a["L2_xattn_b_d2v"][:, None]), "b_img_b": c(a["L2_xattn_b_img"][:, None]),
        "b_att_b": c(np.stack([np.tile(a["L2_xattn_b_att0"], 2), np.tile(a["L2_xattn_b_att1"], 2)], 1)),
        "b_txt_b": a["L2_xattn_b_txt"], "b_f1_b": c(a["L2_xattn_b_f1"].reshape(4, 128).T), "b_f2_b": a["L2_xattn_b_f2"],
        "m2_wg": c(a["L2_ffn_w_gate"].T), "m2_fc": c(a["L2_ffn_w_fc"].reshape(512, F).T),
        "m2_proj": c(a["L2_ffn_w_proj"].transpose(0, 2, 1).reshape(4, 128, F).transpose(1, 0, 2)),
        "c_spread": np.tile(np.arange(8)[:, None, None] == 2 * np.arange(4)[None, :, None] + p[None, None, :] // 64, (3, 1, 1)).astype(np.float32),
        "a3_wq": c(a["L3_xattn_Wq"].T), "a3_wk": c(wkv3[:, 0].reshape(128, CK).T), "a3_wv": c(wkv3[:, 1].reshape(128, CK).T),
        "a3_wo": c(a["L3_xattn_Wo"].T[:, None, :]), "a3_bq": c(a["L3_xattn_bq"][:, None]), "a3_bk": c(bkv3[:, 0].reshape(128, 1)),
        "a3_bv": c(bkv3[:, 1].reshape(128)), "a3_bo": a["L3_xattn_bo"],
        "m3_w": c(np.concatenate([a["L3_ffn_w_up"].reshape(3, 128, F).transpose(1, 0, 2).reshape(128, 384),
                                  a["L3_ffn_w_gate"].reshape(3, 128, F).transpose(1, 0, 2).reshape(128, 384),
                                  a["L3_ffn_w_down"]], axis=1)),
        "m1_mu": c(np.stack([a["L1_ffn_mu_r"], a["L1_ffn_mu_k"]], 1)),
    }


def program(nc, inputs, layers=tuple(range(8))):
    arrays = {f"in_{k}": v for k, v in layouts(inputs).items()}
    d = {k[3:]: nc.dram_tensor(k, v.shape, mybir.dt.from_np(v.dtype), kind="ExternalInput").ap() for k, v in arrays.items()}
    d["out"] = nc.dram_tensor("out", (NB, T, F), F32, kind="ExternalOutput").ap()
    d["keys"] = nc.dram_tensor("keys", (NB, 2, 128, NK), F32, kind="Internal").ap()
    build(nc, d, layers)
    return arrays


def kernel(**inputs):
    import concourse.bacc as bacc
    from concourse.bass_utils import run_bass_kernel_spmd

    nc = bacc.Bacc("TRN2", target_bir_lowering=False, num_devices=1)
    arrays = program(nc, inputs)
    return run_bass_kernel_spmd(nc, [arrays], core_ids=[0]).results[0]["out"]
```
